# Optimizing a Trainium2 kernel written in Bass

```python
import numpy as np
import jax
import jax.numpy as jnp

def _softmax(x, axis=-1):
    return jax.nn.softmax(x, axis=axis)

def _gelu(x):
    return jax.nn.gelu(x, approximate=True)

def _silu(x):
    return jax.nn.silu(x)

def _sigmoid(x):
    return jax.nn.sigmoid(x)

def _layernorm(x, axis=-1, eps=1e-05):
    m = jnp.mean(x, axis=axis, keepdims=True)
    v = jnp.var(x, axis=axis, keepdims=True)
    return (x - m) / jnp.sqrt(v + eps)

def _scatter_add(tgt, idx, src, axis=0):
    return tgt.at[idx].add(src)

def _segment_sum(src, seg, n):
    return jax.ops.segment_sum(src, seg, n)
kernel_name = 'mk_flamingo_gated_d2_seqx_r8_f0d53f'

def setup_inputs(seed: int=0):
    np.random.seed(seed)
    _w = jnp.asarray

    def _rec_inputs():
        import jax
        import jax.numpy as jnp
        _rk = jax.random.key(seed)
        x = 7.22e-05 + 1 * jax.random.normal(jax.random.fold_in(_rk, 1), (16, 128, 256), jnp.float32)
        _lenS = 128 - jax.random.randint(jax.random.fold_in(_rk, 7), (16,), 0, max(1, 128 // 4) + 1, jnp.int32)
        _lenS2 = 128 - jax.random.randint(jax.random.fold_in(_rk, 8), (16,), 0, max(1, 128 // 4) + 1, jnp.int32)
        _ctx_2048P = jax.random.normal(jax.random.fold_in(_rk, 11), (16, 16, 256), jnp.float32)
        _ctx_2048c = jax.random.dirichlet(jax.random.fold_in(_rk, 511), 0.3 * jnp.ones((16,), jnp.float32), (16, 128))
        _ctx_2048t = jnp.einsum('bsk,bkd->bsd', _ctx_2048c, _ctx_2048P)
        _ctx_2048t = _ctx_2048t * jax.lax.rsqrt(jnp.mean(jnp.square(_ctx_2048t)) + 1e-12) * 0.953939
        ctx_2048 = 4.13588e-05 + 0.999923 * (_ctx_2048t + 0.3 * jax.random.normal(jax.random.fold_in(_rk, 611), (16, 128, 256), jnp.float32))
        _g = jax.random.normal(jax.random.fold_in(_rk, 9001), (2, 2), jnp.float32)
        _g = jnp.sign(_g) * jnp.maximum(jnp.abs(_g), 1.0) + (_g == 0) * 1.0
        g_xattn = _g[0]
        g_ffn = _g[1]
        return (x, ctx_2048, g_xattn, g_ffn)
    x, ctx_2048, g_xattn, g_ffn = _rec_inputs()

    def _L0_xattn_setup():
        import jax, jax.numpy as jnp
        import numpy as np
        B, D, N, H = (4, 128, 256, 16)
        HD = D // H

        def rotate_half(x):
            x1 = x[..., 0::2]
            x2 = x[..., 1::2]
            return jnp.stack((-x2, x1), axis=-1).reshape(x.shape)

        def apply_cached_rotary_emb(freqs, t):
            return t * freqs[0] + rotate_half(t) * freqs[1]
        key = jax.random.key(seed)
        ks = jax.random.split(key, 13)
        s = 1.0 / np.sqrt(D)
        inp = {'query': jax.random.normal(ks[0], (B, D, N), jnp.float32), 'key': jax.random.normal(ks[1], (B, D, N), jnp.float32), 'value': jax.random.normal(ks[2], (B, D, N), jnp.float32), 'encoding': jax.random.normal(ks[3], (2, 1, 1, N, HD), jnp.float32), 'Wq': jax.random.normal(ks[4], (D, D), jnp.float32) * s, 'bq': jax.random.normal(ks[5], (D,), jnp.float32) * s, 'Wk': jax.random.normal(ks[6], (D, D), jnp.float32) * s, 'bk': jax.random.normal(ks[7], (D,), jnp.float32) * s, 'Wv': jax.random.normal(ks[8], (D, D), jnp.float32) * s, 'bv': jax.random.normal(ks[9], (D,), jnp.float32) * s, 'Wm': jax.random.normal(ks[10], (D, D), jnp.float32) * s, 'bm': jax.random.normal(ks[11], (D,), jnp.float32) * s}
        return inp
    _L0_xattn_all = _L0_xattn_setup()
    _L0_xattn_in = {k: v for k, v in _L0_xattn_all.items() if k in ('encoding', 'Wq', 'bq', 'Wk', 'bk', 'Wv', 'bv', 'Wm', 'bm')}
    del _L0_xattn_all

    def _L0_ffn_setup():
        import jax, jax.numpy as jnp
        import numpy as np
        EPS = 1e-05

        def _quant_weight(w):
            scale = jnp.mean(jnp.abs(w)) + EPS
            wq = jnp.clip(jnp.round(w / scale), -1.0, 1.0)
            return (wq, scale)

        def _quant_act(x):
            s = jnp.max(jnp.abs(x), axis=-1, keepdims=True) / 127.0 + EPS
            xq = jnp.clip(jnp.round(x / s), -128.0, 127.0)
            return (xq, s)

        def _qlinear(x, w):
            wq, ws = _quant_weight(w)
            xq, xs = _quant_act(x)
            y = jnp.einsum('bsi,oi->bso', xq, wq)
            return y * xs * ws
        key = jax.random.key(seed)
        k1, k2, k3, k4 = jax.random.split(key, 4)
        H, I = (256, 1024)
        x = jax.random.normal(k1, (4, 512, H), dtype=jnp.float32)
        w_gate = jax.random.normal(k2, (I, H), dtype=jnp.float32) * (1.0 / np.sqrt(H))
        w_up = jax.random.normal(k3, (I, H), dtype=jnp.float32) * (1.0 / np.sqrt(H))
        w_down = jax.random.normal(k4, (H, I), dtype=jnp.float32) * (1.0 / np.sqrt(I))
        return {'x': x, 'w_gate': w_gate, 'w_up': w_up, 'w_down': w_down}
    _L0_ffn_all = _L0_ffn_setup()
    _L0_ffn_in = {k: v for k, v in _L0_ffn_all.items() if k in ('w_gate', 'w_up', 'w_down')}
    del _L0_ffn_all

    def _L1_xattn_setup():
        import jax, jax.numpy as jnp
        import numpy as np
        HIDDEN = 256
        N_HEADS = 16
        N_KV_HEADS = 4
        HEAD_DIM = 128
        EPS = 1e-06

        def rms_norm(x, w, eps=EPS):
            xf = x.astype(jnp.float32)
            var = jnp.mean(xf * xf, axis=-1, keepdims=True)
            return w * (xf * jax.lax.rsqrt(var + eps)).astype(x.dtype)
        key = jax.random.key(seed)
        ks = jax.random.split(key, 8)
        B, S, S_ENC = (4, 256, 128)
        inner = N_HEADS * HEAD_DIM
        kv_dim = N_KV_HEADS * HEAD_DIM
        s = 0.02
        return {'hidden_states': jax.random.normal(ks[0], (B, S, HIDDEN), jnp.float32), 'encoder_hidden_states': jax.random.normal(ks[1], (B, S_ENC, HIDDEN), jnp.float32), 'Wq': jax.random.normal(ks[2], (HIDDEN, inner), jnp.float32) * s, 'Wk': jax.random.normal(ks[3], (HIDDEN, kv_dim), jnp.float32) * s, 'Wv': jax.random.normal(ks[4], (HIDDEN, kv_dim), jnp.float32) * s, 'Wo': jax.random.normal(ks[5], (inner, HIDDEN), jnp.float32) * s, 'q_norm_w': jnp.ones((HEAD_DIM,), jnp.float32), 'k_norm_w': jnp.ones((HEAD_DIM,), jnp.float32)}
    _L1_xattn_all = _L1_xattn_setup()
    _L1_xattn_in = {k: v for k, v in _L1_xattn_all.items() if k in ('Wq', 'Wk', 'Wv', 'Wo', 'q_norm_w', 'k_norm_w')}
    del _L1_xattn_all

    def _L1_ffn_setup():
        import jax, jax.numpy as jnp
        import numpy as np
        TOP_K = 6
        CAP_FACTOR = 2

        def _moe_block(x2d, wg_router, w_gate, w_up, w_down, ws_gate, ws_up, ws_down):
            T, D = x2d.shape
            E = wg_router.shape[0]
            scores = jax.nn.softmax(x2d @ wg_router.T, axis=-1)
            topk_w, topk_idx = jax.lax.top_k(scores, TOP_K)
            topk_w = topk_w / (jnp.sum(topk_w, axis=-1, keepdims=True) + 1e-20)
            flat_idx = topk_idx.reshape(-1)
            oh = jax.nn.one_hot(flat_idx, E, dtype=jnp.int32)
            pos = jnp.cumsum(oh, axis=0) - 1
            pos_in_e = jnp.take_along_axis(pos, flat_idx[:, None], axis=1)[:, 0]
            C = CAP_FACTOR * (T * TOP_K // E)
            valid = pos_in_e < C
            safe_pos = jnp.where(valid, pos_in_e, 0)
            tok_id = jnp.repeat(jnp.arange(T), TOP_K)
            vmask = valid[:, None].astype(x2d.dtype)
            x_rep = x2d[tok_id] * vmask
            xe = jnp.zeros((E, C, D), x2d.dtype).at[flat_idx, safe_pos].add(x_rep)
            g = jnp.einsum('ecd,edf->ecf', xe, w_gate)
            u = jnp.einsum('ecd,edf->ecf', xe, w_up)
            ye = jnp.einsum('ecf,efd->ecd', jax.nn.silu(g) * u, w_down)
            y_tok = ye[flat_idx, safe_pos] * vmask
            y = jnp.sum(y_tok.reshape(T, TOP_K, D) * topk_w[..., None], axis=1)
            sh = jax.nn.silu(x2d @ ws_gate) * (x2d @ ws_up) @ ws_down
            return y + sh
        key = jax.random.key(seed)
        ks = jax.random.split(key, 9)
        B, S, D, F, E = (1, 256, 256, 176, 32)
        FS = F * 2
        s = 0.02
        return {'hidden_states': jax.random.normal(ks[0], (B, S, D), jnp.float32), 'wg_router': jax.random.normal(ks[1], (E, D), jnp.float32) * s, 'w_gate': jax.random.normal(ks[2], (E, D, F), jnp.float32) * s, 'w_up': jax.random.normal(ks[3], (E, D, F), jnp.float32) * s, 'w_down': jax.random.normal(ks[4], (E, F, D), jnp.float32) * s, 'ws_gate': jax.random.normal(ks[5], (D, FS), jnp.float32) * s, 'ws_up': jax.random.normal(ks[6], (D, FS), jnp.float32) * s, 'ws_down': jax.random.normal(ks[7], (FS, D), jnp.float32) * s}
    _L1_ffn_all = _L1_ffn_setup()
    _L1_ffn_in = {k: v for k, v in _L1_ffn_all.items() if k in ('wg_router', 'w_gate', 'w_up', 'w_down', 'ws_gate', 'ws_up', 'ws_down')}
    del _L1_ffn_all
    return {'x': x, 'ctx_2048': ctx_2048, 'g_xattn': g_xattn, 'g_ffn': g_ffn, 'L0_xattn_encoding': _L0_xattn_in['encoding'], 'L0_xattn_Wq': _L0_xattn_in['Wq'], 'L0_xattn_bq': _L0_xattn_in['bq'], 'L0_xattn_Wk': _L0_xattn_in['Wk'], 'L0_xattn_bk': _L0_xattn_in['bk'], 'L0_xattn_Wv': _L0_xattn_in['Wv'], 'L0_xattn_bv': _L0_xattn_in['bv'], 'L0_xattn_Wm': _L0_xattn_in['Wm'], 'L0_xattn_bm': _L0_xattn_in['bm'], 'L0_ffn_w_gate': _L0_ffn_in['w_gate'], 'L0_ffn_w_up': _L0_ffn_in['w_up'], 'L0_ffn_w_down': _L0_ffn_in['w_down'], 'L1_xattn_Wq': _L1_xattn_in['Wq'], 'L1_xattn_Wk': _L1_xattn_in['Wk'], 'L1_xattn_Wv': _L1_xattn_in['Wv'], 'L1_xattn_Wo': _L1_xattn_in['Wo'], 'L1_xattn_q_norm_w': _L1_xattn_in['q_norm_w'], 'L1_xattn_k_norm_w': _L1_xattn_in['k_norm_w'], 'L1_ffn_wg_router': _L1_ffn_in['wg_router'], 'L1_ffn_w_gate': _L1_ffn_in['w_gate'], 'L1_ffn_w_up': _L1_ffn_in['w_up'], 'L1_ffn_w_down': _L1_ffn_in['w_down'], 'L1_ffn_ws_gate': _L1_ffn_in['ws_gate'], 'L1_ffn_ws_up': _L1_ffn_in['ws_up'], 'L1_ffn_ws_down': _L1_ffn_in['ws_down']}

def reference(x, ctx_2048, g_xattn, g_ffn, L0_xattn_encoding, L0_xattn_Wq, L0_xattn_bq, L0_xattn_Wk, L0_xattn_bk, L0_xattn_Wv, L0_xattn_bv, L0_xattn_Wm, L0_xattn_bm, L0_ffn_w_gate, L0_ffn_w_up, L0_ffn_w_down, L1_xattn_Wq, L1_xattn_Wk, L1_xattn_Wv, L1_xattn_Wo, L1_xattn_q_norm_w, L1_xattn_k_norm_w, L1_ffn_wg_router, L1_ffn_w_gate, L1_ffn_w_up, L1_ffn_w_down, L1_ffn_ws_gate, L1_ffn_ws_up, L1_ffn_ws_down):
    import jax
    import jax.numpy as jnp

    def _L0_xattn_ref(query, key, value, encoding, Wq, bq, Wk, bk, Wv, bv, Wm, bm):
        import jax, jax.numpy as jnp
        import numpy as np
        B, D, N, H = (4, 128, 256, 16)
        HD = D // H

        def rotate_half(x):
            x1 = x[..., 0::2]
            x2 = x[..., 1::2]
            return jnp.stack((-x2, x1), axis=-1).reshape(x.shape)

        def apply_cached_rotary_emb(freqs, t):
            return t * freqs[0] + rotate_half(t) * freqs[1]
        b, d_model, n = query.shape

        def proj(W, bias, x):
            return jnp.einsum('oi,bin->bon', W, x) + bias[None, :, None]
        q = proj(Wq, bq, query).reshape(b, HD, H, n)
        k = proj(Wk, bk, key).reshape(b, HD, H, n)
        v = proj(Wv, bv, value).reshape(b, HD, H, n)
        q = jnp.transpose(apply_cached_rotary_emb(encoding, jnp.transpose(q, (0, 2, 3, 1))), (0, 3, 1, 2))
        k = jnp.transpose(apply_cached_rotary_emb(encoding, jnp.transpose(k, (0, 2, 3, 1))), (0, 3, 1, 2))
        scores = jnp.einsum('bdhn,bdhm->bhnm', q, k) / np.float32(np.sqrt(HD))
        prob = jax.nn.softmax(scores, axis=-1)
        x = jnp.einsum('bhnm,bdhm->bdhn', prob, v)
        out = jnp.einsum('oi,bin->bon', Wm, x.reshape(b, d_model, n)) + bm[None, :, None]
        return out

    def _L0_ffn_ref(x, w_gate, w_up, w_down):
        import jax, jax.numpy as jnp
        import numpy as np
        EPS = 1e-05

        def _quant_weight(w):
            scale = jnp.mean(jnp.abs(w)) + EPS
            wq = jnp.clip(jnp.round(w / scale), -1.0, 1.0)
            return (wq, scale)

        def _quant_act(x):
            s = jnp.max(jnp.abs(x), axis=-1, keepdims=True) / 127.0 + EPS
            xq = jnp.clip(jnp.round(x / s), -128.0, 127.0)
            return (xq, s)

        def _qlinear(x, w):
            wq, ws = _quant_weight(w)
            xq, xs = _quant_act(x)
            y = jnp.einsum('bsi,oi->bso', xq, wq)
            return y * xs * ws
        gate = jax.nn.silu(_qlinear(x, w_gate))
        up = _qlinear(x, w_up)
        return _qlinear(gate * up, w_down)

    def _L1_xattn_ref(hidden_states, encoder_hidden_states, Wq, Wk, Wv, Wo, q_norm_w, k_norm_w):
        import jax, jax.numpy as jnp
        import numpy as np
        HIDDEN = 256
        N_HEADS = 16
        N_KV_HEADS = 4
        HEAD_DIM = 128
        EPS = 1e-06

        def rms_norm(x, w, eps=EPS):
            xf = x.astype(jnp.float32)
            var = jnp.mean(xf * xf, axis=-1, keepdims=True)
            return w * (xf * jax.lax.rsqrt(var + eps)).astype(x.dtype)
        B, S, _ = hidden_states.shape
        S_enc = encoder_hidden_states.shape[1]
        groups = N_HEADS // N_KV_HEADS
        scale = 1.0 / HEAD_DIM ** 0.5
        q = (hidden_states @ Wq).reshape(B, S, N_HEADS, HEAD_DIM)
        k = (encoder_hidden_states @ Wk).reshape(B, S_enc, N_KV_HEADS, HEAD_DIM)
        v = (encoder_hidden_states @ Wv).reshape(B, S_enc, N_KV_HEADS, HEAD_DIM)
        q = rms_norm(q, q_norm_w)
        k = rms_norm(k, k_norm_w)
        k = jnp.repeat(k, groups, axis=2)
        v = jnp.repeat(v, groups, axis=2)
        scores = jnp.einsum('bqhd,bkhd->bhqk', q, k) * scale
        probs = jax.nn.softmax(scores, axis=-1)
        out = jnp.einsum('bhqk,bkhd->bqhd', probs, v)
        out = out.reshape(B, S, N_HEADS * HEAD_DIM)
        return out @ Wo

    def _L1_ffn_ref(hidden_states, wg_router, w_gate, w_up, w_down, ws_gate, ws_up, ws_down):
        import jax, jax.numpy as jnp
        import numpy as np
        TOP_K = 6
        CAP_FACTOR = 2

        def _moe_block(x2d, wg_router, w_gate, w_up, w_down, ws_gate, ws_up, ws_down):
            T, D = x2d.shape
            E = wg_router.shape[0]
            scores = jax.nn.softmax(x2d @ wg_router.T, axis=-1)
            topk_w, topk_idx = jax.lax.top_k(scores, TOP_K)
            topk_w = topk_w / (jnp.sum(topk_w, axis=-1, keepdims=True) + 1e-20)
            flat_idx = topk_idx.reshape(-1)
            oh = jax.nn.one_hot(flat_idx, E, dtype=jnp.int32)
            pos = jnp.cumsum(oh, axis=0) - 1
            pos_in_e = jnp.take_along_axis(pos, flat_idx[:, None], axis=1)[:, 0]
            C = CAP_FACTOR * (T * TOP_K // E)
            valid = pos_in_e < C
            safe_pos = jnp.where(valid, pos_in_e, 0)
            tok_id = jnp.repeat(jnp.arange(T), TOP_K)
            vmask = valid[:, None].astype(x2d.dtype)
            x_rep = x2d[tok_id] * vmask
            xe = jnp.zeros((E, C, D), x2d.dtype).at[flat_idx, safe_pos].add(x_rep)
            g = jnp.einsum('ecd,edf->ecf', xe, w_gate)
            u = jnp.einsum('ecd,edf->ecf', xe, w_up)
            ye = jnp.einsum('ecf,efd->ecd', jax.nn.silu(g) * u, w_down)
            y_tok = ye[flat_idx, safe_pos] * vmask
            y = jnp.sum(y_tok.reshape(T, TOP_K, D) * topk_w[..., None], axis=1)
            sh = jax.nn.silu(x2d @ ws_gate) * (x2d @ ws_up) @ ws_down
            return y + sh
        B, S, D = hidden_states.shape
        x2d = hidden_states.reshape(-1, D)
        out = _moe_block(x2d, wg_router, w_gate, w_up, w_down, ws_gate, ws_up, ws_down)
        return out.reshape(B, S, D)
    x = x + jnp.tanh(g_xattn[0]) * _L0_xattn_ref(_layernorm(x, axis=-1), ctx_2048, ctx_2048, L0_xattn_encoding, L0_xattn_Wq, L0_xattn_bq, L0_xattn_Wk, L0_xattn_bk, L0_xattn_Wv, L0_xattn_bv, L0_xattn_Wm, L0_xattn_bm)
    x = x + jnp.tanh(g_ffn[0]) * _L0_ffn_ref(_layernorm(x, axis=-1), L0_ffn_w_gate, L0_ffn_w_up, L0_ffn_w_down)
    x = x + jnp.tanh(g_xattn[1]) * _L1_xattn_ref(_layernorm(x, axis=-1), ctx_2048, L1_xattn_Wq, L1_xattn_Wk, L1_xattn_Wv, L1_xattn_Wo, L1_xattn_q_norm_w, L1_xattn_k_norm_w)
    x = x + jnp.tanh(g_ffn[1]) * _L1_ffn_ref(_layernorm(x, axis=-1), L1_ffn_wg_router, L1_ffn_w_gate, L1_ffn_w_up, L1_ffn_w_down, L1_ffn_ws_gate, L1_ffn_ws_up, L1_ffn_ws_down)
    return x

_drawn_inputs = setup_inputs


def setup_inputs(seed=0):
    import zlib

    import numpy as np

    out = dict(_drawn_inputs(seed))
    spreads = {'g_ffn': (-1.0, 0.6), 'L1_xattn_q_norm_w': (1.0, 0.6), 'L1_xattn_k_norm_w': (1.0, 0.6)}
    factors = {'L1_ffn_wg_router': 8.0,
     'L1_ffn_w_gate': 8.0,
     'L1_ffn_w_up': 8.0,
     'L1_ffn_w_down': 8.0,
     'L1_ffn_ws_gate': 3.898,
     'L1_ffn_ws_up': 3.856,
     'L1_ffn_ws_down': 3.852,
     'L0_xattn_bv': 4.398,
     'L0_xattn_bm': 4.568}
    for name, (base, spread) in spreads.items():
        noise = np.random.default_rng([zlib.crc32(name.encode()), seed]).standard_normal(out[name].shape)
        drawn = base * np.exp(spread * noise) if base else spread * noise
        out[name] = jnp.asarray(drawn.astype(out[name].dtype))
    for name, factor in factors.items():
        out[name] = (out[name] * factor).astype(out[name].dtype)
    return out
```

```python
from contextlib import ExitStack

import numpy as np

import concourse.bass as bass
from concourse import mybir

F32 = mybir.dt.float32
BF16 = mybir.dt.bfloat16
U32 = mybir.dt.uint32
ALU = mybir.AluOpType
ACT = mybir.ActivationFunctionType
AX = mybir.AxisListType.X

P = 128
NB = 16
D = 256
LN_EPS = 1e-5
MAGIC = 12582912.0

EXPERTS, FE, TOP_K = 32, 176, 6
CAPACITY = 2 * (NB * P * TOP_K // EXPERTS)
SHARED = 2
FH = FE // 2
KE = D // P
ROUTED_JOBS = NB * TOP_K + EXPERTS
JOBS = ROUTED_JOBS + SHARED * NB
TOKEN_ROW = EXPERTS * CAPACITY
IDLE_ROW = TOKEN_ROW + NB * P
ALL_ROWS = IDLE_ROW + ROUTED_JOBS * P
SKIP = float(1 << 20)
ZERO_ROWS = 4

def after(eng, sem, count):
    if isinstance(count, int) and count <= 0:
        return
    eng.wait_ge(sem, count)


def alone(eng, sem, count, stood):
    if isinstance(count, int) and count <= 0:
        return
    eng.wait_ge(sem, count)
    eng.sem_inc(stood, 1)


def layer_stats(dve, stats, moments, x_tile, b, stats_step, stood):
    alone(dve, stats_step, 3 * b, stood)
    dve.bn_stats(stats[:, 0:6], x_tile).then_inc(stats_step, 1)
    alone(dve, stats_step, 3 * b + 1, stood)
    dve.bn_aggr(stats[:, 6:8], stats[:, 0:6]).then_inc(stats_step, 1)
    alone(dve, stats_step, 3 * b + 2, stood)
    dve.tensor_copy(moments[:, bass.ds(b, 1), :], stats[:, 6:8].unsqueeze(1)).then_inc(stats_step, 1)


def setup(nc, keep, x, consts, gates):
    with ExitStack() as ctx:
        sem = lambda n: ctx.enter_context(nc.semaphore(n))
        raw = ctx.enter_context(nc.sbuf_tensor("gates_raw", [P, 4], F32))
        stats = ctx.enter_context(nc.sbuf_tensor("stats0", [P, 8], F32))
        x_in, const_in = sem("x_in"), sem("const_in")
        consts_made = sem("consts_made")
        stats_step = sem("stats_step0")
        stood = keep.stood
        block = ctx.enter_context(nc.Block())

        @block.sync
        def _(sp):
            sp.dma_start(raw[:, :], gates.partition_broadcast(P)).then_inc(const_in, 16)
            sp.dma_start(keep.identity[:, :], consts[:, 0:P]).then_inc(const_in, 16)
            sp.dma_start(keep.x[:, :, :], x.rearrange("b p n -> p b n")).then_inc(x_in, 16)

        @block.scalar
        def _(act):
            act.wait_ge(const_in, 32)
            act.activation(keep.gate[:, :], raw[:, :], ACT.Tanh).then_inc(consts_made, 1)
            act.activation(keep.identity_bf[:, :], keep.identity[:, :], ACT.Copy).then_inc(consts_made, 1)

        @block.vector
        def _(dve):
            dve.memset(keep.ln_eps[:, :], LN_EPS)
            dve.memset(keep.ones[:, :], 1.0)
            dve.memset(keep.minus_half[:, :], -0.5).then_inc(consts_made, 1)
            dve.wait_ge(x_in, 16)
            for b in range(NB):
                layer_stats(dve, stats, keep.moments, keep.x[:, b, :], b, stats_step, stood)

        @block.gpsimd
        def _(pool):
            pool.wait_ge(stats_step, 3 * NB)
            inverse_deviation(pool, keep, 0)


def inverse_deviation(pool, keep, norm):
    done = keep.rstd_done
    pool.tensor_scalar(keep.rstd[:, :], keep.moments[:, :, 1], LN_EPS, None, ALU.add).then_inc(done, 1)
    pool.wait_ge(done, 2 * norm + 1)
    pool.tensor_tensor(keep.rstd[:, :], keep.rstd[:, :], keep.minus_half[:, :], ALU.pow).then_inc(done, 1)


HEADS0, HD0, N0 = 16, 8, 256
PAIRS = HEADS0 // 2
COUPLES = PAIRS // 2
PRODUCTS = 6
STACK = PRODUCTS * HD0
SLOTS = 3
UNITS = 2 * PAIRS


def layer0_attention(nc, keep, ctx_in_dram, w, dbg):
    with ExitStack() as ctx:
        sem = lambda n: ctx.enter_context(nc.semaphore(n))
        sems = lambda n, k: [sem(f"{n}{i}") for i in range(k)]
        sb = lambda n, shape, dt=F32: ctx.enter_context(nc.sbuf_tensor(n, shape, dt))
        bank = lambda n: ctx.enter_context(nc.psum_tensor(n, [P, 512], F32))

        w_qk = sb("w_qk", [P, 4, P])
        w_v = sb("w_v", [P, P])
        w_m = sb("w_m", [P, P])
        b_qk = sb("b_qk", [P, 4])
        b_v = sb("b_v", [P, P])
        b_m = sb("b_m", [P, 1])
        gate_bm = sb("gate_bm", [P, 1])
        sign = sb("sign", [P, 1])
        rope = sb("rope", [P, 2, N0])
        source = sb("source", [P, 3, N0])
        xn = sb("xn", [P, N0])
        turned = sb("turned", [P, 2, 2, N0])
        qk = sb("qk", [P, 2, N0])
        rest = sb("rest", [P, 2, N0])
        parts = sb("parts", [P, 2, 3, N0], BF16)
        q_stack = sb("q_stack", [P, SLOTS, PAIRS, N0], BF16)
        k_stack = sb("k_stack", [P, SLOTS, PAIRS, N0], BF16)
        values = sb("values", [P, SLOTS, 2, HEADS0, 32])
        top = sb("top", [P, 2, 2, PAIRS])
        top_rest = sb("top_rest", [P, 2, 2 * PAIRS])
        top_parts = sb("top_parts", [P, 2, 3, 2 * PAIRS], BF16)
        top_rows = sb("top_rows", [3 * HEADS0, N0], BF16)
        probs = sb("probs", [P, 2, 2, 2, 2, N0])
        sums_inv = sb("sums_inv", [P, 2, HEADS0])
        outs = sb("outs", [P, COUPLES, N0])
        mixed = sb("mixed", [P, 2, HEADS0, HD0])
        mixed_t = sb("mixed_t", [P, N0])
        x_plus = sb("x_plus", [P, 2, N0])
        stats = sb("stats_a", [P, 8])
        scratch = nc.dram_tensor("stack_scratch", [SLOTS, 2, 2, PRODUCTS, P // 2, N0], BF16)
        top_scratch = nc.dram_tensor("top_scratch", [SLOTS, 3 * HEADS0, N0], BF16)

        ps_score = [bank("ps_score0"), bank("ps_score1")]
        ps_prob = [bank("ps_prob0"), bank("ps_prob1")]
        ps_qk = bank("ps_qk")
        ps_v = bank("ps_v")
        ps_o = ctx.enter_context(nc.psum_tensor("ps_o", [P, 2, 512], F32))

        w_in, made = sem("w_in"), sem("made")
        source_in = sems("source_in", 3)
        xn_ready, q_ready, k_ready, v_ready = sem("xn_ready"), sem("q_ready"), sem("k_ready"), sem("v_ready")
        q_read = sem("q_read")
        rope_read, v_read = sem("rope_read"), sem("v_read")
        qk_sum, high_ready, rest_ready, mid_ready, parts_ready = (
            sem("qk_sum"), sem("high_ready"), sem("rest_ready"), sem("mid_ready"), sem("parts_ready"))
        scratch_in, stack_in = sems("scratch_in", 3), sems("stack_in", 3)
        score_ready, score_read = sem("score_ready"), sem("score_read")
        prob_ready, prob_read = sem("prob_ready"), sem("prob_read")
        pv_done, outs_ready, outs_t = sem("pv_done"), sem("outs_ready"), sem("outs_t")
        pool_step, top_split = sem("pool_step"), sem("top_split")
        top_t, top_rows_ready = sem("top_t"), sem("top_rows_ready")
        top_scratch_in, top_in = sems("top_scratch_in", 3), sems("top_in", 3)
        norm_step, mixed_ready = sem("norm_step"), sem("mixed_ready")
        mixed_t_ps, mixed_t_ready = sem("mixed_t_ps"), sem("mixed_t_ready")
        merged, x_plus_ready, x_done = sem("merged"), sem("x_plus_ready"), sem("x_done")
        stats_step = sem("stats_step")
        stood = keep.stood
        block = ctx.enter_context(nc.Block())

        def steps(eng, step):
            for i in (-2, -1, 0):
                step(i, lambda b: (b, b % 3, b // 3))
            with eng.Fori(0, 4) as t:
                for c in range(3):
                    step(c + 1, lambda b: (t * 3 + b, b % 3, t + b // 3), looped=True)
            for i in (13, 14, 15):
                step(i, lambda b: (b, b % 3, b // 3))

        def stages(i, looped):
            if looped:
                return i + 2, i + 1, i
            return tuple(b if 0 <= b < NB else None for b in (i + 2, i + 1, i))

        @block.sync
        def _(sp):
            for dst, src in ((w_qk[:, :, :], w.qk), (w_v[:, :], w.v), (w_m[:, :], w.m), (b_qk[:, :], w.bqk),
                             (b_v[:, :], w.bv.partition_broadcast(P)), (b_m[:, :], w.bm), (rope[:, :, :], w.enc),
                             (sign[:, :], w.sign)):
                sp.dma_start(dst, src).then_inc(w_in, 16)

            def load_source(at):
                b, slot, trip = at
                alone(sp, k_ready, b - 2, stood)
                sp.dma_start(source[:, slot:slot + 1, :], ctx_in_dram[bass.ds(b, 1)].rearrange("b p n -> p b n")).then_inc(source_in[slot], 16)

            def stack(at):
                b, slot, trip = at
                sp.wait_ge(parts_ready, b + 1)
                after(sp, stack_in[slot], 64 * trip)
                for o, blocks in ((0, (0, 0, 0, 1, 1, 2)), (1, (0, 1, 2, 0, 1, 0))):
                    for r, part in enumerate(blocks):
                        sp.dma_start(scratch[slot, o, :, r], parts[:, o, part, :]).then_inc(scratch_in[slot], 16)
                sp.wait_ge(scratch_in[slot], 192 * (trip + 1))
                sp.sem_inc(stood, 1)
                after(sp, prob_ready, UNITS * (b - 2))
                for o, dst in ((0, q_stack), (1, k_stack)):
                    for j in range(2):
                        sp.dma_start(dst[64 * j:64 * j + STACK, slot, :, :],
                                     scratch[slot, o, j].rearrange("r (d p) n -> (r d) p n", d=HD0)).then_inc(stack_in[slot], 16)

            def stack_top(at):
                b, slot, trip = at
                sp.wait_ge(top_rows_ready, b + 1)
                sp.dma_start(top_scratch[slot], top_rows[:, :]).then_inc(top_scratch_in[slot], 16)
                sp.wait_ge(top_scratch_in[slot], 16 * (trip + 1))
                view = top_scratch[slot].rearrange("(r j p) n -> j r p n", r=3, j=2)
                for j in range(2):
                    sp.dma_start(q_stack[64 * j + STACK:64 * j + STACK + 3, slot, :, :], view[j]).then_inc(top_in[slot], 16)

            def step(i, at, looped=False):
                first, second, third = stages(i, looped)
                if looped or 0 <= i + 3 < NB:
                    load_source(at(i + 3))
                if first is not None:
                    stack(at(first))
                if second is not None:
                    stack_top(at(second))

            load_source((0, 0, 0))
            steps(sp, step)

        @block.tensor
        def _(pe):
            pe.wait_ge(w_in, 8 * 16)

            def project(at):
                b, slot, trip = at
                pe.wait_ge(xn_ready, b + 1)
                pe.wait_ge(source_in[slot], 16 * (trip + 1))
                after(pe, rope_read, b)
                after(pe, top_rows_ready, b - 1)
                for k in range(2):
                    mm = pe.matmul(ps_qk[:, k * N0:(k + 1) * N0], w_qk[:, k, :], xn[:, :], start=True, stop=True)
                mm.then_inc(q_ready, 1)
                after(pe, x_done, b - 2)
                for half in range(2):
                    mm = pe.matmul(ps_v[:, half * P:(half + 1) * P], source[:, slot, half * P:(half + 1) * P], w_v[:, :],
                                   start=True, stop=True)
                mm.then_inc(v_ready, 1)
                pe.wait_ge(q_read, b + 1)
                for k in range(2):
                    mm = pe.matmul(ps_qk[:, k * N0:(k + 1) * N0], w_qk[:, 2 + k, :], source[:, slot, :], start=True, stop=True)
                mm.then_inc(k_ready, 1)

            def tiles(second, third, u):
                jobs = []
                if second is not None:
                    b, slot, trip = second
                    half, couple, j = u // 8, u // 2 % 4, u % 2
                    if u == 0:
                        pe.wait_ge(stack_in[slot], 64 * (trip + 1))
                    after(pe, score_read, b * UNITS + u - 1)
                    rows = slice(64 * j, 64 * j + STACK)
                    jobs.append((ps_score[j], q_stack, k_stack, rows, slot, 2 * couple, half, score_ready))
                if third is not None:
                    b, slot, trip = third
                    couple, half, j = u // 4, u // 2 % 2, 1 - u % 2
                    if u == 0:
                        pe.wait_ge(top_in[slot], 32 * (trip + 1))
                    after(pe, prob_read, b * UNITS + u - 1)
                    rows = slice(64 * j, 64 * j + STACK + 3)
                    jobs.append((ps_prob[j], k_stack, q_stack, rows, slot, 2 * couple, half, prob_ready))
                for k in range(2):
                    for ps, stationary, moving, rows, slot, pair, half, ready in jobs:
                        mm = pe.matmul(ps[:, k * N0:(k + 1) * N0],
                                       stationary[rows, slot, pair + k, half * P:(half + 1) * P],
                                       moving[rows, slot, pair + k, :], start=True, stop=True)
                        if k == 1:
                            mm.then_inc(ready, 1)

            def mix(at, couple):
                b, slot, trip = at
                pe.wait_ge(prob_read, b * UNITS + 4 * couple + 4)
                if couple == 0:
                    after(pe, mixed_ready, b)
                    pe.wait_ge(v_read, b + 1)
                for m in range(2):
                    for k, j in np.ndindex(2, 2):
                        q = 2 * k + j
                        mm = pe.matmul(ps_o[32 * q:32 * q + 32, couple // 2, (couple % 2) * N0:(couple % 2 + 1) * N0],
                                       values[:, slot, m, 4 * couple + q, :], probs[:, couple % 2, m, j, k, :],
                                       start=(m == 0), stop=(m == 1))
                mm.then_inc(pv_done, 1)

            def turn_outs(at):
                b, slot, trip = at
                for half in range(2):
                    pe.wait_ge(outs_ready, 2 * b + 2)
                    for couple in range(COUPLES):
                        mm = pe.transpose(ps_o[:, half, couple * P:(couple + 1) * P],
                                          outs[:, couple, half * P:(half + 1) * P], keep.identity[:, :])
                mm.then_inc(outs_t, 1)

            def turn_top(at):
                b, slot, trip = at
                alone(pe, top_split, b + 1, stood)
                for half in range(2):
                    mm = pe.transpose(ps_qk[0:3 * HEADS0, :].bitcast(BF16)[:, half * P:(half + 1) * P],
                                      top_parts[:, half].rearrange("p r h -> p (r h)"), keep.identity_bf[:, :])
                mm.then_inc(top_t, 1)

            def merge(at, v_count):
                b, slot, trip = at
                pe.wait_ge(mixed_ready, b + 1)
                pe.wait_ge(v_read, v_count)
                for half in range(2):
                    mm = pe.transpose(ps_v[:, half * P:(half + 1) * P],
                                      mixed[:, half].rearrange("p h d -> p (h d)"), keep.identity[:, :])
                mm.then_inc(mixed_t_ps, 1)
                pe.wait_ge(mixed_t_ready, b + 1)
                pe.matmul(ps_v[:, N0:2 * N0], w_m[:, :], mixed_t[:, :], start=True, stop=True).then_inc(merged, 1)

            def step(i, at, looped=False):
                first, second, third = stages(i, looped)
                if first is not None:
                    project(at(first))
                    pe.wait_ge(rope_read, at(first)[0] + 1)
                for u in range(UNITS):
                    tiles(at(second) if second is not None else None, at(third) if third is not None else None, u)
                    if third is not None and u % 4 == 1 and u > 4:
                        mix(at(third), u // 4 - 1)
                if second is not None:
                    turn_top(at(second))
                if third is not None:
                    mix(at(third), COUPLES - 1)
                    turn_outs(at(third))
                    merge(at(third), at(first)[0] + 1 if first is not None else NB)

            steps(pe, step)

        @block.vector
        def _(dve):
            def normalise(b):
                after(dve, q_ready, b)
                dve.tensor_scalar(xn[:, :], keep.x[:, bass.ds(b, 1), :], keep.moments[:, bass.ds(b, 1), 0:1],
                                  keep.rstd[:, bass.ds(b, 1)], ALU.subtract, ALU.mult).then_inc(xn_ready, 1)

            dve.memset(q_stack[:, :, :, :], 1.0)
            dve.memset(k_stack[:, :, :, :], 1.0)
            dve.memset(values[:, :, :, :, :], 0.0).then_inc(made, 1)
            dve.wait_ge(made, 1)
            dve.memset(values[:, :, :, :, HD0:HD0 + 1], 1.0).then_inc(made, 1)
            normalise(0)
            dve.wait_ge(w_in, 8 * 16)
            dve.tensor_scalar(rope[:, 1, :], rope[:, 1, :], sign[:, :], None, ALU.mult).then_inc(made, 1)
            dve.tensor_scalar(gate_bm[:, :], b_m[:, :], keep.gate[:, 0:1], None, ALU.mult).then_inc(made, 1)
            dve.wait_ge(made, 4)

            def rotate(at, more):
                b, slot, trip = at
                after(dve, qk_sum, b)
                for o, ready, read in ((0, q_ready, q_read), (1, k_ready, rope_read)):
                    dve.wait_ge(ready, b + 1)
                    for k in range(2):
                        op = dve.scalar_tensor_tensor(turned[:, o, k, :], ps_qk[:, k * N0:(k + 1) * N0],
                                                      b_qk[:, 2 * o + k:2 * o + k + 1], rope[:, k, :], ALU.add, ALU.mult)
                    op.then_inc(read, 1)
                dve.wait_ge(v_ready, b + 1)
                after(dve, pv_done, COUPLES * (b - 2))
                dve.tensor_tensor(values[:, slot, :, :, 0:HD0],
                                  ps_v[:, 0:2 * P].rearrange("p (m h d) -> p m h d", m=2, h=HEADS0),
                                  b_v[:, :].rearrange("p (o h d) -> p o h d", o=1, h=HEADS0).broadcast_to([P, 2, HEADS0, HD0]),
                                  ALU.add).then_inc(v_read, 1)
                if more:
                    normalise(b + 1)

            def maxima(at, u):
                b, slot, trip = at
                half, couple, j = u // 8, u // 2 % 4, u % 2
                dve.wait_ge(score_ready, b * UNITS + u + 1)
                if u == 0:
                    after(dve, top_split, b)
                dve.tensor_reduce(top[:, half, j, 2 * couple:2 * couple + 2], ps_score[j][:, :].rearrange("p (k n) -> p k n", k=2),
                                  AX, ALU.max).then_inc(score_read, 1)

            def finish(at):
                b, slot, trip = at
                dve.wait_ge(outs_t, b + 1)
                out = ps_o[:, :, :].rearrange("p m (h d) -> p m h d", h=HEADS0)
                dve.reciprocal(sums_inv[:, :, :], out[:, :, :, HD0]).then_inc(norm_step, 1)
                dve.wait_ge(norm_step, b + 1)
                after(dve, mixed_t_ps, b)
                dve.tensor_tensor(mixed[:, :, :, :], out[:, :, :, 0:HD0],
                                  sums_inv[:, :, :].unsqueeze(3).broadcast_to([P, 2, HEADS0, HD0]),
                                  ALU.mult).then_inc(mixed_ready, 1)
                dve.wait_ge(merged, b + 1)
                dve.wait_ge(x_plus_ready, b + 1)
                dve.scalar_tensor_tensor(keep.x[:, bass.ds(b, 1), :], ps_v[:, N0:2 * N0].unsqueeze(1), keep.gate[:, 0:1],
                                         x_plus[:, 0:1, :], ALU.mult, ALU.add).then_inc(x_done, 1)
                alone(dve, x_done, b + 1, stood)
                layer_stats(dve, stats, keep.moments, keep.x[:, bass.ds(b, 1), :], b, stats_step, stood)

            def step(i, at, looped=False):
                first, second, third = stages(i, looped)
                if first is not None:
                    rotate(at(first), looped or first < NB - 1)
                if second is not None:
                    for u in range(UNITS):
                        maxima(at(second), u)
                if third is not None:
                    finish(at(third))

            steps(dve, step)

        @block.scalar
        def _(act):
            def high(at):
                b, slot, trip = at
                act.wait_ge(qk_sum, b + 1)
                act.activation(parts[:, :, 0, :], qk[:, :, :], ACT.Copy).then_inc(high_ready, 1)

            def middle(at):
                b, slot, trip = at
                act.wait_ge(rest_ready, b + 1)
                act.activation(parts[:, :, 1, :], rest[:, :, :], ACT.Copy).then_inc(mid_ready, 1)

            def exponent(at, u):
                b, slot, trip = at
                act.wait_ge(prob_ready, b * UNITS + u + 1)
                couple, half, j = u // 4, u // 2 % 2, 1 - u % 2
                after(act, pv_done, b * COUPLES + couple - 1)
                act.activation(probs[:, couple % 2, half, j], ps_prob[j][:, :].rearrange("p (k n) -> p k n", k=2), ACT.Exp,
                               scale=float(HD0) ** -0.5).then_inc(prob_read, 1)

            def step(i, at, looped=False):
                first, second, third = stages(i, looped)
                for u in range(UNITS):
                    if third is not None:
                        exponent(at(third), u)
                    if first is not None and u == 2:
                        if isinstance(at(first)[0], int):
                            b, slot, trip = at(first)
                            if b:
                                act.wait_ge(scratch_in[(b - 1) % 3], 192 * ((b - 1) // 3 + 1))
                        else:
                            pb, pslot, ptrip = at(first - 1)
                            act.wait_ge(scratch_in[pslot], 192 * (ptrip + 1))
                        high(at(first))
                    if first is not None and u == 5:
                        middle(at(first))
                if second is not None:
                    b, slot, trip = at(second)
                    act.wait_ge(top_t, b + 1)
                    if looped:
                        pb, pslot, ptrip = at(second - 1)
                        act.wait_ge(top_scratch_in[pslot], 16 * (ptrip + 1))
                    elif second > 0:
                        act.wait_ge(top_scratch_in[(b - 1) % 3], 16 * ((b - 1) // 3 + 1))
                    act.activation(top_rows[:, :], ps_qk[0:3 * HEADS0, :].bitcast(BF16)[:, 0:N0], ACT.Copy).then_inc(top_rows_ready, 1)
                if third is not None:
                    b, slot, trip = at(third)
                    for half in range(2):
                        act.wait_ge(pv_done, b * COUPLES + 2 * half + 2)
                        after(act, outs_t, b)
                        act.activation(outs[:, 2 * half:2 * half + 2, :], ps_o[:, half, :].rearrange("p (c n) -> p c n", c=2),
                                       ACT.Copy).then_inc(outs_ready, 1)
                    act.wait_ge(mixed_t_ps, b + 1)
                    act.activation(mixed_t[:, :], ps_v[:, 0:N0], ACT.Copy).then_inc(mixed_t_ready, 1)

            steps(act, step)

        @block.gpsimd
        def _(pool):
            pool.wait_ge(made, 4)

            def split(at, scratch_prev):
                b, slot, trip = at
                pool.wait_ge(rope_read, b + 1)
                pool.tensor_tensor(qk[:, :, :], turned[:, :, 0, :], turned[:, :, 1, :], ALU.add).then_inc(qk_sum, 1)
                pool.wait_ge(high_ready, b + 1)
                pool.tensor_tensor(rest[:, :, :], qk[:, :, :], parts[:, :, 0, :], ALU.subtract).then_inc(rest_ready, 1)
                pool.wait_ge(mid_ready, b + 1)
                pool.tensor_tensor(parts[:, :, 2, :], rest[:, :, :], parts[:, :, 1, :], ALU.subtract).then_inc(parts_ready, 1)

            def split_top(at):
                b, slot, trip = at
                pool.wait_ge(score_read, UNITS * (b + 1))
                alone(pool, top_t, b, stood)
                flat = top[:, :, :, :].rearrange("p m j q -> p m (j q)")
                pool.tensor_scalar(top_parts[:, :, 0, :], flat, -1.0, None, ALU.mult).then_inc(pool_step, 1)
                pool.wait_ge(pool_step, 4 * b + 1)
                pool.tensor_tensor(top_rest[:, :, :], flat, top_parts[:, :, 0, :], ALU.add).then_inc(pool_step, 1)
                alone(pool, pool_step, 4 * b + 2, stood)
                pool.tensor_scalar(top_parts[:, :, 1, :], top_rest[:, :, :], -1.0, None, ALU.mult).then_inc(pool_step, 1)
                pool.wait_ge(pool_step, 4 * b + 3)
                pool.tensor_tensor(top_rest[:, :, :], top_rest[:, :, :], top_parts[:, :, 1, :], ALU.add).then_inc(pool_step, 1)
                alone(pool, pool_step, 4 * b + 4, stood)
                pool.tensor_scalar(top_parts[:, :, 2, :], top_rest[:, :, :], -1.0, None, ALU.mult).then_inc(top_split, 1)

            def step(i, at, looped=False):
                first, second, third = stages(i, looped)
                if third is not None:
                    b, slot, trip = at(third)
                    alone(pool, x_done, b, stood)
                    pool.tensor_tensor(x_plus[:, 0:1, :], keep.x[:, bass.ds(b, 1), :],
                                       gate_bm[:, 0:1].unsqueeze(2).broadcast_to([P, 1, N0]), ALU.add).then_inc(x_plus_ready, 1)
                if first is not None:
                    split(at(first), None)
                if second is not None:
                    split_top(at(second))

            steps(pool, step)
            pool.wait_ge(stats_step, 3 * NB)
            inverse_deviation(pool, keep, 1)


F0 = 1024
Q_EPS = 1e-5
KD, KF = D // P, F0 // P


def layer0_ffn(nc, keep, w):
    with ExitStack() as ctx:
        sem = lambda n: ctx.enter_context(nc.semaphore("f_" + n))
        sems = lambda n, k: [sem(f"{n}{i}") for i in range(k)]
        sb = lambda n, shape, dt=F32: ctx.enter_context(nc.sbuf_tensor("f_" + n, shape, dt))
        ps = lambda n, shape, dt=F32: ctx.enter_context(nc.psum_tensor("f_" + n, shape, dt))
        WIDE = KD * F0

        raw = sb("raw", [P, 3, WIDE])
        rounded = sb("rounded", [P, WIDE])
        ternary = sb("ternary", [P, 3, WIDE], BF16)
        w_gu = [ternary[:, k, :].rearrange("p (k f) -> p k f", k=KD) for k in range(2)]
        w_d = ternary[:, 2, :].rearrange("p (k n) -> p k n", k=KF)
        w_abs = sb("w_abs", [P, 3])
        w_scale = sb("w_scale", [P, 3])
        w_inv = sb("w_inv", [P, 3])
        up_127 = sb("up_127", [P, 1])
        down_gate = sb("down_gate", [P, 1])
        xn = sb("xn", [P, D])
        x_top = sb("x_top", [P, 1])
        x_scale = sb("x_scale", [P, 2, 1])
        x_inv = sb("x_inv", [P, 2, 1])
        gate_scale = sb("gate_scale", [P, 2, 3])
        x_round = sb("x_round", [P, D])
        x_int = sb("x_int", [P, D], BF16)
        x_int_t = sb("x_int_t", [P, 2, KD, P], BF16)
        silu = sb("silu", [P, F0])
        hidden = sb("hidden", [P, 2, F0])
        h_top = sb("h_top", [P, 1])
        h_scale = sb("h_scale", [P, 2, 1])
        h_inv = sb("h_inv", [P, 1])
        h_mult = sb("h_mult", [P, 2, 1])
        out_scale = sb("out_scale", [P, 2, 1])
        h_round = sb("h_round", [P, F0])
        h_int = sb("h_int", [P, F0], BF16)
        h_int_t = sb("h_int_t", [P, KF, P], BF16)
        stats = sb("stats", [P, 8])
        zeros = sb("zeros", [P, ZERO_ROWS * D])

        ps_gate = ps("ps_gate", [P, F0])
        ps_up = ps("ps_up", [P, F0])
        ps_x = ps("ps_x", [P, KD, P], BF16)
        ps_h = ps("ps_h", [P, KF, P], BF16)
        ps_down = ps("ps_down", [P, 512])

        w_in = sems("w_in", 3)
        w_summed, w_total, w_step, w_ready = sem("w_summed"), sem("w_total"), sem("w_step"), sem("w_ready")
        w_rounded, w_cut = sem("w_rounded"), sem("w_cut")
        x_step, scales_ready = sem("x_step"), sem("scales_ready")
        x_round_ready, x_int_ready, x_t_ready, x_t_read = (
            sem("x_round_ready"), sem("x_int_ready"), sem("x_t_ready"), sem("x_t_read"))
        gate_ready, up_ready, silu_ready, hidden_ready = (
            sem("gate_ready"), sem("up_ready"), sem("silu_ready"), sem("hidden_ready"))
        h_step, h_mult_ready, out_scale_ready = sem("h_step"), sem("h_mult_ready"), sem("out_scale_ready")
        h_round_ready, h_int_ready, h_t_ready, h_t_read = (
            sem("h_round_ready"), sem("h_int_ready"), sem("h_t_ready"), sem("h_t_read"))
        down_ready, x_done, stats_step = sem("down_ready"), sem("x_done"), sem("stats_step")
        zeros_made, filled = sem("zeros_made"), sem("filled")
        stood = keep.stood
        block = ctx.enter_context(nc.Block())

        def steps(step):
            def run(eng):
                for i in range(-2, 2):
                    step(i, lambda b: (b, b % 2))
                with eng.Fori(1, 7) as t:
                    for c in range(2):
                        step(c, lambda b: (t * 2 + b, b % 2), looped=True)
                for i in (14, 15):
                    step(i, lambda b: (b, b % 2))
            return run

        def stages(i, looped):
            if looped:
                return i + 2, i + 1, i
            return tuple(b if 0 <= b < NB else None for b in (i + 2, i + 1, i))

        @block.sync
        def _(sp):
            for k, (src, chunks) in enumerate(((w.gate, KD), (w.up, KD), (w.down, KF))):
                sp.dma_start(raw[:, k, :].rearrange("p (k f) -> p k f", k=chunks),
                             src.rearrange("(k p) f -> p k f", p=P)).then_inc(w_in[k], 16)
            sp.wait_ge(zeros_made, 1)
            share = TOKEN_ROW // P
            for n in range(0, share, share // 4):
                rows = keep.rows[0:TOKEN_ROW, :].rearrange("(p n) d -> p n d", p=P)[:, n:n + share // 4, :]
                sp.dma_start(rows.rearrange("p (a n) d -> p a (n d)", n=ZERO_ROWS),
                             zeros[:, :].unsqueeze(1).broadcast_to([P, share // 4 // ZERO_ROWS, ZERO_ROWS * D])).then_inc(filled, 16)
            sp.wait_ge(filled, 4 * 16)

        @block.tensor
        def _(pe):
            pe.wait_ge(w_summed, 3)
            pe.matmul(ps_down[:, 0:3], keep.ones[:, :], w_abs[:, :], start=True, stop=True).then_inc(w_total, 1)
            pe.wait_ge(w_ready, 3)

            def gate_up(at):
                b, slot = at
                pe.wait_ge(x_t_read, b + 1)
                after(pe, silu_ready, b)
                for k, (dst, ready) in enumerate(((ps_gate, gate_ready), (ps_up, up_ready))):
                    if k:
                        after(pe, hidden_ready, b)
                    for n in range(0, F0, 512):
                        for c in range(KD):
                            mm = pe.matmul(dst[:, n:n + 512], x_int_t[:, slot, c, :], w_gu[k][:, c, n:n + 512],
                                           start=(c == 0), stop=(c == KD - 1))
                    mm.then_inc(ready, 1)

            def turn_x(at):
                b, slot = at
                pe.wait_ge(x_int_ready, b + 1)
                after(pe, x_t_read, b)
                for c in range(KD):
                    mm = pe.transpose(ps_x[:, c, :], x_int[:, c * P:(c + 1) * P], keep.identity_bf[:, :])
                mm.then_inc(x_t_ready, 1)

            def down(at):
                b, slot = at
                pe.wait_ge(h_int_ready, b + 1)
                for c in range(KF):
                    mm = pe.transpose(ps_h[:, c, :], h_int[:, c * P:(c + 1) * P], keep.identity_bf[:, :])
                mm.then_inc(h_t_ready, 1)
                pe.wait_ge(h_t_read, b + 1)
                after(pe, x_done, b)
                for c in range(KF):
                    mm = pe.matmul(ps_down[:, 0:D], h_int_t[:, c, :], w_d[:, c, :], start=(c == 0), stop=(c == KF - 1))
                mm.then_inc(down_ready, 1)

            def step(i, at, looped=False):
                first, second, third = stages(i, looped)
                if second is not None:
                    gate_up(at(second))
                if first is not None:
                    turn_x(at(first))
                if third is not None:
                    down(at(third))

            steps(step)(pe)

        @block.vector
        def _(dve):
            for k in range(3):
                dve.wait_ge(w_in[k], 16)
                dve.tensor_reduce(w_abs[:, k:k + 1], raw[:, k, :], AX, ALU.add, apply_absolute_value=True).then_inc(w_summed, 1)
            dve.wait_ge(w_total, 1)
            dve.tensor_scalar(w_scale[:, :], ps_down[:, 0:3], 1.0 / (D * F0), Q_EPS, ALU.mult, ALU.add).then_inc(w_step, 1)
            dve.wait_ge(w_step, 1)
            dve.reciprocal(w_inv[:, :], w_scale[:, :]).then_inc(w_step, 1)
            dve.tensor_scalar(up_127[:, :], w_scale[:, 1:2], 1.0 / 127.0, None, ALU.mult).then_inc(w_step, 1)
            dve.tensor_scalar(down_gate[:, :], w_scale[:, 2:3], keep.gate[:, 2:3], None, ALU.mult).then_inc(w_step, 1)
            for k in range(3):
                dve.wait_ge(w_rounded, k + 1)
                dve.tensor_scalar(rounded[:, :], rounded[:, :], MAGIC, -1.0, ALU.subtract, ALU.max).then_inc(w_cut, 1)
                dve.wait_ge(w_cut, k + 1)
                dve.tensor_scalar(ternary[:, k, :], rounded[:, :], 1.0, None, ALU.min).then_inc(w_ready, 1)

            def quantise_x(at):
                b, slot = at
                after(dve, x_round_ready, b)
                dve.tensor_scalar(xn[:, :].unsqueeze(1), keep.x[:, bass.ds(b, 1), :], keep.moments[:, bass.ds(b, 1), 0:1],
                                  keep.rstd[:, bass.ds(b, 1)], ALU.subtract, ALU.mult).then_inc(x_step, 1)
                dve.wait_ge(x_step, 4 * b + 1)
                dve.tensor_reduce(x_top[:, :], xn[:, :], AX, ALU.max, apply_absolute_value=True).then_inc(x_step, 1)
                dve.wait_ge(x_step, 4 * b + 2)
                dve.tensor_scalar(x_scale[:, slot, :], x_top[:, :], 1.0 / 127.0, Q_EPS, ALU.mult, ALU.add).then_inc(x_step, 1)
                dve.wait_ge(x_step, 4 * b + 3)
                dve.reciprocal(x_inv[:, slot, :], x_scale[:, slot, :]).then_inc(x_step, 1)

            def hide(at):
                b, slot = at
                dve.wait_ge(silu_ready, b + 1)
                dve.wait_ge(up_ready, b + 1)
                dve.tensor_tensor(hidden[:, slot, :], silu[:, :], ps_up[:, :], ALU.mult).then_inc(hidden_ready, 1)
                dve.wait_ge(hidden_ready, b + 1)
                dve.tensor_reduce(h_top[:, :], hidden[:, slot, :], AX, ALU.max, apply_absolute_value=True).then_inc(h_step, 1)
                dve.wait_ge(h_step, 3 * b + 1)
                dve.wait_ge(scales_ready, 3 * b + 3)
                after(dve, out_scale_ready, b - 1)
                dve.tensor_scalar(h_scale[:, slot, :], h_top[:, :], gate_scale[:, slot, 2:3], Q_EPS, ALU.mult,
                                  ALU.add).then_inc(h_step, 1)
                dve.wait_ge(h_step, 3 * b + 2)
                dve.reciprocal(h_inv[:, :], h_scale[:, slot, :]).then_inc(h_step, 1)
                dve.wait_ge(h_step, 3 * b + 3)
                dve.tensor_scalar(h_mult[:, slot, :], h_inv[:, :], gate_scale[:, slot, 1:2], None, ALU.mult).then_inc(h_mult_ready, 1)

            def finish(at):
                b, slot = at
                dve.wait_ge(down_ready, b + 1)
                dve.wait_ge(out_scale_ready, b + 1)
                dve.scalar_tensor_tensor(keep.x[:, bass.ds(b, 1), :], ps_down[:, 0:D].unsqueeze(1), out_scale[:, slot, :],
                                         keep.x[:, bass.ds(b, 1), :], ALU.mult, ALU.add).then_inc(x_done, 1)
                alone(dve, x_done, b + 1, stood)
                layer_stats(dve, stats, keep.moments, keep.x[:, bass.ds(b, 1), :], b, stats_step, stood)

            def step(i, at, looped=False):
                first, second, third = stages(i, looped)
                if first is not None:
                    quantise_x(at(first))
                if second is not None:
                    hide(at(second))
                if third is not None:
                    finish(at(third))

            steps(step)(dve)

        @block.scalar
        def _(act):
            act.wait_ge(w_step, 4)
            for k in range(3):
                after(act, w_ready, k)
                act.activation(rounded[:, :], raw[:, k, :], ACT.Copy, bias=MAGIC, scale=w_inv[:, k:k + 1]).then_inc(w_rounded, 1)

            def step(i, at, looped=False):
                first, second, third = stages(i, looped)
                if third is not None:
                    b, slot = at(third)
                    act.wait_ge(h_mult_ready, b + 1)
                    after(act, h_int_ready, b)
                    act.activation(h_round[:, :], hidden[:, slot, :], ACT.Copy, bias=MAGIC,
                                   scale=h_mult[:, slot, :]).then_inc(h_round_ready, 1)
                if first is not None:
                    b, slot = at(first)
                    act.wait_ge(x_step, 4 * b + 4)
                    after(act, x_int_ready, b)
                    act.activation(x_round[:, :], xn[:, :], ACT.Copy, bias=MAGIC,
                                   scale=x_inv[:, slot, :]).then_inc(x_round_ready, 1)
                if second is not None:
                    b, slot = at(second)
                    act.wait_ge(gate_ready, b + 1)
                    act.wait_ge(scales_ready, 3 * b + 3)
                    after(act, hidden_ready, b)
                    act.activation(silu[:, :], ps_gate[:, :], ACT.Silu, scale=gate_scale[:, slot, 0:1]).then_inc(silu_ready, 1)
                if first is not None:
                    b, slot = at(first)
                    act.wait_ge(x_t_ready, b + 1)
                    after(act, up_ready, b - 1)
                    act.activation(x_int_t[:, slot], ps_x[:, :, :], ACT.Copy).then_inc(x_t_read, 1)
                if third is not None:
                    b, slot = at(third)
                    act.wait_ge(h_t_ready, b + 1)
                    after(act, down_ready, b)
                    act.activation(h_int_t[:, :, :], ps_h[:, :, :], ACT.Copy).then_inc(h_t_read, 1)

            steps(step)(act)

        @block.gpsimd
        def _(pool):
            pool.memset(zeros[:, :], 0.0).then_inc(zeros_made, 1)
            pool.wait_ge(w_step, 4)

            def step(i, at, looped=False):
                first, second, third = stages(i, looped)
                if third is not None:
                    b, slot = at(third)
                    pool.wait_ge(h_round_ready, b + 1)
                    alone(pool, h_t_ready, b, stood)
                    pool.sem_inc(stood, 1)
                    pool.tensor_scalar(h_int[:, :], h_round[:, :], MAGIC, None, ALU.subtract).then_inc(h_int_ready, 1)
                if first is not None:
                    b, slot = at(first)
                    pool.wait_ge(x_round_ready, b + 1)
                    alone(pool, x_t_ready, b, stood)
                    pool.sem_inc(stood, 1)
                    pool.tensor_scalar(x_int[:, :], x_round[:, :], MAGIC, None, ALU.subtract).then_inc(x_int_ready, 1)
                    after(pool, h_mult_ready, b - 1)
                    for k, other in enumerate((w_scale[:, 0:1], w_scale[:, 1:2], up_127[:, :])):
                        pool.tensor_tensor(gate_scale[:, slot, k:k + 1], x_scale[:, slot, :], other, ALU.mult).then_inc(scales_ready, 1)
                if second is not None:
                    b, slot = at(second)
                    pool.wait_ge(h_step, 3 * b + 2)
                    after(pool, x_done, b - 1)
                    pool.tensor_tensor(out_scale[:, slot, :], h_scale[:, slot, :], down_gate[:, :], ALU.mult).then_inc(out_scale_ready, 1)

            steps(step)(pool)
            pool.wait_ge(stats_step, 3 * NB)
            inverse_deviation(pool, keep, 2)


HEADS1, GROUPS, HD1 = 16, 4, 128
SHARE = HEADS1 // GROUPS
WIDTH = SHARE * HD1
RMS_EPS = 1e-6


def layer1_attention(nc, keep, w):
    with ExitStack() as ctx:
        sem = lambda n: ctx.enter_context(nc.semaphore("g_" + n))
        sems = lambda n, k: [sem(f"{n}{i}") for i in range(k)]
        sb = lambda n, shape, dt=F32: ctx.enter_context(nc.sbuf_tensor("g_" + n, shape, dt))
        bank = lambda n: ctx.enter_context(nc.psum_tensor("g_" + n, [P, 512], F32))

        w_q = sb("w_q", [P, KD, HEADS1 * HD1])
        w_k = sb("w_k", [P, KD, WIDTH])
        w_v = sb("w_v", [P, KD, WIDTH])
        w_o = sb("w_o", [P, HEADS1, D])
        norms = sb("norms", [P, 2])
        k_weight = sb("k_weight", [P, 1])
        ctx_t = sb("ctx_t", [P, 2, KD, P])
        xn = sb("xn", [P, D])
        x_t = sb("x_t", [P, KD, P])
        square = sb("square", [P, 2, SHARE, HD1])
        power = sb("power", [P, 2, SHARE])
        inverse = sb("inverse", [P, 2, SHARE])
        normed = sb("normed", [P, 2, SHARE, HD1])
        q_t = sb("q_t", [P, 2, GROUPS, WIDTH])
        k_t = sb("k_t", [P, 2, GROUPS, P])
        values = sb("values", [P, 2, WIDTH])
        bias = sb("bias", [P, 2, SHARE])
        probs = sb("probs", [P, 2, SHARE, P])
        sums = sb("sums", [P, 2, SHARE])
        sums_inv = sb("sums_inv", [P, 2, SHARE])
        weights = sb("weights", [P, 2, SHARE, P])
        weights_t = sb("weights_t", [P, 2, WIDTH])
        out_t = sb("out_t", [P, 2, SHARE, P])
        stats = sb("stats", [P, 8])

        ps_proj = [bank("ps_proj0"), bank("ps_proj1")]
        ps_turn = bank("ps_turn")
        ps_score = [bank("ps_score0"), bank("ps_score1")]
        ps_w = bank("ps_w")
        ps_out = bank("ps_out")
        ps_x = bank("ps_x")

        w_in, made = sem("w_in"), sem("made")
        ctx_in = sems("ctx_in", 2)
        xn_ready, x_turned, x_t_ready = sem("xn_ready"), sem("x_turned"), sem("x_t_ready")
        proj_ready, squared, powered, inv_step, normed_ready, turned, turned_read = (
            sem("proj_ready"), sem("squared"), sem("powered"), sem("inv_step"), sem("normed_ready"), sem("turned"),
            sem("turned_read"))
        v_ready, v_read = sem("v_ready"), sem("v_read")
        score_ready, bias_ready, probs_ready, inv_ready, weights_ready = (
            sem("score_ready"), sem("bias_ready"), sem("probs_ready"), sem("inv_ready"), sem("weights_ready"))
        w_turned, w_t_ready, out_ready, out_read, merged = (
            sem("w_turned"), sem("w_t_ready"), sem("out_ready"), sem("out_read"), sem("merged"))
        x_done, stats_step = sem("x_done"), sem("stats_step")
        stood = keep.stood
        block = ctx.enter_context(nc.Block())
        NP = 1 + GROUPS

        def steps(step):
            def run(eng):
                for i in (-1, 0):
                    step(i, lambda b: (b, b % 2, b // 2))
                with eng.Fori(0, 6) as t:
                    for c in (1, 2):
                        step(c, lambda b: (t * 2 + b, b % 2, t + b // 2), looped=True)
                for i in (13, 14, 15):
                    step(i, lambda b: (b, b % 2, b // 2))
            return run

        def stages(i, looped):
            if looped:
                return i + 1, i
            return tuple(b if 0 <= b < NB else None for b in (i + 1, i))

        @block.sync
        def _(sp):
            for dst, src in ((norms[:, :], w.norms), (w_k[:, :, :], w.k.rearrange("(k p) n -> p k n", p=P)),
                             (w_v[:, :, :], w.v.rearrange("(k p) n -> p k n", p=P)),
                             (w_q[:, :, :], w.q.rearrange("(k p) n -> p k n", p=P)),
                             (w_o[:, :, :], w.o.rearrange("(h p) n -> p h n", p=P))):
                sp.dma_start(dst, src).then_inc(w_in, 16)

            def load_ctx(at):
                b, slot, trip = at
                alone(sp, v_ready, b - 1, stood)
                sp.dma_start(ctx_t[:, slot], w.ctx_t[bass.ds(b, 1)].rearrange("b (k p) n -> p (b k) n", p=P)).then_inc(ctx_in[slot], 16)

            load_ctx((0, 0, 0))

            def step(i, at, looped=False):
                if looped or i + 2 < NB:
                    load_ctx(at(i + 2))
            for i in (-1, 0):
                step(i, lambda b: (b, b % 2, b // 2))
            with sp.Fori(0, 6) as t:
                for c in (1, 2):
                    step(c, lambda b: (t * 2 + b, b % 2, t + b // 2), looped=True)
            step(13, lambda b: (b, b % 2, b // 2))

        @block.tensor
        def _(pe):
            pe.wait_ge(w_in, 5 * 16)

            def turn_x(at):
                b, slot, trip = at
                pe.wait_ge(xn_ready, b + 1)
                after(pe, turned_read, NP * b)
                for c in range(KD):
                    mm = pe.transpose(ps_turn[:, c * P:(c + 1) * P], xn[:, c * P:(c + 1) * P], keep.identity[:, :])
                mm.then_inc(x_turned, 1)

            def project(at, n):
                b, slot, trip = at
                if n == 0:
                    pe.wait_ge(ctx_in[slot], 16 * (trip + 1))
                elif n == 1:
                    pe.wait_ge(x_t_ready, b + 1)
                if n == 1:
                    pe.wait_ge(v_read, b + 1)
                else:
                    after(pe, normed_ready, NP * b + n - 2 + (n == 0))
                bank = ps_proj[0 if n == 0 else n % 2]
                for c in range(KD):
                    if n == 0:
                        mm = pe.matmul(bank[:, :], ctx_t[:, slot, c, :], w_k[:, c, :], start=(c == 0), stop=(c == KD - 1))
                    else:
                        mm = pe.matmul(bank[:, :], x_t[:, c, :], w_q[:, c, (n - 1) * WIDTH:n * WIDTH],
                                       start=(c == 0), stop=(c == KD - 1))
                mm.then_inc(proj_ready, 1)

            def project_v(at):
                b, slot, trip = at
                after(pe, normed_ready, NP * b)
                for c in range(KD):
                    mm = pe.matmul(ps_proj[1][:, :], ctx_t[:, slot, c, :], w_v[:, c, :], start=(c == 0), stop=(c == KD - 1))
                mm.then_inc(v_ready, 1)

            def turn_normed(at, n):
                b, slot, trip = at
                pe.wait_ge(normed_ready, NP * b + n + 1)
                if n == 0:
                    pe.wait_ge(x_t_ready, b + 1)
                else:
                    pe.wait_ge(turned_read, NP * b + n)
                for h in range(SHARE):
                    mm = pe.transpose(ps_turn[:, h * P:(h + 1) * P], normed[:, n % 2, h, :], keep.identity[:, :])
                mm.then_inc(turned, 1)

            def score(at, g):
                b, slot, trip = at
                if g == 0:
                    pe.wait_ge(turned_read, NP * (b + 1))
                after(pe, probs_ready, GROUPS * b + g - 1)
                for h in range(SHARE):
                    mm = pe.matmul(ps_score[g % 2][:, h * P:(h + 1) * P], q_t[:, slot, g, h * P:(h + 1) * P], k_t[:, slot, g, :],
                                   start=True, stop=True)
                mm.then_inc(score_ready, 1)

            def turn_weights(at, g):
                b, slot, trip = at
                n = GROUPS * b + g
                pe.wait_ge(weights_ready, n + 1)
                after(pe, w_t_ready, n)
                for h in range(SHARE):
                    mm = pe.transpose(ps_w[:, h * P:(h + 1) * P], weights[:, g % 2, h, :], keep.identity[:, :])
                mm.then_inc(w_turned, 1)

            def mix(at, g):
                b, slot, trip = at
                n = GROUPS * b + g
                pe.wait_ge(w_t_ready, n + 1)
                after(pe, out_read, n)
                pe.matmul(ps_out[:, :], values[:, slot, g * P:(g + 1) * P], weights_t[:, g % 2, :],
                          start=True, stop=True).then_inc(out_ready, 1)

            def merge(at, g):
                b, slot, trip = at
                pe.wait_ge(out_read, GROUPS * b + g + 1)
                if g == 0:
                    after(pe, x_done, b)
                for h in range(SHARE):
                    mm = pe.matmul(ps_x[:, 0:D], out_t[:, g % 2, h, :], w_o[:, SHARE * g + h, :],
                                   start=(g == 0 and h == 0), stop=(g == GROUPS - 1 and h == SHARE - 1))
                mm.then_inc(merged, 1)

            def step(i, at, looped=False):
                first, second = stages(i, looped)
                f = at(first) if first is not None else None
                s = at(second) if second is not None else None
                if s:
                    score(s, 0)
                if f:
                    turn_x(f)
                    project(f, 0)
                    project_v(f)
                for g in range(GROUPS):
                    if s and g + 1 < GROUPS:
                        score(s, g + 1)
                    if f:
                        project(f, g + 1)
                    if s:
                        turn_weights(s, g)
                    if f:
                        turn_normed(f, g)
                    if s:
                        mix(s, g)
                        if g:
                            merge(s, g - 1)
                if f:
                    turn_normed(f, GROUPS)
                if s:
                    merge(s, GROUPS - 1)

            steps(step)(pe)

        @block.vector
        def _(dve):
            def normalise(b):
                after(dve, x_turned, b)
                dve.tensor_scalar(xn[:, :].unsqueeze(1), keep.x[:, bass.ds(b, 1), :], keep.moments[:, bass.ds(b, 1), 0:1],
                                  keep.rstd[:, bass.ds(b, 1)], ALU.subtract, ALU.mult).then_inc(xn_ready, 1)

            normalise(0)
            dve.wait_ge(w_in, 16 * 5)
            dve.tensor_scalar(k_weight[:, :], norms[:, 0:1], norms[:, 1:2], float(HD1) ** -0.5, ALU.mult, ALU.mult).then_inc(made, 1)

            def power_of(at, n):
                b, slot, trip = at
                dve.wait_ge(squared, NP * b + n + 1)
                after(dve, normed_ready, NP * b + n - 1)
                dve.tensor_reduce(power[:, n % 2, :], square[:, n % 2], AX, ALU.add).then_inc(powered, 1)

            def norm(at, n):
                b, slot, trip = at
                dve.wait_ge(inv_step, 2 * (NP * b + n) + 2)
                after(dve, turned, NP * b + n - 1)
                dve.tensor_tensor(normed[:, n % 2], ps_proj[n % 2][:, :].rearrange("p (h d) -> p h d", h=SHARE),
                                  inverse[:, n % 2, :].unsqueeze(2).broadcast_to([P, SHARE, HD1]), ALU.mult).then_inc(normed_ready, 1)

            def top(at, g):
                b, slot, trip = at
                n = GROUPS * b + g
                dve.wait_ge(score_ready, n + 1)
                after(dve, probs_ready, n - 1)
                dve.tensor_reduce(bias[:, g % 2, :], ps_score[g % 2][:, :].rearrange("p (h m) -> p h m", h=SHARE), AX, ALU.max,
                                  negate=True).then_inc(bias_ready, 1)

            def invert(at, g):
                b, slot, trip = at
                n = GROUPS * b + g
                dve.wait_ge(probs_ready, n + 1)
                after(dve, weights_ready, n - 1)
                dve.reciprocal(sums_inv[:, g % 2, :], sums[:, g % 2, :]).then_inc(inv_ready, 1)

            def weights_out(at, g):
                b, slot, trip = at
                n = GROUPS * b + g
                dve.wait_ge(w_turned, n + 1)
                after(dve, out_ready, n - 1)
                dve.tensor_copy(weights_t[:, g % 2, :], ps_w[:, :]).then_inc(w_t_ready, 1)

            def step(i, at, looped=False):
                first, second = stages(i, looped)
                f = at(first) if first is not None else None
                s = at(second) if second is not None else None
                if s:
                    top(s, 0)
                if f:
                    power_of(f, 0)
                for g in range(GROUPS):
                    if s:
                        if g + 1 < GROUPS:
                            top(s, g + 1)
                        invert(s, g)
                    if f:
                        norm(f, g)
                        power_of(f, g + 1)
                    if s:
                        weights_out(s, g)
                if f:
                    norm(f, GROUPS)
                    if looped or first + 1 < NB:
                        normalise(at(first)[0] + 1)
                if s:
                    b = s[0]
                    dve.wait_ge(merged, GROUPS * (b + 1))
                    dve.scalar_tensor_tensor(keep.x[:, bass.ds(b, 1), :], ps_x[:, 0:D].unsqueeze(1), keep.gate[:, 1:2],
                                             keep.x[:, bass.ds(b, 1), :], ALU.mult, ALU.add).then_inc(x_done, 1)
                    alone(dve, x_done, b + 1, stood)
                    layer_stats(dve, stats, keep.moments, keep.x[:, bass.ds(b, 1), :], b, stats_step, stood)

            steps(step)(dve)

        @block.scalar
        def _(act):
            act.wait_ge(made, 1)

            def squares(at, n):
                b, slot, trip = at
                act.wait_ge(proj_ready, NP * b + n + 1)
                after(act, powered, NP * b + n - 1)
                act.activation(square[:, n % 2], ps_proj[n % 2][:, :].rearrange("p (h d) -> p h d", h=SHARE), ACT.Square).then_inc(squared, 1)

            def turned_out(at, n):
                b, slot, trip = at
                act.wait_ge(turned, NP * b + n + 1)
                after(act, score_ready, GROUPS * (b - 1))
                if n == 0:
                    act.activation(k_t[:, slot], ps_turn[:, :].rearrange("p (g m) -> p g m", g=GROUPS), ACT.Copy,
                                   scale=k_weight[:, :]).then_inc(turned_read, 1)
                else:
                    act.activation(q_t[:, slot, n - 1, :], ps_turn[:, :], ACT.Copy).then_inc(turned_read, 1)

            def exponents(at, g):
                b, slot, trip = at
                n = GROUPS * b + g
                act.wait_ge(bias_ready, n + 1)
                after(act, weights_ready, n - 1)
                for h in range(SHARE):
                    op = act.activation(probs[:, g % 2, h, :], ps_score[g % 2][:, h * P:(h + 1) * P], ACT.Exp,
                                        bias=bias[:, g % 2, h:h + 1], accum_out=sums[:, g % 2, h:h + 1])
                op.then_inc(probs_ready, 1)

            def step(i, at, looped=False):
                first, second = stages(i, looped)
                f = at(first) if first is not None else None
                s = at(second) if second is not None else None
                if s:
                    exponents(s, 0)
                if f:
                    b, slot, trip = f
                    act.wait_ge(x_turned, b + 1)
                    after(act, proj_ready, NP * b)
                    act.activation(x_t[:, :, :], ps_turn[:, 0:D].rearrange("p (k n) -> p k n", k=KD), ACT.Copy).then_inc(x_t_ready, 1)
                    squares(f, 0)
                    act.wait_ge(v_ready, b + 1)
                    after(act, out_ready, GROUPS * (b - 1))
                    act.activation(values[:, slot, :], ps_proj[1][:, :], ACT.Copy).then_inc(v_read, 1)
                for g in range(GROUPS):
                    if f:
                        squares(f, g + 1)
                    if s and g + 1 < GROUPS:
                        exponents(s, g + 1)
                    if f:
                        turned_out(f, g)
                    if s:
                        n = GROUPS * s[0] + g
                        act.wait_ge(out_ready, n + 1)
                        after(act, merged, n - 1)
                        act.activation(out_t[:, g % 2], ps_out[:, :].rearrange("p (h n) -> p h n", h=SHARE), ACT.Copy).then_inc(out_read, 1)
                if f:
                    turned_out(f, GROUPS)

            steps(step)(act)

        @block.gpsimd
        def _(pool):
            def inverse_rms(at, n):
                b, slot, trip = at
                m = NP * b + n
                alone(pool, powered, m + 1, stood)
                pool.tensor_scalar(inverse[:, n % 2, :], power[:, n % 2, :], 1.0 / HD1, RMS_EPS, ALU.mult, ALU.add).then_inc(inv_step, 1)
                pool.wait_ge(inv_step, 2 * m + 1)
                pool.tensor_tensor(inverse[:, n % 2, :], inverse[:, n % 2, :], keep.minus_half[:, 0:SHARE], ALU.pow).then_inc(inv_step, 1)

            def weigh(at, g):
                b, slot, trip = at
                n = GROUPS * b + g
                pool.wait_ge(inv_ready, n + 1)
                after(pool, w_turned, n - 1)
                pool.tensor_tensor(weights[:, g % 2], probs[:, g % 2], sums_inv[:, g % 2, :].unsqueeze(2).broadcast_to([P, SHARE, P]),
                                   ALU.mult).then_inc(weights_ready, 1)

            def step(i, at, looped=False):
                first, second = stages(i, looped)
                f = at(first) if first is not None else None
                s = at(second) if second is not None else None
                if f:
                    inverse_rms(f, 0)
                for g in range(GROUPS):
                    if s:
                        weigh(s, g)
                    if f:
                        inverse_rms(f, g + 1)

            steps(step)(pool)
            pool.wait_ge(stats_step, 3 * NB)
            inverse_deviation(pool, keep, 3)




def normalise(dve, keep, xn, b, done):
    row = bass.ds(b, 1)
    dve.tensor_scalar(xn.unsqueeze(1), keep.x[:, row, :], keep.moments[:, row, 0:1], keep.rstd[:, row], ALU.subtract, ALU.mult).then_inc(done, 1)


def layer1_route(nc, keep, w, weights_in):
    with ExitStack() as ctx:
        sem = lambda n: ctx.enter_context(nc.semaphore("r_" + n))
        sb = lambda n, shape, dt=F32: ctx.enter_context(nc.sbuf_tensor("r_" + n, shape, dt))
        bank = lambda n: ctx.enter_context(nc.psum_tensor("r_" + n, [P, 512], F32))
        w_r = sb("w_r", [P, KE, EXPERTS])
        earlier = sb("earlier", [P, P])
        numbers = sb("numbers", [P, P])
        xn = sb("xn", [P, 2, D])
        x_t = sb("x_t", [P, KE, P])
        top = sb("top", [P, 8])
        low = sb("low", [P, 1])
        exps = sb("exps", [P, EXPERTS])
        total = sb("total", [P, 1])
        total_inv = sb("total_inv", [P, 1])
        scores = sb("scores", [P, EXPERTS])
        best = sb("best", [P, 8])
        best_expert = sb("best_expert", [P, 8], U32)
        expert = sb("expert", [P, TOP_K])
        hits = sb("hits", [P, TOP_K, EXPERTS])
        chosen = sb("chosen", [P, EXPERTS])
        best_sum = sb("best_sum", [P, 1])
        best_inv = sb("best_inv", [P, 1])
        places = sb("places", [P, TOP_K, EXPERTS])
        place = sb("place", [P, TOP_K])
        row = sb("row", [P, TOP_K])
        over = sb("over", [P, TOP_K])
        send_row = sb("send_row", [P, 2, TOP_K], U32)
        before = sb("before", [P, EXPERTS])
        tiles = sb("tiles", [EXPERTS, P])
        passed = sb("passed", [EXPERTS, 2, P])
        at_row = sb("at_row", [EXPERTS, P])
        beyond = sb("beyond", [EXPERTS, P])
        ps_turn, ps_place, ps_jobs = bank("ps_turn"), bank("ps_place"), bank("ps_jobs")
        ps_logits = [bank("ps_logits0"), bank("ps_logits1")]

        w_in, made, xn_ready, x_turned, x_t_ready, logits_ready = (
            sem("w_in"), sem("made"), sem("xn_ready"), sem("x_turned"), sem("x_t_ready"), sem("logits_ready"))
        low_ready, exps_ready, chosen_ready, place_ready, rows_ready, step_done, table_step = (
            sem("low_ready"), sem("exps_ready"), sem("chosen_ready"), sem("place_ready"), sem("rows_ready"),
            sem("step_done"), sem("table_step"))
        placed, finish_step = sem("placed"), sem("finish_step")
        sent = [sem("sent0"), sem("sent1")]
        kept = [sem("kept0"), sem("kept1")]
        table_in = sem("table_in")
        stood = keep.stood
        block = ctx.enter_context(nc.Block())

        def steps(step):
            def run(eng):
                for i in (-1, 0):
                    step(i, lambda b: (b, b % 2, b // 2))
                with eng.Fori(0, 6) as t:
                    for c in (1, 2):
                        step(c, lambda b: (t * 2 + b, b % 2, t + b // 2), looped=True)
                for i in (13, 14, 15):
                    step(i, lambda b: (b, b % 2, b // 2))
            return run

        def stages(i, at, looped):
            return tuple(at(b) if looped or 0 <= b < NB else None for b in (i + 1, i))

        @block.sync
        def _(sp):
            sp.dma_start(w_r[:, :, :], w.router.rearrange("(k p) n -> p k n", p=P)).then_inc(w_in, 16)
            sp.dma_start(earlier[:, :], w.earlier).then_inc(w_in, 16)
            sp.dma_start(numbers[:, :], w.numbers).then_inc(w_in, 16)
            sp.dma_start(keep.jobs[0:1, 0:2, ROUTED_JOBS:], w.shared_jobs.unsqueeze(0)).then_inc(table_in, 16)

            def step(i, at, looped=False):
                first, _ = stages(i, at, looped)
                if first:
                    b, slot, trip = first
                    alone(sp, xn_ready, b + 1, stood)
                    sp.dma_start(keep.rows[bass.ds(b * P + TOKEN_ROW, P), :], xn[:, slot, :]).then_inc(kept[slot], 16)
                if i == -1:
                    for q in range(4):
                        e = slice(q * (EXPERTS + SHARED) // 4, (q + 1) * (EXPERTS + SHARED) // 4)
                        sp.dma_start(keep.w_gu[:, e], w.gu[e].rearrange("e (k p) n -> p e k n", p=P)).then_inc(weights_in, 16)
                        sp.dma_start(keep.w_down[:, e], w.down_e[e].rearrange("e (k p) n -> p e k n", p=FH)).then_inc(weights_in, 16)

            steps(step)(sp)
            sp.wait_ge(table_in, 16)
            for slot in range(2):
                sp.wait_ge(kept[slot], 16 * NB // 2)

        @block.tensor
        def _(pe):
            pe.wait_ge(w_in, 3 * 16)
            pe.wait_ge(made, 1)

            def step(i, at, looped=False):
                first, second = stages(i, at, looped)
                if first:
                    b, slot, trip = first
                    alone(pe, xn_ready, b + 1, stood)
                    for c in range(KE):
                        mm = pe.transpose(ps_turn[:, c * P:(c + 1) * P], xn[:, slot, c * P:(c + 1) * P], keep.identity[:, :])
                    mm.then_inc(x_turned, 1)
                    alone(pe, x_t_ready, b + 1, stood)
                    for c in range(KE):
                        mm = pe.matmul(ps_logits[slot][:, 0:EXPERTS], x_t[:, c, :], w_r[:, c, :], start=(c == 0), stop=(c == KE - 1))
                    mm.then_inc(logits_ready, 1)
                if second:
                    b, slot, trip = second
                    alone(pe, chosen_ready, b + 1, stood)
                    pe.matmul(ps_place[:, 0:EXPERTS], earlier[:, :], chosen[:, :], start=True, stop=False)
                    pe.matmul(ps_place[:, 0:EXPERTS], keep.ones[:, :], before[:, :], start=False, stop=True).then_inc(place_ready, 1)

            steps(step)(pe)
            pe.wait_ge(rows_ready, NB)
            pe.matmul(ps_jobs[0:EXPERTS, 0:P], before[:, :], keep.ones[:, :], start=True, stop=True).then_inc(table_step, 1)
            pe.wait_ge(table_step, 7)
            pe.matmul(ps_jobs[0:EXPERTS, P:2 * P], earlier[0:EXPERTS, 0:EXPERTS], tiles[:, :], start=True, stop=True).then_inc(table_step, 1)
            pe.wait_ge(table_step, 10)
            pe.matmul(ps_jobs[0:EXPERTS, 2 * P:4 * P], keep.ones[0:EXPERTS, 0:EXPERTS], passed[:, :, :].rearrange("p a n -> p (a n)"),
                      start=True, stop=True).then_inc(table_step, 1)

        @block.scalar
        def _(act):
            def step(i, at, looped=False):
                first, second = stages(i, at, looped)
                if first:
                    b, slot, trip = first
                    alone(act, x_turned, b + 1, stood)
                    act.activation(x_t[:, :, :], ps_turn[:, 0:D].rearrange("p (k n) -> p k n", k=KE), ACT.Copy).then_inc(x_t_ready, 1)
                if second:
                    b, slot, trip = second
                    alone(act, low_ready, b + 1, stood)
                    act.activation(exps[:, :], ps_logits[slot][:, 0:EXPERTS], ACT.Exp, bias=low[:, :],
                                   accum_out=total[:, :]).then_inc(exps_ready, 1)

            steps(step)(act)

        @block.vector
        def _(dve):
            LINKS = 14
            dve.memset(before[:, :], 0.0).then_inc(made, 1)
            dve.wait_ge(w_in, 3 * 16)

            def place_batch(b, slot, trip):
                def done(n):
                    alone(dve, step_done, b * LINKS + n, stood)

                alone(dve, logits_ready, b + 1, stood)
                dve.max(top[:, :], ps_logits[slot][:, 0:EXPERTS]).then_inc(step_done, 1)
                done(1)
                dve.tensor_scalar(low[:, :], top[:, 0:1], -1.0, None, ALU.mult).then_inc(low_ready, 1)
                alone(dve, exps_ready, b + 1, stood)
                dve.reciprocal(total_inv[:, :], total[:, :]).then_inc(step_done, 1)
                done(2)
                dve.tensor_scalar(scores[:, :], exps[:, :], total_inv[:, :], None, ALU.mult).then_inc(step_done, 1)
                done(3)
                dve.max(best[:, :], scores[:, :]).then_inc(step_done, 1)
                done(4)
                dve.max_index(best_expert[:, :], best[:, :], scores[:, :]).then_inc(step_done, 1)
                dve.tensor_reduce(best_sum[:, :], best[:, 0:TOP_K], AX, ALU.add).then_inc(step_done, 1)
                done(5)
                dve.tensor_copy(expert[:, :], best_expert[:, 0:TOP_K]).then_inc(step_done, 1)
                done(7)
                dve.tensor_tensor(hits[:, :, :], numbers[:, 0:EXPERTS].unsqueeze(1).broadcast_to([P, TOP_K, EXPERTS]),
                                  expert[:, :].unsqueeze(2).broadcast_to([P, TOP_K, EXPERTS]), ALU.is_equal).then_inc(step_done, 1)
                done(8)
                dve.tensor_reduce(chosen[:, :], hits[:, :, :].rearrange("p k e -> p e k"), AX, ALU.add).then_inc(chosen_ready, 1)
                dve.tensor_scalar(best_sum[:, :], best_sum[:, :], 1e-20, None, ALU.add).then_inc(step_done, 1)
                done(9)
                dve.reciprocal(best_inv[:, :], best_sum[:, :]).then_inc(step_done, 1)
                done(10)
                dve.tensor_scalar(keep.weight[:, bass.ds(b, 1), :], best[:, 0:TOP_K].unsqueeze(1), best_inv[:, :], None,
                                  ALU.mult).then_inc(step_done, 1)
                dve.tensor_copy(keep.first_row[:, bass.ds(b, 1), :], expert[:, :].unsqueeze(1)).then_inc(step_done, 1)
                alone(dve, place_ready, b + 1, stood)
                dve.tensor_tensor(places[:, :, :], hits[:, :, :], ps_place[:, 0:EXPERTS].unsqueeze(1).broadcast_to([P, TOP_K, EXPERTS]),
                                  ALU.mult).then_inc(step_done, 1)
                dve.tensor_tensor(before[:, :], before[:, :], chosen[:, :], ALU.add).then_inc(rows_ready, 1)
                done(13)
                dve.tensor_reduce(place[:, :], places[:, :, :], AX, ALU.add).then_inc(step_done, 1)
                done(14)
                dve.tensor_copy(keep.place[:, bass.ds(b, 1), :], place[:, :].unsqueeze(1)).then_inc(placed, 1)
                dve.tensor_scalar(over[:, :], place[:, :], float(CAPACITY), SKIP, ALU.is_gt, ALU.mult).then_inc(placed, 1)
                dve.scalar_tensor_tensor(row[:, :], expert[:, :], float(CAPACITY), place[:, :], ALU.mult, ALU.add).then_inc(placed, 1)
                alone(dve, placed, 4 * b + 3, stood)
                dve.scalar_tensor_tensor(send_row[:, slot, :], over[:, :], -1.0, row[:, :], ALU.add, ALU.add).then_inc(placed, 1)

            def step(i, at, looped=False):
                first, second = stages(i, at, looped)
                if first:
                    b, slot, trip = first
                    alone(dve, sent[slot], 16 * TOP_K * trip, stood)
                    alone(dve, kept[slot], 16 * trip, stood)
                    normalise(dve, keep, xn[:, slot, :], b, xn_ready)
                if second:
                    place_batch(*second)

            steps(step)(dve)
            dve.wait_ge(placed, 4 * NB)

            every = lambda x: x[:, :, :].rearrange("p b k -> p (b k)")
            dve.scalar_tensor_tensor(every(keep.weight), every(keep.place), float(CAPACITY), every(keep.weight),
                                     ALU.is_le, ALU.mult).then_inc(finish_step, 1)
            dve.tensor_scalar(every(keep.valid), every(keep.place), float(CAPACITY), None, ALU.is_le).then_inc(finish_step, 1)
            dve.tensor_scalar(every(keep.place), every(keep.place), -1.0, None, ALU.add).then_inc(finish_step, 1)
            dve.wait_ge(finish_step, 3)
            dve.tensor_tensor(every(keep.place), every(keep.place), every(keep.valid), ALU.mult).then_inc(finish_step, 1)
            dve.wait_ge(finish_step, 4)
            dve.scalar_tensor_tensor(every(keep.result_row), every(keep.first_row), float(CAPACITY), every(keep.place),
                                     ALU.mult, ALU.add).then_inc(finish_step, 1)

            dve.wait_ge(table_step, 1)
            dve.tensor_scalar(tiles[:, :], ps_jobs[0:EXPERTS, 0:P], 0.0, None, ALU.is_gt).then_inc(table_step, 1)
            for n in range(1, CAPACITY // P):
                dve.wait_ge(table_step, n + 1)
                dve.scalar_tensor_tensor(tiles[:, :], ps_jobs[0:EXPERTS, 0:P], float(n * P), tiles[:, :], ALU.is_gt, ALU.add).then_inc(table_step, 1)
            dve.wait_ge(table_step, 8)
            dve.tensor_tensor(passed[:, 0, :], ps_jobs[0:EXPERTS, P:2 * P], numbers[0:EXPERTS, :], ALU.is_le).then_inc(table_step, 1)
            dve.wait_ge(table_step, 9)
            dve.tensor_tensor(passed[:, 1, :], passed[:, 0, :], tiles[:, :], ALU.mult).then_inc(table_step, 1)
            dve.wait_ge(table_step, 11)
            dve.tensor_scalar(keep.jobs[0:1, 0, 0:ROUTED_JOBS], ps_jobs[0:1, 2 * P:3 * P], float(EXPERTS - 1), None, ALU.min).then_inc(table_step, 1)
            dve.scalar_tensor_tensor(at_row[0:1, :], ps_jobs[0:1, 3 * P:4 * P], -1.0, numbers[0:1, :], ALU.mult, ALU.add).then_inc(table_step, 1)
            dve.wait_ge(table_step, 13)
            dve.tensor_scalar(at_row[0:1, :], at_row[0:1, :], float(P), None, ALU.mult).then_inc(table_step, 1)
            dve.wait_ge(table_step, 14)
            dve.scalar_tensor_tensor(at_row[0:1, :], ps_jobs[0:1, 2 * P:3 * P], float(CAPACITY), at_row[0:1, :], ALU.mult, ALU.add).then_inc(table_step, 1)
            dve.wait_ge(table_step, 15)
            dve.tensor_scalar(keep.jobs[0:1, 1, 0:ROUTED_JOBS], at_row[0:1, :], float(TOKEN_ROW), None, ALU.min).then_inc(table_step, 1)
            dve.tensor_scalar(beyond[0:1, :], at_row[0:1, :], float(TOKEN_ROW), float(NB * P), ALU.is_ge, ALU.mult).then_inc(table_step, 1)
            dve.wait_ge(table_step, 17)
            dve.tensor_tensor(keep.jobs[0:1, 2, 0:ROUTED_JOBS], at_row[0:1, :], beyond[0:1, :], ALU.add).then_inc(table_step, 1)

        @block.gpsimd
        def _(pool):
            def step(i, at, looped=False):
                first, second = stages(i, at, looped)
                if second:
                    b, slot, trip = second
                    alone(pool, placed, 4 * (b + 1), stood)
                    for k in range(TOP_K):
                        pool.indirect_dma_start(keep.rows[0:TOKEN_ROW, :], bass.IndirectOffsetOnAxis(ap=send_row[:, slot, k:k + 1], axis=0),
                                                xn[:, slot, :], None, bounds_check=TOKEN_ROW - 1, oob_is_err=False).then_inc(sent[slot], 16)

            steps(step)(pool)
            for slot in range(2):
                pool.wait_ge(sent[slot], 16 * TOP_K * NB // 2)


def layer1_experts(nc, keep, w, weights_in):
    with ExitStack() as ctx:
        sem = lambda n: ctx.enter_context(nc.semaphore("h_" + n))
        sb = lambda n, shape, dt=F32: ctx.enter_context(nc.sbuf_tensor("h_" + n, shape, dt))
        bank = lambda n: ctx.enter_context(nc.psum_tensor("h_" + n, [P, 512], F32))
        rows = sb("rows", [P, 4, D])
        x_t = sb("x_t", [P, 2, KE, P])
        act_gate = sb("act_gate", [P, 2, FE])
        h = sb("h", [P, 2, FE])
        h_t = sb("h_t", [FH, 2, 2, P])
        results = sb("results", [P, 2, D])
        gather_row = sb("gather_row", [P, 2, TOP_K], U32)
        gathered = sb("gathered", [P, 2, TOP_K, D])
        weight = sb("weight", [P, TOP_K])
        ps_turn = [bank("ps_turn0"), bank("ps_turn1")]
        ps_gu = [bank("ps_gu0"), bank("ps_gu1")]
        ps_h = [bank("ps_h0"), bank("ps_h1")]
        ps_y = [bank("ps_y0"), bank("ps_y1")]
        sems = lambda n, k: [sem(f"{n}{i}") for i in range(k)]
        rows_in, stored, gathered_in = sems("rows_in", 4), sems("stored", 2), sems("gathered_in", 2)
        x_turned, x_t_ready, gu_ready, silu_ready, h_ready, h_turned, h_t_ready, down_done, result_ready = (
            sem("x_turned"), sem("x_t_ready"), sem("gu_ready"), sem("silu_ready"), sem("h_ready"), sem("h_turned"),
            sem("h_t_ready"), sem("down_done"), sem("result_ready"))
        row_ready, summed, x_done = sem("row_ready"), sem("summed"), sem("x_done")
        stood = keep.stood
        block = ctx.enter_context(nc.Block())

        def run(step):
            def program(eng):
                for s in range(4):
                    step(s, s, 0)
                with eng.Fori(0, (ROUTED_JOBS - 4) // 4) as t:
                    for c in range(4, 8):
                        step(t * 4 + c, c, t + 1)
                for s in range(ROUTED_JOBS, ROUTED_JOBS + 4):
                    step(s, s, s // 4)
                with eng.Fori(0, (JOBS - ROUTED_JOBS - 4) // 4) as t:
                    for c in range(ROUTED_JOBS + 4, ROUTED_JOBS + 8):
                        step(t * 4 + c, c, t + (ROUTED_JOBS + 4) // 4)
                for s in range(JOBS, JOBS + 3):
                    step(s, s, s // 4)
            return program

        def batch_of(c, quad):
            if c < ROUTED_JOBS + 4 or c % 2:
                return None
            trip, slot = quad - (ROUTED_JOBS + 4) // 4, c % 4 // 2
            return trip * 2 + slot, slot, trip

        @block.sync
        def _(sp):
            def load(s, c):
                row = sp.value_load(keep.jobs[0:1, 1, bass.ds(s, 1)], min_val=0, max_val=IDLE_ROW - P)
                if c >= 4:
                    alone(sp, x_turned, s - 3, stood)
                sp.dma_start(rows[:, c % 4, :], keep.rows[bass.ds(row, P), :]).then_inc(rows_in[c % 4], 16)

            def store(s, c):
                n = s - 4
                row = sp.value_load(keep.jobs[0:1, 2, bass.ds(n, 1)], min_val=0, max_val=ALL_ROWS - P)
                alone(sp, result_ready, n + 1, stood)
                sp.dma_start(keep.rows[bass.ds(row, P), :], results[:, c % 2, :]).then_inc(stored[c % 2], 16)

            def step(s, c, quad):
                if c < JOBS:
                    load(s, c)
                if 4 <= c < ROUTED_JOBS + 4:
                    store(s, c)
            run(step)(sp)

        @block.tensor
        def _(pe):
            pe.wait_ge(weights_in, 8 * 16)

            def expert_of(n):
                return pe.value_load(keep.jobs[0:1, 0, bass.ds(n, 1)], min_val=0, max_val=EXPERTS + SHARED - 1)

            def step(s, c, quad):
                if 1 <= c <= JOBS:
                    slot = (c - 1) % 2
                    e = expert_of(s - 1)
                    alone(pe, x_t_ready, s, stood)
                    if c > 2:
                        alone(pe, h_ready, s - 2, stood)
                    for k in range(KE):
                        mm = pe.matmul(ps_gu[slot][:, 0:2 * FE].unsqueeze(1), x_t[:, slot, k, :], keep.w_gu[:, bass.ds(e, 1), k, :],
                                       start=(k == 0), stop=(k == KE - 1))
                    mm.then_inc(gu_ready, 1)
                if 2 <= c <= JOBS + 1:
                    slot = c % 2
                    alone(pe, h_ready, s - 1, stood)
                    if c > 3:
                        alone(pe, h_t_ready, s - 3, stood)
                    for k in range(2):
                        mm = pe.transpose(ps_h[slot][0:FH, k * P:(k + 1) * P], h[:, slot, k * FH:(k + 1) * FH], keep.identity[:, :])
                    mm.then_inc(h_turned, 1)
                if c < JOBS:
                    alone(pe, rows_in[c % 4], 16 * (quad + 1), stood)
                    if c > 1:
                        alone(pe, x_t_ready, s - 1, stood)
                    for k in range(KE):
                        mm = pe.transpose(ps_turn[c % 2][:, k * P:(k + 1) * P], rows[:, c % 4, k * P:(k + 1) * P], keep.identity[:, :])
                    mm.then_inc(x_turned, 1)
                if c >= 3:
                    slot = (c - 3) % 2
                    e = expert_of(s - 3)
                    alone(pe, h_t_ready, s - 2, stood)
                    if c < ROUTED_JOBS + 3:
                        bank, start, stop = ps_y[slot], True, True
                        if c > 4:
                            alone(pe, result_ready, s - 4, stood)
                    else:
                        bank, start, stop = ps_y[0], slot == 0, slot == 1
                        if c == ROUTED_JOBS + 3:
                            pe.wait_ge(result_ready, ROUTED_JOBS)
                        elif slot == 0:
                            at = batch_of(c - 1, quad if c % 4 else quad - 1)
                            alone(pe, x_done, at[0] + 1, stood)
                    for k in range(2):
                        mm = pe.matmul(bank[:, 0:D].unsqueeze(1), h_t[:, slot, k, :], keep.w_down[:, bass.ds(e, 1), k, :],
                                       start=(start and k == 0), stop=(stop and k == 1))
                    mm.then_inc(down_done, 1)

            run(step)(pe)

        @block.scalar
        def _(act):
            def step(s, c, quad):
                if 1 <= c <= JOBS:
                    slot = (c - 1) % 2
                    alone(act, gu_ready, s, stood)
                    if c > 2:
                        alone(act, h_ready, s - 2, stood)
                    act.activation(act_gate[:, slot, :], ps_gu[slot][:, 0:FE], ACT.Silu).then_inc(silu_ready, 1)
                if 2 <= c <= JOBS + 1:
                    slot = c % 2
                    alone(act, h_turned, s - 1, stood)
                    if c > 3:
                        alone(act, down_done, s - 3, stood)
                    act.activation(h_t[:, slot], ps_h[slot][0:FH, 0:2 * P].rearrange("p (k n) -> p k n", k=2), ACT.Copy).then_inc(h_t_ready, 1)
                if c < JOBS:
                    alone(act, x_turned, s + 1, stood)
                    if c > 1:
                        alone(act, gu_ready, s - 1, stood)
                    act.activation(x_t[:, c % 2], ps_turn[c % 2][:, 0:D].rearrange("p (k n) -> p k n", k=KE), ACT.Copy).then_inc(x_t_ready, 1)

            run(step)(act)

        @block.vector
        def _(dve):
            def rows_for(b, slot):
                dve.tensor_copy(gather_row[:, slot, :].unsqueeze(1), keep.result_row[:, bass.ds(b, 1), :]).then_inc(row_ready, 1)

            def combine(at):
                b, slot, trip = at
                alone(dve, down_done, b * SHARED + ROUTED_JOBS + SHARED, stood)
                alone(dve, gathered_in[slot], 16 * TOP_K * (trip + 1), stood)
                if not isinstance(b, int) or b + 2 < NB:
                    rows_for(b + 2, slot)
                dve.tensor_copy(weight[:, :].unsqueeze(1), keep.weight[:, bass.ds(b, 1), :]).then_inc(summed, 1)
                alone(dve, summed, b * (TOP_K + 1) + 1, stood)
                total = gathered[:, slot, 0, :]
                for k in range(TOP_K):
                    dve.scalar_tensor_tensor(total, gathered[:, slot, k, :], weight[:, k:k + 1],
                                             total if k else ps_y[0][:, 0:D], ALU.mult, ALU.add).then_inc(summed, 1)
                    alone(dve, summed, b * (TOP_K + 1) + k + 2, stood)
                row = keep.x[:, bass.ds(b, 1), :]
                dve.scalar_tensor_tensor(row, total.unsqueeze(1), keep.gate[:, 3:4], row, ALU.mult, ALU.add).then_inc(x_done, 1)
                alone(dve, x_done, b + 1, stood)

            def step(s, c, quad):
                if 1 <= c <= JOBS:
                    slot = (c - 1) % 2
                    alone(dve, silu_ready, s, stood)
                    if c > 2:
                        alone(dve, h_turned, s - 2, stood)
                    dve.tensor_tensor(h[:, slot, :], ps_gu[slot][:, FE:2 * FE], act_gate[:, slot, :], ALU.mult).then_inc(h_ready, 1)
                if 3 <= c < ROUTED_JOBS + 3:
                    slot = (c - 3) % 2
                    n = s - 3
                    alone(dve, down_done, n + 1, stood)
                    if c >= 5:
                        alone(dve, stored[slot], 16 * (quad * 2 + (c % 4 - 3) // 2), stood)
                    dve.tensor_copy(results[:, slot, :], ps_y[slot][:, 0:D]).then_inc(result_ready, 1)
                at = batch_of(c, quad)
                if at:
                    combine(at)

            for b in range(2):
                rows_for(b, b)
            run(step)(dve)

        @block.gpsimd
        def _(pool):
            for slot in range(2):
                pool.wait_ge(stored[slot], 16 * ROUTED_JOBS // 2)

            def gather(at):
                b, slot, trip = at
                alone(pool, row_ready, b + 1, stood)
                alone(pool, x_done, b - 1, stood)
                for k in range(TOP_K):
                    pool.indirect_dma_start(gathered[:, slot, k, :], None, keep.rows[0:TOKEN_ROW, :],
                                            bass.IndirectOffsetOnAxis(ap=gather_row[:, slot, k:k + 1], axis=0),
                                            bounds_check=TOKEN_ROW - 1, oob_is_err=False).then_inc(gathered_in[slot], 16)

            for b in range(2):
                gather((b, b, 0))
            with pool.Fori(0, NB // 2 - 1) as t:
                for b in (2, 3):
                    gather((t * 2 + b, b % 2, t + 1))


def write_out(nc, keep, out):
    with ExitStack() as ctx:
        out_done = ctx.enter_context(nc.semaphore("out_done"))
        block = ctx.enter_context(nc.Block())

        @block.sync
        def _(sp):
            sp.dma_start(out.rearrange("b p n -> p b n"), keep.x[:, :, :]).then_inc(out_done, 16)
            sp.wait_ge(out_done, 16)


class Named:
    pass


def build(nc, t, out):
    with ExitStack() as ctx:
        keep = Named()
        sb = lambda n, shape, dt=F32: ctx.enter_context(nc.sbuf_tensor(n, shape, dt))
        keep.x = sb("x_tokens", [P, NB, D])
        keep.identity = sb("identity", [P, P])
        keep.identity_bf = sb("identity_bf", [P, P], BF16)
        keep.gate = sb("gate", [P, 4])
        keep.ln_eps = sb("ln_eps", [P, 1])
        keep.ones = sb("ones", [P, P])
        keep.minus_half = sb("minus_half", [P, NB])
        keep.moments = sb("moments", [P, NB, 2])
        keep.rstd = sb("rstd", [P, NB])
        keep.stood = ctx.enter_context(nc.semaphore("stood"))
        keep.rstd_done = ctx.enter_context(nc.semaphore("rstd_done"))
        keep.rows = nc.dram_tensor("expert_rows", [ALL_ROWS, D], F32).ap()
        setup(nc, keep, t["x"], t["consts"], t["gates"])
        w = Named()
        w.qk, w.v, w.m, w.bqk, w.bv, w.bm, w.enc, w.sign = (
            t[n] for n in ("a_qk", "a_v", "a_m", "a_bqk", "a_bv", "a_bm", "a_enc", "a_sign"))
        layer0_attention(nc, keep, t["ctx"], w, None)
        w.gate, w.up, w.down = t["b_gate"], t["b_up"], t["b_down"]
        layer0_ffn(nc, keep, w)
        w.q, w.k, w.v, w.o, w.norms, w.ctx_t = (t[n] for n in ("c_q", "c_k", "c_v", "c_o", "c_norms", "ctx_t"))
        layer1_attention(nc, keep, w)
        w.router, w.earlier, w.numbers, w.shared_jobs, w.gu, w.down_e = (
            t[n] for n in ("d_router", "d_earlier", "d_numbers", "d_jobs", "d_gu", "d_down"))
        with ExitStack() as moe:
            sb = lambda n, shape, dt=F32: moe.enter_context(nc.sbuf_tensor(n, shape, dt))
            keep.w_gu = sb("w_gu", [P, EXPERTS + SHARED, KE, 2 * FE])
            keep.w_down = sb("w_down", [FH, EXPERTS + SHARED, 2, D])
            keep.jobs = sb("jobs", [1, 3, JOBS], U32)
            keep.weight = sb("choice_weight", [P, NB, TOP_K])
            keep.place = sb("choice_place", [P, NB, TOP_K])
            keep.valid = sb("choice_valid", [P, NB, TOP_K])
            keep.first_row = sb("choice_expert", [P, NB, TOP_K])
            keep.result_row = sb("result_row", [P, NB, TOP_K], U32)
            weights_in = moe.enter_context(nc.semaphore("weights_in"))
            layer1_route(nc, keep, w, weights_in)
            layer1_experts(nc, keep, w, weights_in)
        write_out(nc, keep, out)


def lay_out(i):
    a = {k: np.asarray(v) for k, v in i.items()}
    channel = np.arange(P).reshape(HD0, HEADS0)
    order = channel.T.reshape(-1)
    split = channel.reshape(HD0, PAIRS, 2).transpose(2, 0, 1)
    straight, turned = split.reshape(-1), split[:, np.arange(HD0) ^ 1].reshape(-1)
    wq, wqr, bq, bqr = (a[f"L0_xattn_{n}"][o] for n in ("Wq", "bq") for o in (straight, turned))
    wk, wkr, bk, bkr = (a[f"L0_xattn_{n}"][o] for n in ("Wk", "bk") for o in (straight, turned))
    wv, bv = a["L0_xattn_Wv"][order], a["L0_xattn_bv"][order]
    enc = a["L0_xattn_encoding"][:, 0, 0]
    t = {
        "x": a["x"], "ctx": a["ctx_2048"],
        "gates": np.stack([a["g_xattn"], a["g_ffn"]]).reshape(4),
        "consts": np.eye(P, dtype=np.float32),
        "a_qk": np.stack([wq.T, wqr.T, wk.T, wkr.T], axis=1),
        "a_v": wv.T, "a_m": a["L0_xattn_Wm"][:, order].T,
        "a_bqk": np.stack([bq, bqr, bk, bkr], axis=1),
        "a_bv": bv, "a_bm": a["L0_xattn_bm"][:, None],
        "a_enc": np.tile(np.repeat(enc.transpose(2, 0, 1), PAIRS, axis=0), (2, 1, 1)),
        "a_sign": np.tile(np.repeat(np.array([-1.0, 1.0] * (HD0 // 2), np.float32), PAIRS), 2)[:, None],
    }
    t |= {"b_" + n: a["L0_ffn_w_" + n].T for n in ("gate", "up", "down")}
    t |= {"c_" + n: a["L1_xattn_W" + n] for n in "qkvo"}
    t["c_norms"] = np.stack([a["L1_xattn_q_norm_w"], a["L1_xattn_k_norm_w"]], axis=1)
    shared = np.stack([a["L1_ffn_ws_gate"], a["L1_ffn_ws_up"]], axis=1).reshape(D, 2, 2, FE).transpose(2, 0, 1, 3)
    routed = np.stack([a["L1_ffn_w_gate"], a["L1_ffn_w_up"]], axis=2)
    t["d_gu"] = np.concatenate([routed, shared]).reshape(EXPERTS + SHARED, D, 2 * FE)
    t["d_down"] = np.concatenate([a["L1_ffn_w_down"], a["L1_ffn_ws_down"].reshape(2, FE, D)])
    t["d_router"] = a["L1_ffn_wg_router"].T
    t["d_earlier"] = np.triu(np.ones((P, P), np.float32))
    t["d_numbers"] = np.tile(np.arange(P, dtype=np.float32), (P, 1))
    job = np.arange(SHARED * NB, dtype=np.uint32)
    t["d_jobs"] = np.stack([EXPERTS + job % SHARED, TOKEN_ROW + job // SHARED * P]).astype(np.uint32)
    t["ctx_t"] = a["ctx_2048"].transpose(0, 2, 1)
    return {k: np.ascontiguousarray(v) for k, v in t.items()}


def kernel(**inputs):
    import concourse.bacc as bacc
    from concourse.bass_utils import run_bass_kernel_spmd

    nc = bacc.Bacc("TRN2", target_bir_lowering=False, num_devices=1)
    arrays = lay_out(inputs)
    tensors = {n: nc.dram_tensor(f"in_{n}", a.shape, mybir.dt.from_np(a.dtype), kind="ExternalInput").ap()
               for n, a in arrays.items()}
    out = nc.dram_tensor("out", (NB, P, D), F32, kind="ExternalOutput").ap()
    build(nc, tensors, out)
    result = run_bass_kernel_spmd(nc, [{f"in_{n}": a for n, a in arrays.items()}], core_ids=[0])
    return result.results[0]["out"]
```

```python
from contextlib import ExitStack

import numpy as np

import concourse.bass as bass
from concourse import mybir

F32 = mybir.dt.float32
BF16 = mybir.dt.bfloat16
U32 = mybir.dt.uint32
ALU = mybir.AluOpType
ACT = mybir.ActivationFunctionType
AX = mybir.AxisListType.X

P = 128
NB = 16
D = 256
LN_EPS = 1e-5
MAGIC = 12582912.0

EXPERTS, FE, TOP_K = 32, 176, 6
CAPACITY = 2 * (NB * P * TOP_K // EXPERTS)
SHARED = 2
FH = FE // 2
KE = D // P
ROUTED_JOBS = NB * TOP_K + EXPERTS
JOBS = ROUTED_JOBS + SHARED * NB
TOKEN_ROW = EXPERTS * CAPACITY
IDLE_ROW = TOKEN_ROW + NB * P
ALL_ROWS = IDLE_ROW + ROUTED_JOBS * P
SKIP = float(1 << 20)
PACK_BITS = 6
PACK = 1 << PACK_BITS
QUADS = (JOBS + 3 + 3) // 4
ZERO_ROWS = 4

def after(eng, sem, count):
    if isinstance(count, int) and count <= 0:
        return
    eng.wait_ge(sem, count)


def alone(eng, sem, count, stood):
    if isinstance(count, int) and count <= 0:
        return
    eng.wait_ge(sem, count)
    eng.sem_inc(stood, 1)


def layer_stats(dve, stats, moments, x_tile, b, stats_step, stood):
    alone(dve, stats_step, 3 * b, stood)
    dve.bn_stats(stats[:, 0:6], x_tile).then_inc(stats_step, 1)
    alone(dve, stats_step, 3 * b + 1, stood)
    dve.bn_aggr(stats[:, 6:8], stats[:, 0:6]).then_inc(stats_step, 1)
    alone(dve, stats_step, 3 * b + 2, stood)
    dve.tensor_copy(moments[:, bass.ds(b, 1), :], stats[:, 6:8].unsqueeze(1)).then_inc(stats_step, 1)


def setup(nc, keep, x, consts, gates):
    with ExitStack() as ctx:
        sem = lambda n: ctx.enter_context(nc.semaphore(n))
        raw = ctx.enter_context(nc.sbuf_tensor("gates_raw", [P, 4], F32))
        stats = ctx.enter_context(nc.sbuf_tensor("stats0", [P, NB, 6], F32))
        x_in, const_in = sem("x_in"), sem("const_in")
        stats_step = sem("stats_step0")
        stood = keep.stood
        block = ctx.enter_context(nc.Block())

        @block.sync
        def _(sp):
            sp.dma_start(raw[:, :], gates.partition_broadcast(P)).then_inc(const_in, 16)
            sp.dma_start(keep.identity[:, :], consts[:, 0:P]).then_inc(const_in, 16)
            sp.dma_start(keep.x[:, :, :], x.rearrange("b p n -> p b n")).then_inc(x_in, 16)

        @block.scalar
        def _(act):
            act.wait_ge(const_in, 32)
            act.activation(keep.gate[:, :], raw[:, :], ACT.Tanh)
            act.activation(keep.identity_bf[:, :], keep.identity[:, :], ACT.Copy)

        @block.vector
        def _(dve):
            dve.memset(keep.ones[:, :], 1.0)
            dve.memset(keep.minus_half[:, :], -0.5)
            dve.wait_ge(x_in, 16)
            for b in range(NB):
                dve.bn_stats(stats[:, b, :], keep.x[:, b, :]).then_inc(stats_step, 1)
            for b in range(NB):
                dve.wait_ge(stats_step, b + 1)
                dve.bn_aggr(keep.moments[:, b, :], stats[:, b, :]).then_inc(stats_step, 1)

        @block.gpsimd
        def _(pool):
            pool.wait_ge(stats_step, 2 * NB)
            inverse_deviation(pool, keep, 0)


def inverse_deviation(pool, keep, norm):
    done = keep.rstd_done
    pool.tensor_scalar(keep.rstd[:, :], keep.moments[:, :, 1], LN_EPS, None, ALU.add).then_inc(done, 1)
    pool.wait_ge(done, 2 * norm + 1)
    pool.tensor_tensor(keep.rstd[:, :], keep.rstd[:, :], keep.minus_half[:, :], ALU.pow).then_inc(done, 1)


HEADS0, HD0, N0 = 16, 8, 256
PAIRS = HEADS0 // 2
COUPLES = PAIRS // 2
PRODUCTS = 6
STACK = PRODUCTS * HD0
SLOTS = 3
UNITS = 2 * PAIRS
LAG = 2


def layer0_attention(nc, keep, ctx_in_dram, w):
    with ExitStack() as ctx:
        sem = lambda n: ctx.enter_context(nc.semaphore(n))
        sems = lambda n, k: [sem(f"{n}{i}") for i in range(k)]
        sb = lambda n, shape, dt=F32: ctx.enter_context(nc.sbuf_tensor(n, shape, dt))
        bank = lambda n: ctx.enter_context(nc.psum_tensor(n, [P, 512], F32))

        w_qk = sb("w_qk", [P, 4, P])
        w_v = sb("w_v", [P, P])
        w_m = sb("w_m", [P, P])
        b_qk = sb("b_qk", [P, 4])
        b_v = sb("b_v", [P, P])
        b_m = sb("b_m", [P, 1])
        gate_bm = sb("gate_bm", [P, 1])
        sign = sb("sign", [P, 1])
        rope = sb("rope", [P, 2, N0])
        source = sb("source", [P, 3, N0])
        xn = sb("xn", [P, N0])
        turned = sb("turned", [P, 2, 2, N0])
        qk = sb("qk", [P, 2, N0])
        rest = sb("rest", [P, 2, N0])
        parts = sb("parts", [P, 2, 3, N0], BF16)
        q_stack = sb("q_stack", [P, SLOTS, PAIRS, N0], BF16)
        k_stack = sb("k_stack", [P, SLOTS, PAIRS, N0], BF16)
        values = sb("values", [P, SLOTS, 2, HEADS0, 32])
        top = sb("top", [P, 2, 2, PAIRS])
        top_rest = sb("top_rest", [P, 2, 2 * PAIRS])
        top_parts = sb("top_parts", [P, 2, 3, 2 * PAIRS], BF16)
        top_rows = sb("top_rows", [3 * HEADS0, N0], BF16)
        probs = sb("probs", [P, 2, 2, 2, 2, N0])
        sums_inv = sb("sums_inv", [P, 2, HEADS0])
        outs = sb("outs", [P, COUPLES, N0])
        mixed = sb("mixed", [P, 2, HEADS0, HD0])
        mixed_t = sb("mixed_t", [P, N0])
        x_plus = sb("x_plus", [P, 2, N0])
        stats = sb("stats_a", [P, 8])
        raw = sb("raw", [P, 3, KD * F0])
        w_abs = sb("w_abs", [P, 3])
        scratch = nc.dram_tensor("stack_scratch", [SLOTS, 2, 2, PRODUCTS, P // 2, N0], BF16)
        top_scratch = nc.dram_tensor("top_scratch", [SLOTS, 3 * HEADS0, N0], BF16)

        ps_score = [bank("ps_score0"), bank("ps_score1")]
        ps_prob = [bank("ps_prob0"), bank("ps_prob1")]
        ps_qk = bank("ps_qk")
        ps_v = bank("ps_v")
        ps_o = ctx.enter_context(nc.psum_tensor("ps_o", [P, 2, 512], F32))

        w_in, made = sem("w_in"), sem("made")
        source_in = sems("source_in", 3)
        xn_ready, q_ready, k_ready, v_ready = sem("xn_ready"), sem("q_ready"), sem("k_ready"), sem("v_ready")
        q_read = sem("q_read")
        rope_read, v_read = sem("rope_read"), sem("v_read")
        qk_sum, high_ready, rest_ready, mid_ready, parts_ready = (
            sem("qk_sum"), sem("high_ready"), sem("rest_ready"), sem("mid_ready"), sem("parts_ready"))
        scratch_in, stack_in = sems("scratch_in", 3), sems("stack_in", 3)
        score_ready, score_read = sem("score_ready"), sem("score_read")
        prob_ready, prob_read = sem("prob_ready"), sem("prob_read")
        pv_done, outs_ready, outs_t = sem("pv_done"), sem("outs_ready"), sem("outs_t")
        pool_step, top_split = sem("pool_step"), sem("top_split")
        top_t, top_rows_ready = sem("top_t"), sem("top_rows_ready")
        top_scratch_in, top_in = sems("top_scratch_in", 3), sems("top_in", 3)
        norm_step, mixed_ready = sem("norm_step"), sem("mixed_ready")
        mixed_t_ps, mixed_t_ready = sem("mixed_t_ps"), sem("mixed_t_ready")
        merged, x_plus_ready, x_done = sem("merged"), sem("x_plus_ready"), sem("x_done")
        stats_step = sem("stats_step")
        f_in, w_summed, w_total, w_step = sems("f_in", 3), sem("w_summed"), sem("w_total"), sem("w_step")
        w_rounded, w_cut = sem("w_rounded"), sem("w_cut")
        ones_made = sem("ones_made")
        f_w = keep.ffn
        stood = keep.stood
        block = ctx.enter_context(nc.Block())

        def steps(eng, step):
            for i in range(-2, 4):
                step(i, lambda b: (b, b % 3, b // 3))
            with eng.Fori(1, 4) as t:
                for c in range(3):
                    step(c + 1, lambda b: (t * 3 + b, b % 3, t + b // 3), looped=True)
            for i in (13, 14, 15, 16):
                step(i, lambda b: (b, b % 3, b // 3))

        def stages(i, at, looped):
            return tuple(at(b) if looped or 0 <= b < NB else None for b in (i + 2, i + 1, i, i - 1))

        @block.sync
        def _(sp):
            for dst, src in ((w_qk[:, :, :], w.qk), (w_v[:, :], w.v), (w_m[:, :], w.m), (b_qk[:, :], w.bqk),
                             (b_v[:, :], w.bv.partition_broadcast(P)), (b_m[:, :], w.bm), (rope[:, :, :], w.enc),
                             (sign[:, :], w.sign)):
                sp.dma_start(dst, src).then_inc(w_in, 16)

            def load_source(at):
                b, slot, trip = at
                alone(sp, k_ready, b - 2, stood)
                sp.dma_start(source[:, slot:slot + 1, :], ctx_in_dram[bass.ds(b, 1)].rearrange("b p n -> p b n")).then_inc(source_in[slot], 16)

            def stack(at):
                b, slot, trip = at
                sp.wait_ge(parts_ready, b + 1)
                after(sp, stack_in[slot], 64 * trip)
                for o, blocks in ((0, (0, 0, 0, 1, 1, 2)), (1, (0, 1, 2, 0, 1, 0))):
                    for r, part in enumerate(blocks):
                        sp.dma_start(scratch[slot, o, :, r], parts[:, o, part, :]).then_inc(scratch_in[slot], 16)
                sp.wait_ge(scratch_in[slot], 192 * (trip + 1))
                sp.sem_inc(stood, 1)
                after(sp, prob_ready, UNITS * (b - 2))
                for o, dst in ((0, q_stack), (1, k_stack)):
                    for j in range(2):
                        sp.dma_start(dst[64 * j:64 * j + STACK, slot, :, :],
                                     scratch[slot, o, j].rearrange("r (d p) n -> (r d) p n", d=HD0)).then_inc(stack_in[slot], 16)

            def stack_top(at):
                b, slot, trip = at
                sp.wait_ge(top_rows_ready, b + 1)
                sp.dma_start(top_scratch[slot], top_rows[:, :]).then_inc(top_scratch_in[slot], 16)
                sp.wait_ge(top_scratch_in[slot], 16 * (trip + 1))
                view = top_scratch[slot].rearrange("(r j p) n -> j r p n", r=3, j=2)
                for j in range(2):
                    sp.dma_start(q_stack[64 * j + STACK:64 * j + STACK + 3, slot, :, :], view[j]).then_inc(top_in[slot], 16)

            def step(i, at, looped=False):
                first, second, third, fourth = stages(i, at, looped)
                if looped or 0 <= i + 3 < NB:
                    load_source(at(i + 3))
                if first:
                    stack(first)
                if second:
                    stack_top(second)

            load_source((0, 0, 0))
            for k, (src, chunks) in enumerate(((w.gate, KD), (w.up, KD), (w.down, KF))):
                sp.dma_start(raw[:, k, :].rearrange("p (k f) -> p k f", k=chunks),
                             src.rearrange("(k p) f -> p k f", p=P)).then_inc(f_in[k], 16)
            steps(sp, step)

        @block.tensor
        def _(pe):
            pe.wait_ge(w_in, 8 * 16)

            def project(at):
                b, slot, trip = at
                pe.wait_ge(xn_ready, b + 1)
                pe.wait_ge(source_in[slot], 16 * (trip + 1))
                after(pe, rope_read, b)
                after(pe, top_rows_ready, b - 1)
                for k in range(2):
                    mm = pe.matmul(ps_qk[:, k * N0:(k + 1) * N0], w_qk[:, k, :], xn[:, :], start=True, stop=True)
                mm.then_inc(q_ready, 1)
                after(pe, x_done, b - 3)
                for half in range(2):
                    mm = pe.matmul(ps_v[:, half * P:(half + 1) * P], source[:, slot, half * P:(half + 1) * P], w_v[:, :],
                                   start=True, stop=True)
                mm.then_inc(v_ready, 1)

            def project_k(at):
                b, slot, trip = at
                pe.wait_ge(q_read, b + 1)
                for k in range(2):
                    mm = pe.matmul(ps_qk[:, k * N0:(k + 1) * N0], w_qk[:, 2 + k, :], source[:, slot, :], start=True, stop=True)
                mm.then_inc(k_ready, 1)

            def tiles(second, third, v):
                jobs = []
                u = v
                if second and u < UNITS:
                    b, slot, trip = second
                    half, couple, j = u // 8, u // 2 % 4, u % 2
                    if u == 0:
                        pe.wait_ge(stack_in[slot], 64 * (trip + 1))
                    after(pe, score_read, b * UNITS + u - 1)
                    rows = slice(64 * j, 64 * j + STACK)
                    jobs.append((ps_score[j], q_stack, k_stack, rows, slot, 2 * couple, half, score_ready))
                u = v - LAG
                if third and u >= 0:
                    b, slot, trip = third
                    couple, half, j = u // 4, u // 2 % 2, 1 - u % 2
                    if u == 0:
                        pe.wait_ge(top_in[slot], 32 * (trip + 1))
                    after(pe, prob_read, b * UNITS + u - 1)
                    rows = slice(64 * j, 64 * j + STACK + 3)
                    jobs.append((ps_prob[j], k_stack, q_stack, rows, slot, 2 * couple, half, prob_ready))
                for k in range(2):
                    for ps, stationary, moving, rows, slot, pair, half, ready in jobs:
                        mm = pe.matmul(ps[:, k * N0:(k + 1) * N0],
                                       stationary[rows, slot, pair + k, half * P:(half + 1) * P],
                                       moving[rows, slot, pair + k, :], start=True, stop=True)
                        if k == 1:
                            mm.then_inc(ready, 1)

            def mix(at, couple):
                b, slot, trip = at
                pe.wait_ge(prob_read, b * UNITS + 4 * couple + 4)
                if couple == 0:
                    after(pe, mixed_ready, b)
                    pe.wait_ge(v_read, b + 1)
                for m in range(2):
                    for k, j in np.ndindex(2, 2):
                        q = 2 * k + j
                        mm = pe.matmul(ps_o[32 * q:32 * q + 32, couple // 2, (couple % 2) * N0:(couple % 2 + 1) * N0],
                                       values[:, slot, m, 4 * couple + q, :], probs[:, couple % 2, m, j, k, :],
                                       start=(m == 0), stop=(m == 1))
                mm.then_inc(pv_done, 1)

            def turn_outs(at):
                b, slot, trip = at
                for half in range(2):
                    pe.wait_ge(outs_ready, 2 * b + 2)
                    for couple in range(COUPLES):
                        mm = pe.transpose(ps_o[:, half, couple * P:(couple + 1) * P],
                                          outs[:, couple, half * P:(half + 1) * P], keep.identity[:, :])
                mm.then_inc(outs_t, 1)

            def turn_top(at):
                b, slot, trip = at
                alone(pe, top_split, b + 1, stood)
                for half in range(2):
                    mm = pe.transpose(ps_qk[0:3 * HEADS0, :].bitcast(BF16)[:, half * P:(half + 1) * P],
                                      top_parts[:, half].rearrange("p r h -> p (r h)"), keep.identity_bf[:, :])
                mm.then_inc(top_t, 1)

            def turn_mixed(at, v_count):
                b, slot, trip = at
                pe.wait_ge(mixed_ready, b + 1)
                pe.wait_ge(v_read, v_count)
                for half in range(2):
                    mm = pe.transpose(ps_v[:, half * P:(half + 1) * P],
                                      mixed[:, half].rearrange("p h d -> p (h d)"), keep.identity[:, :])
                mm.then_inc(mixed_t_ps, 1)

            def merge(at):
                b, slot, trip = at
                pe.wait_ge(mixed_t_ready, b + 1)
                pe.matmul(ps_v[:, N0:2 * N0], w_m[:, :], mixed_t[:, :], start=True, stop=True).then_inc(merged, 1)

            def step(i, at, looped=False):
                first, second, third, fourth = stages(i, at, looped)
                if first:
                    project(first)
                if fourth:
                    mix(fourth, COUPLES - 1)
                for v in range(UNITS + LAG):
                    tiles(second, third, v)
                    if fourth and v == 2:
                        turn_outs(fourth)
                    if first and v == 0:
                        project_k(first)
                    if fourth and v == 6:
                        turn_mixed(fourth, first[0] + 1 if first else NB)
                    if fourth and v == 8:
                        merge(fourth)
                    u = v - LAG
                    if third and u % 4 == 1 and u > 4:
                        mix(third, u // 4 - 1)
                    if second and v == UNITS + LAG - 1:
                        if first:
                            pe.wait_ge(rope_read, first[0] + 1)
                        turn_top(second)
                if i == -2:
                    pe.wait_ge(w_summed, 3)
                    pe.matmul(ps_o[:, 0, 0:3], keep.ones[:, :], w_abs[:, :], start=True, stop=True).then_inc(w_total, 1)

            steps(pe, step)

        @block.vector
        def _(dve):
            def normalise(b):
                after(dve, q_ready, b)
                dve.tensor_scalar(xn[:, :], keep.x[:, bass.ds(b, 1), :], keep.moments[:, bass.ds(b, 1), 0:1],
                                  keep.rstd[:, bass.ds(b, 1)], ALU.subtract, ALU.mult).then_inc(xn_ready, 1)

            normalise(0)
            dve.memset(values[:, :, :, :, :], 0.0).then_inc(made, 1)
            dve.wait_ge(made, 1)
            dve.memset(values[:, :, :, :, HD0:HD0 + 1], 1.0).then_inc(made, 1)
            dve.wait_ge(w_in, 8 * 16)
            dve.tensor_scalar(rope[:, 1, :], rope[:, 1, :], sign[:, :], None, ALU.mult).then_inc(made, 1)
            dve.tensor_scalar(gate_bm[:, :], b_m[:, :], keep.gate[:, 0:1], None, ALU.mult).then_inc(made, 1)
            dve.wait_ge(made, 4)

            def sum_weights():
                for k in range(3):
                    dve.wait_ge(f_in[k], 16)
                    dve.tensor_reduce(w_abs[:, k:k + 1], raw[:, k, :], AX, ALU.add, apply_absolute_value=True).then_inc(w_summed, 1)
                dve.wait_ge(w_total, 1)
                dve.tensor_scalar(f_w.scale[:, :], ps_o[:, 0, 0:3], 1.0 / (D * F0), Q_EPS, ALU.mult, ALU.add).then_inc(w_step, 1)
                dve.wait_ge(w_step, 1)
                dve.reciprocal(f_w.inv[:, :], f_w.scale[:, :]).then_inc(w_step, 1)
                dve.tensor_scalar(f_w.up_127[:, :], f_w.scale[:, 1:2], 1.0 / 127.0, None, ALU.mult).then_inc(w_step, 1)
                dve.tensor_scalar(f_w.down_gate[:, :], f_w.scale[:, 2:3], keep.gate[:, 2:3], None, ALU.mult).then_inc(w_step, 1)

            def cut_weight(k):
                dve.wait_ge(w_rounded, k + 1)
                dve.tensor_scalar(raw[:, k, :], raw[:, k, :], MAGIC, -1.0, ALU.subtract, ALU.max).then_inc(w_cut, 1)
                dve.wait_ge(w_cut, k + 1)
                dve.tensor_scalar(f_w.ternary[:, k, :], raw[:, k, :], 1.0, None, ALU.min)

            def rotate(at, o):
                b, slot, trip = at
                after(dve, qk_sum, b)
                dve.wait_ge((q_ready, k_ready)[o], b + 1)
                for k in range(2):
                    op = dve.scalar_tensor_tensor(turned[:, o, k, :], ps_qk[:, k * N0:(k + 1) * N0],
                                                  b_qk[:, 2 * o + k:2 * o + k + 1], rope[:, k, :], ALU.add, ALU.mult)
                op.then_inc((q_read, rope_read)[o], 1)

            def values_out(at):
                b, slot, trip = at
                dve.wait_ge(v_ready, b + 1)
                after(dve, pv_done, COUPLES * (b - 2))
                dve.tensor_tensor(values[:, slot, :, :, 0:HD0],
                                  ps_v[:, 0:2 * P].rearrange("p (m h d) -> p m h d", m=2, h=HEADS0),
                                  b_v[:, :].rearrange("p (o h d) -> p o h d", o=1, h=HEADS0).broadcast_to([P, 2, HEADS0, HD0]),
                                  ALU.add).then_inc(v_read, 1)

            def maxima(at, u):
                b, slot, trip = at
                half, couple, j = u // 8, u // 2 % 4, u % 2
                dve.wait_ge(score_ready, b * UNITS + u + 1)
                if u == 0:
                    after(dve, top_split, b)
                dve.tensor_reduce(top[:, half, j, 2 * couple:2 * couple + 2], ps_score[j][:, :].rearrange("p (k n) -> p k n", k=2),
                                  AX, ALU.max).then_inc(score_read, 1)

            def divide(at):
                b, slot, trip = at
                dve.wait_ge(outs_t, b + 1)
                out = ps_o[:, :, :].rearrange("p m (h d) -> p m h d", h=HEADS0)
                dve.reciprocal(sums_inv[:, :, :], out[:, :, :, HD0]).then_inc(norm_step, 1)
                dve.wait_ge(norm_step, b + 1)
                after(dve, mixed_t_ps, b)
                dve.tensor_tensor(mixed[:, :, :, :], out[:, :, :, 0:HD0],
                                  sums_inv[:, :, :].unsqueeze(3).broadcast_to([P, 2, HEADS0, HD0]),
                                  ALU.mult).then_inc(mixed_ready, 1)

            def finish(at):
                b, slot, trip = at
                dve.wait_ge(merged, b + 1)
                dve.wait_ge(x_plus_ready, b + 1)
                dve.scalar_tensor_tensor(keep.x[:, bass.ds(b, 1), :], ps_v[:, N0:2 * N0].unsqueeze(1), keep.gate[:, 0:1],
                                         x_plus[:, 0:1, :], ALU.mult, ALU.add).then_inc(x_done, 1)
                alone(dve, x_done, b + 1, stood)
                layer_stats(dve, stats, keep.moments, keep.x[:, bass.ds(b, 1), :], b, stats_step, stood)

            def step(i, at, looped=False):
                first, second, third, fourth = stages(i, at, looped)
                if first:
                    rotate(first, 0)
                for u in range(UNITS):
                    if second:
                        maxima(second, u)
                    if first and u == 0:
                        rotate(first, 1)
                    if first and u == 2:
                        values_out(first)
                    if fourth and u == 3:
                        divide(fourth)
                    if first and u == 13 and (looped or i + 2 < NB - 1):
                        normalise(first[0] + 1)
                    if fourth and u == 11:
                        finish(fourth)
                if i == -2:
                    sum_weights()
                    for k in range(3):
                        cut_weight(k)

            steps(dve, step)

        @block.scalar
        def _(act):
            def high(at):
                b, slot, trip = at
                act.wait_ge(qk_sum, b + 1)
                act.activation(parts[:, :, 0, :], qk[:, :, :], ACT.Copy).then_inc(high_ready, 1)

            def middle(at):
                b, slot, trip = at
                act.wait_ge(rest_ready, b + 1)
                act.activation(parts[:, :, 1, :], rest[:, :, :], ACT.Copy).then_inc(mid_ready, 1)

            def exponent(at, u):
                b, slot, trip = at
                act.wait_ge(prob_ready, b * UNITS + u + 1)
                couple, half, j = u // 4, u // 2 % 2, 1 - u % 2
                after(act, pv_done, b * COUPLES + couple - 1)
                act.activation(probs[:, couple % 2, half, j], ps_prob[j][:, :].rearrange("p (k n) -> p k n", k=2), ACT.Exp,
                               scale=float(HD0) ** -0.5).then_inc(prob_read, 1)

            def step(i, at, looped=False):
                first, second, third, fourth = stages(i, at, looped)
                if fourth:
                    outs_out(fourth, 1)
                for v in range(UNITS + LAG):
                    u = v - LAG
                    if second and v == UNITS + LAG - 1:
                        rows_out(second, at(i) if looped or i >= 0 else None)
                    if third and u >= 0:
                        exponent(third, u)
                    if first and v == 3:
                        if looped or i + 2 > 0:
                            pb, pslot, ptrip = at(i + 1)
                            act.wait_ge(scratch_in[pslot], 192 * (ptrip + 1))
                        high(first)
                    if fourth and v == 6:
                        b, slot, trip = fourth
                        act.wait_ge(mixed_t_ps, b + 1)
                        act.activation(mixed_t[:, :], ps_v[:, 0:N0], ACT.Copy).then_inc(mixed_t_ready, 1)
                    if first and v == 6:
                        middle(first)
                    if third and u == 10:
                        outs_out(third, 0)
                if i == -2:
                    act.wait_ge(w_step, 2)
                    for k in range(3):
                        act.activation(raw[:, k, :], raw[:, k, :], ACT.Copy, bias=MAGIC, scale=f_w.inv[:, k:k + 1]).then_inc(w_rounded, 1)

            def outs_out(at, half):
                b, slot, trip = at
                act.wait_ge(pv_done, b * COUPLES + 2 * half + 2)
                after(act, outs_t, b)
                act.activation(outs[:, 2 * half:2 * half + 2, :], ps_o[:, half, :].rearrange("p (c n) -> p c n", c=2),
                               ACT.Copy).then_inc(outs_ready, 1)

            def rows_out(at, before):
                b, slot, trip = at
                act.wait_ge(top_t, b + 1)
                if before:
                    pb, pslot, ptrip = before
                    act.wait_ge(top_scratch_in[pslot], 16 * (ptrip + 1))
                act.activation(top_rows[:, :], ps_qk[0:3 * HEADS0, :].bitcast(BF16)[:, 0:N0], ACT.Copy).then_inc(top_rows_ready, 1)

            steps(act, step)

        @block.gpsimd
        def _(pool):
            pool.memset(k_stack[:, :, :, :], 1.0).then_inc(ones_made, 1)
            pool.wait_ge(ones_made, 1)
            pool.wait_ge(made, 4)

            def split(at):
                b, slot, trip = at
                pool.wait_ge(rope_read, b + 1)
                pool.tensor_tensor(qk[:, :, :], turned[:, :, 0, :], turned[:, :, 1, :], ALU.add).then_inc(qk_sum, 1)
                pool.wait_ge(high_ready, b + 1)
                pool.tensor_tensor(rest[:, :, :], qk[:, :, :], parts[:, :, 0, :], ALU.subtract).then_inc(rest_ready, 1)
                pool.wait_ge(mid_ready, b + 1)
                pool.tensor_tensor(parts[:, :, 2, :], rest[:, :, :], parts[:, :, 1, :], ALU.subtract).then_inc(parts_ready, 1)

            def split_top(at):
                b, slot, trip = at
                pool.wait_ge(score_read, UNITS * (b + 1))
                alone(pool, top_t, b, stood)
                flat = top[:, :, :, :].rearrange("p m j q -> p m (j q)")
                pool.tensor_scalar(top_parts[:, :, 0, :], flat, -1.0, None, ALU.mult).then_inc(pool_step, 1)
                pool.wait_ge(pool_step, 4 * b + 1)
                pool.tensor_tensor(top_rest[:, :, :], flat, top_parts[:, :, 0, :], ALU.add).then_inc(pool_step, 1)
                alone(pool, pool_step, 4 * b + 2, stood)
                pool.tensor_scalar(top_parts[:, :, 1, :], top_rest[:, :, :], -1.0, None, ALU.mult).then_inc(pool_step, 1)
                pool.wait_ge(pool_step, 4 * b + 3)
                pool.tensor_tensor(top_rest[:, :, :], top_rest[:, :, :], top_parts[:, :, 1, :], ALU.add).then_inc(pool_step, 1)
                alone(pool, pool_step, 4 * b + 4, stood)
                pool.tensor_scalar(top_parts[:, :, 2, :], top_rest[:, :, :], -1.0, None, ALU.mult).then_inc(top_split, 1)

            def step(i, at, looped=False):
                first, second, third, fourth = stages(i, at, looped)
                if fourth:
                    b, slot, trip = fourth
                    alone(pool, x_done, b, stood)
                    pool.tensor_tensor(x_plus[:, 0:1, :], keep.x[:, bass.ds(b, 1), :],
                                       gate_bm[:, 0:1].unsqueeze(2).broadcast_to([P, 1, N0]), ALU.add).then_inc(x_plus_ready, 1)
                if first:
                    split(first)
                if second:
                    split_top(second)

            steps(pool, step)
            pool.wait_ge(stats_step, 3 * NB)
            inverse_deviation(pool, keep, 1)


F0 = 1024
Q_EPS = 1e-5
KD, KF = D // P, F0 // P


def layer0_ffn(nc, keep, w):
    with ExitStack() as ctx:
        sem = lambda n: ctx.enter_context(nc.semaphore("f_" + n))
        sems = lambda n, k: [sem(f"{n}{i}") for i in range(k)]
        sb = lambda n, shape, dt=F32: ctx.enter_context(nc.sbuf_tensor("f_" + n, shape, dt))
        ps = lambda n, shape, dt=F32: ctx.enter_context(nc.psum_tensor("f_" + n, shape, dt))

        ternary, w_scale, up_127, down_gate = keep.ffn.ternary, keep.ffn.scale, keep.ffn.up_127, keep.ffn.down_gate
        w_gu = [ternary[:, k, :].rearrange("p (k f) -> p k f", k=KD) for k in range(2)]
        w_d = ternary[:, 2, :].rearrange("p (k n) -> p k n", k=KF)
        xn = sb("xn", [P, D])
        x_top = sb("x_top", [P, 1])
        x_scale = sb("x_scale", [P, 2, 1])
        x_inv = sb("x_inv", [P, 2, 1])
        gate_scale = sb("gate_scale", [P, 2, 3])
        x_round = sb("x_round", [P, D])
        x_int = sb("x_int", [P, D], BF16)
        x_int_t = sb("x_int_t", [P, 2, KD, P], BF16)
        silu = sb("silu", [P, F0])
        hidden = sb("hidden", [P, 2, F0])
        h_top = sb("h_top", [P, 1])
        h_scale = sb("h_scale", [P, 2, 1])
        h_inv = sb("h_inv", [P, 1])
        h_mult = sb("h_mult", [P, 2, 1])
        out_scale = sb("out_scale", [P, 2, 1])
        h_round = sb("h_round", [P, F0])
        h_int = sb("h_int", [P, F0], BF16)
        h_int_t = sb("h_int_t", [P, KF, P], BF16)
        stats = sb("stats", [P, 8])
        zeros = sb("zeros", [P, ZERO_ROWS * D])

        ps_gate = ps("ps_gate", [P, F0])
        ps_up = ps("ps_up", [P, F0])
        ps_x = ps("ps_x", [P, KD, P], BF16)
        ps_h = ps("ps_h", [P, KF, P], BF16)
        ps_down = ps("ps_down", [P, 512])

        x_step, scales_ready = sem("x_step"), sem("scales_ready")
        x_round_ready, x_int_ready, x_t_ready, x_t_read = (
            sem("x_round_ready"), sem("x_int_ready"), sem("x_t_ready"), sem("x_t_read"))
        gate_ready, up_ready, silu_ready, hidden_ready = (
            sem("gate_ready"), sem("up_ready"), sem("silu_ready"), sem("hidden_ready"))
        h_step, h_mult_ready, out_scale_ready = sem("h_step"), sem("h_mult_ready"), sem("out_scale_ready")
        h_round_ready, h_int_ready, h_t_ready, h_t_read = (
            sem("h_round_ready"), sem("h_int_ready"), sem("h_t_ready"), sem("h_t_read"))
        down_ready, x_done, stats_step = sem("down_ready"), sem("x_done"), sem("stats_step")
        zeros_made, filled = sem("zeros_made"), sem("filled")
        stood = keep.stood
        block = ctx.enter_context(nc.Block())

        def steps(step):
            def run(eng):
                for i in range(-2, 2):
                    step(i, lambda b: (b, b % 2))
                with eng.Fori(1, 7) as t:
                    for c in range(2):
                        step(c, lambda b: (t * 2 + b, b % 2), looped=True)
                for i in (14, 15):
                    step(i, lambda b: (b, b % 2))
            return run

        def stages(i, looped):
            if looped:
                return i + 2, i + 1, i
            return tuple(b if 0 <= b < NB else None for b in (i + 2, i + 1, i))

        @block.sync
        def _(sp):
            att = keep.attention
            for dst, src in ((att.norms[:, :], w.norms), (att.w_k[:, :, :], w.k.rearrange("(k p) n -> p k n", p=P)),
                             (att.w_v[:, :, :], w.v1.rearrange("(k p) n -> p k n", p=P)),
                             (att.w_q[:, :, :], w.q.rearrange("(k p) n -> p k n", p=P)),
                             (att.w_o[:, :, :], w.o.rearrange("(h p) n -> p h n", p=P))):
                sp.dma_start(dst, src).then_inc(keep.attention_in, 16)
            sp.wait_ge(zeros_made, 1)
            share = TOKEN_ROW // P
            for n in range(0, share, share // 4):
                rows = keep.rows[0:TOKEN_ROW, :].rearrange("(p n) d -> p n d", p=P)[:, n:n + share // 4, :]
                sp.dma_start(rows.rearrange("p (a n) d -> p a (n d)", n=ZERO_ROWS),
                             zeros[:, :].unsqueeze(1).broadcast_to([P, share // 4 // ZERO_ROWS, ZERO_ROWS * D])).then_inc(filled, 16)
            sp.wait_ge(filled, 4 * 16)

        @block.tensor
        def _(pe):
            def gate_up(at):
                b, slot = at
                pe.wait_ge(x_t_read, b + 1)
                after(pe, silu_ready, b)
                for k, (dst, ready) in enumerate(((ps_gate, gate_ready), (ps_up, up_ready))):
                    if k:
                        after(pe, hidden_ready, b)
                    for n in range(0, F0, 512):
                        for c in range(KD):
                            mm = pe.matmul(dst[:, n:n + 512], x_int_t[:, slot, c, :], w_gu[k][:, c, n:n + 512],
                                           start=(c == 0), stop=(c == KD - 1))
                    mm.then_inc(ready, 1)

            def turn_x(at):
                b, slot = at
                pe.wait_ge(x_int_ready, b + 1)
                after(pe, x_t_read, b)
                for c in range(KD):
                    mm = pe.transpose(ps_x[:, c, :], x_int[:, c * P:(c + 1) * P], keep.identity_bf[:, :])
                mm.then_inc(x_t_ready, 1)

            def turn_hidden(at):
                b, slot = at
                pe.wait_ge(h_int_ready, b + 1)
                for c in range(KF):
                    mm = pe.transpose(ps_h[:, c, :], h_int[:, c * P:(c + 1) * P], keep.identity_bf[:, :])
                mm.then_inc(h_t_ready, 1)

            def down(at):
                b, slot = at
                pe.wait_ge(h_t_read, b + 1)
                after(pe, x_done, b)
                for c in range(KF):
                    mm = pe.matmul(ps_down[:, 0:D], h_int_t[:, c, :], w_d[:, c, :], start=(c == 0), stop=(c == KF - 1))
                mm.then_inc(down_ready, 1)

            def step(i, at, looped=False):
                first, second, third = stages(i, looped)
                if second is not None:
                    gate_up(at(second))
                if third is not None:
                    turn_hidden(at(third))
                if third is not None:
                    down(at(third))
                if first is not None:
                    turn_x(at(first))

            steps(step)(pe)

        @block.vector
        def _(dve):
            def quantise_x(at):
                b, slot = at
                after(dve, x_round_ready, b)
                dve.tensor_scalar(xn[:, :].unsqueeze(1), keep.x[:, bass.ds(b, 1), :], keep.moments[:, bass.ds(b, 1), 0:1],
                                  keep.rstd[:, bass.ds(b, 1)], ALU.subtract, ALU.mult).then_inc(x_step, 1)
                dve.wait_ge(x_step, 4 * b + 1)
                dve.tensor_reduce(x_top[:, :], xn[:, :], AX, ALU.max, apply_absolute_value=True).then_inc(x_step, 1)
                dve.wait_ge(x_step, 4 * b + 2)
                dve.tensor_scalar(x_scale[:, slot, :], x_top[:, :], 1.0 / 127.0, Q_EPS, ALU.mult, ALU.add).then_inc(x_step, 1)
                dve.wait_ge(x_step, 4 * b + 3)
                dve.reciprocal(x_inv[:, slot, :], x_scale[:, slot, :]).then_inc(x_step, 1)

            def hide(at):
                b, slot = at
                dve.wait_ge(silu_ready, b + 1)
                dve.wait_ge(up_ready, b + 1)
                dve.tensor_tensor(hidden[:, slot, :], silu[:, :], ps_up[:, :], ALU.mult).then_inc(hidden_ready, 1)
                dve.wait_ge(hidden_ready, b + 1)
                dve.tensor_reduce(h_top[:, :], hidden[:, slot, :], AX, ALU.max, apply_absolute_value=True).then_inc(h_step, 1)
                dve.wait_ge(h_step, 3 * b + 1)
                dve.wait_ge(scales_ready, 3 * b + 3)
                after(dve, out_scale_ready, b - 1)
                dve.tensor_scalar(h_scale[:, slot, :], h_top[:, :], gate_scale[:, slot, 2:3], Q_EPS, ALU.mult,
                                  ALU.add).then_inc(h_step, 1)
                dve.wait_ge(h_step, 3 * b + 2)
                dve.reciprocal(h_inv[:, :], h_scale[:, slot, :]).then_inc(h_step, 1)
                dve.wait_ge(h_step, 3 * b + 3)
                dve.tensor_scalar(h_mult[:, slot, :], h_inv[:, :], gate_scale[:, slot, 1:2], None, ALU.mult).then_inc(h_mult_ready, 1)

            def finish(at):
                b, slot = at
                dve.wait_ge(down_ready, b + 1)
                dve.wait_ge(out_scale_ready, b + 1)
                dve.scalar_tensor_tensor(keep.x[:, bass.ds(b, 1), :], ps_down[:, 0:D].unsqueeze(1), out_scale[:, slot, :],
                                         keep.x[:, bass.ds(b, 1), :], ALU.mult, ALU.add).then_inc(x_done, 1)
                alone(dve, x_done, b + 1, stood)
                layer_stats(dve, stats, keep.moments, keep.x[:, bass.ds(b, 1), :], b, stats_step, stood)

            def step(i, at, looped=False):
                first, second, third = stages(i, looped)
                if third is not None:
                    b, slot = at(third)
                    dve.wait_ge(h_round_ready, b + 1)
                    after(dve, h_t_ready, b)
                    dve.tensor_scalar(h_int[:, :], h_round[:, :], MAGIC, None, ALU.subtract).then_inc(h_int_ready, 1)
                if first is not None:
                    quantise_x(at(first))
                if first is not None:
                    b, slot = at(first)
                    dve.wait_ge(x_round_ready, b + 1)
                    after(dve, x_t_ready, b)
                    dve.tensor_scalar(x_int[:, :], x_round[:, :], MAGIC, None, ALU.subtract).then_inc(x_int_ready, 1)
                if second is not None:
                    hide(at(second))
                if third is not None:
                    finish(at(third))

            steps(step)(dve)

        @block.scalar
        def _(act):
            def step(i, at, looped=False):
                first, second, third = stages(i, looped)
                if third is not None:
                    b, slot = at(third)
                    act.wait_ge(h_mult_ready, b + 1)
                    after(act, h_int_ready, b)
                    act.activation(h_round[:, :], hidden[:, slot, :], ACT.Copy, bias=MAGIC,
                                   scale=h_mult[:, slot, :]).then_inc(h_round_ready, 1)
                if second is not None:
                    b, slot = at(second)
                    act.wait_ge(gate_ready, b + 1)
                    act.wait_ge(scales_ready, 3 * b + 3)
                    after(act, hidden_ready, b)
                    act.activation(silu[:, :], ps_gate[:, :], ACT.Silu, scale=gate_scale[:, slot, 0:1]).then_inc(silu_ready, 1)
                if first is not None:
                    b, slot = at(first)
                    act.wait_ge(x_step, 4 * b + 4)
                    after(act, x_int_ready, b)
                    act.activation(x_round[:, :], xn[:, :], ACT.Copy, bias=MAGIC,
                                   scale=x_inv[:, slot, :]).then_inc(x_round_ready, 1)
                if third is not None:
                    b, slot = at(third)
                    act.wait_ge(h_t_ready, b + 1)
                    after(act, down_ready, b)
                    act.activation(h_int_t[:, :, :], ps_h[:, :, :], ACT.Copy).then_inc(h_t_read, 1)
                if first is not None:
                    b, slot = at(first)
                    act.wait_ge(x_t_ready, b + 1)
                    after(act, up_ready, b - 1)
                    act.activation(x_int_t[:, slot], ps_x[:, :, :], ACT.Copy).then_inc(x_t_read, 1)

            steps(step)(act)

        @block.gpsimd
        def _(pool):
            pool.memset(zeros[:, :], 0.0).then_inc(zeros_made, 1)

            def step(i, at, looped=False):
                first, second, third = stages(i, looped)
                if first is not None:
                    b, slot = at(first)
                    pool.wait_ge(x_step, 4 * b + 3)
                    after(pool, h_mult_ready, b - 1)
                    for k, other in enumerate((w_scale[:, 0:1], w_scale[:, 1:2], up_127[:, :])):
                        pool.tensor_tensor(gate_scale[:, slot, k:k + 1], x_scale[:, slot, :], other, ALU.mult).then_inc(scales_ready, 1)
                if second is not None:
                    b, slot = at(second)
                    pool.wait_ge(h_step, 3 * b + 2)
                    after(pool, x_done, b - 1)
                    pool.tensor_tensor(out_scale[:, slot, :], h_scale[:, slot, :], down_gate[:, :], ALU.mult).then_inc(out_scale_ready, 1)

            steps(step)(pool)
            pool.wait_ge(stats_step, 3 * NB)
            inverse_deviation(pool, keep, 2)


HEADS1, GROUPS, HD1 = 16, 4, 128
SHARE = HEADS1 // GROUPS
WIDTH = SHARE * HD1
RMS_EPS = 1e-6


def layer1_attention(nc, keep, w):
    with ExitStack() as ctx:
        sem = lambda n: ctx.enter_context(nc.semaphore("g_" + n))
        sems = lambda n, k: [sem(f"{n}{i}") for i in range(k)]
        sb = lambda n, shape, dt=F32: ctx.enter_context(nc.sbuf_tensor("g_" + n, shape, dt))
        bank = lambda n: ctx.enter_context(nc.psum_tensor("g_" + n, [P, 512], F32))

        att = keep.attention
        w_q, w_k, w_v, w_o, norms, w_in = att.w_q, att.w_k, att.w_v, att.w_o, att.norms, keep.attention_in
        k_weight = sb("k_weight", [P, 1])
        ctx_t = sb("ctx_t", [P, 2, KD, P])
        xn = sb("xn", [P, D])
        x_t = sb("x_t", [P, KD, P])
        square = sb("square", [P, 2, SHARE, HD1])
        power = sb("power", [P, 2, SHARE])
        inverse = sb("inverse", [P, 2, SHARE])
        normed = sb("normed", [P, 2, SHARE, HD1])
        q_t = sb("q_t", [P, 2, GROUPS, WIDTH])
        k_t = sb("k_t", [P, 2, GROUPS, P])
        values = sb("values", [P, 2, WIDTH])
        bias = sb("bias", [P, 2, SHARE])
        probs = sb("probs", [P, 2, SHARE, P])
        sums = sb("sums", [P, 2, SHARE])
        sums_inv = sb("sums_inv", [P, 2, SHARE])
        weights = sb("weights", [P, 2, SHARE, P])
        weights_t = sb("weights_t", [P, 2, WIDTH])
        out_t = sb("out_t", [P, 2, SHARE, P])
        stats = sb("stats", [P, 8])

        ps_proj = [bank("ps_proj0"), bank("ps_proj1")]
        ps_turn = bank("ps_turn")
        ps_score = [bank("ps_score0"), bank("ps_score1")]
        ps_w = bank("ps_w")
        ps_out = bank("ps_out")
        ps_x = bank("ps_x")

        made = sem("made")
        ctx_in = sems("ctx_in", 2)
        xn_ready, x_turned, x_t_ready = sem("xn_ready"), sem("x_turned"), sem("x_t_ready")
        proj_ready, squared, powered, inv_step, normed_ready, turned, turned_read = (
            sem("proj_ready"), sem("squared"), sem("powered"), sem("inv_step"), sem("normed_ready"), sem("turned"),
            sem("turned_read"))
        v_ready, v_read = sem("v_ready"), sem("v_read")
        score_ready, bias_ready, probs_ready, inv_ready, weights_ready = (
            sem("score_ready"), sem("bias_ready"), sem("probs_ready"), sem("inv_ready"), sem("weights_ready"))
        w_turned, w_t_ready, out_ready, out_read, merged = (
            sem("w_turned"), sem("w_t_ready"), sem("out_ready"), sem("out_read"), sem("merged"))
        x_done, stats_step = sem("x_done"), sem("stats_step")
        stood = keep.stood
        block = ctx.enter_context(nc.Block())
        NP = 1 + GROUPS

        def steps(step):
            def run(eng):
                for i in (-1, 0):
                    step(i, lambda b: (b, b % 2, b // 2))
                with eng.Fori(0, 6) as t:
                    for c in (1, 2):
                        step(c, lambda b: (t * 2 + b, b % 2, t + b // 2), looped=True)
                for i in (13, 14, 15):
                    step(i, lambda b: (b, b % 2, b // 2))
            return run

        def stages(i, looped):
            if looped:
                return i + 1, i
            return tuple(b if 0 <= b < NB else None for b in (i + 1, i))

        @block.sync
        def _(sp):
            def load_ctx(at):
                b, slot, trip = at
                alone(sp, v_ready, b - 1, stood)
                sp.dma_start(ctx_t[:, slot], w.ctx_t[bass.ds(b, 1)].rearrange("b (k p) n -> p (b k) n", p=P)).then_inc(ctx_in[slot], 16)

            load_ctx((0, 0, 0))

            def step(i, at, looped=False):
                if looped or i + 2 < NB:
                    load_ctx(at(i + 2))
            for i in (-1, 0):
                step(i, lambda b: (b, b % 2, b // 2))
            with sp.Fori(0, 6) as t:
                for c in (1, 2):
                    step(c, lambda b: (t * 2 + b, b % 2, t + b // 2), looped=True)
            step(13, lambda b: (b, b % 2, b // 2))

        @block.tensor
        def _(pe):
            pe.wait_ge(w_in, 5 * 16)

            def turn_x(at):
                b, slot, trip = at
                pe.wait_ge(xn_ready, b + 1)
                after(pe, turned_read, NP * b)
                for c in range(KD):
                    mm = pe.transpose(ps_turn[:, c * P:(c + 1) * P], xn[:, c * P:(c + 1) * P], keep.identity[:, :])
                mm.then_inc(x_turned, 1)

            def project(at, n):
                b, slot, trip = at
                if n == 0:
                    pe.wait_ge(ctx_in[slot], 16 * (trip + 1))
                elif n == 1:
                    pe.wait_ge(x_t_ready, b + 1)
                if n == 1:
                    pe.wait_ge(v_read, b + 1)
                else:
                    after(pe, normed_ready, NP * b + n - 2 + (n == 0))
                bank = ps_proj[0 if n == 0 else n % 2]
                for c in range(KD):
                    if n == 0:
                        mm = pe.matmul(bank[:, :], ctx_t[:, slot, c, :], w_k[:, c, :], start=(c == 0), stop=(c == KD - 1))
                    else:
                        mm = pe.matmul(bank[:, :], x_t[:, c, :], w_q[:, c, (n - 1) * WIDTH:n * WIDTH],
                                       start=(c == 0), stop=(c == KD - 1))
                mm.then_inc(proj_ready, 1)

            def project_v(at):
                b, slot, trip = at
                after(pe, normed_ready, NP * b)
                for c in range(KD):
                    mm = pe.matmul(ps_proj[1][:, :], ctx_t[:, slot, c, :], w_v[:, c, :], start=(c == 0), stop=(c == KD - 1))
                mm.then_inc(v_ready, 1)

            def turn_normed(at, n):
                b, slot, trip = at
                pe.wait_ge(normed_ready, NP * b + n + 1)
                if n == 0:
                    pe.wait_ge(x_t_ready, b + 1)
                else:
                    pe.wait_ge(turned_read, NP * b + n)
                for h in range(SHARE):
                    mm = pe.transpose(ps_turn[:, h * P:(h + 1) * P], normed[:, n % 2, h, :], keep.identity[:, :])
                mm.then_inc(turned, 1)

            def score(at, g):
                b, slot, trip = at
                if g == 0:
                    pe.wait_ge(turned_read, NP * (b + 1))
                after(pe, probs_ready, GROUPS * b + g - 1)
                for h in range(SHARE):
                    mm = pe.matmul(ps_score[g % 2][:, h * P:(h + 1) * P], q_t[:, slot, g, h * P:(h + 1) * P], k_t[:, slot, g, :],
                                   start=True, stop=True)
                mm.then_inc(score_ready, 1)

            def turn_weights(at, g):
                b, slot, trip = at
                n = GROUPS * b + g
                pe.wait_ge(weights_ready, n + 1)
                after(pe, w_t_ready, n)
                for h in range(SHARE):
                    mm = pe.transpose(ps_w[:, h * P:(h + 1) * P], weights[:, g % 2, h, :], keep.identity[:, :])
                mm.then_inc(w_turned, 1)

            def mix(at, g):
                b, slot, trip = at
                n = GROUPS * b + g
                pe.wait_ge(w_t_ready, n + 1)
                after(pe, out_read, n)
                pe.matmul(ps_out[:, :], values[:, slot, g * P:(g + 1) * P], weights_t[:, g % 2, :],
                          start=True, stop=True).then_inc(out_ready, 1)

            def merge(at, g):
                b, slot, trip = at
                pe.wait_ge(out_read, GROUPS * b + g + 1)
                if g == 0:
                    after(pe, x_done, b)
                for h in range(SHARE):
                    mm = pe.matmul(ps_x[:, 0:D], out_t[:, g % 2, h, :], w_o[:, SHARE * g + h, :],
                                   start=(g == 0 and h == 0), stop=(g == GROUPS - 1 and h == SHARE - 1))
                mm.then_inc(merged, 1)

            def step(i, at, looped=False):
                first, second = stages(i, looped)
                f = at(first) if first is not None else None
                s = at(second) if second is not None else None
                if s:
                    score(s, 0)
                if f:
                    turn_x(f)
                    project(f, 0)
                    project_v(f)
                for g in range(GROUPS):
                    if s and g + 1 < GROUPS:
                        score(s, g + 1)
                    if f:
                        project(f, g + 1)
                    if s:
                        turn_weights(s, g)
                    if f:
                        turn_normed(f, g)
                    if s:
                        if g:
                            merge(s, g - 1)
                        mix(s, g)
                if f:
                    turn_normed(f, GROUPS)
                if s:
                    merge(s, GROUPS - 1)

            steps(step)(pe)

        @block.vector
        def _(dve):
            def normalise(b):
                after(dve, x_turned, b)
                dve.tensor_scalar(xn[:, :].unsqueeze(1), keep.x[:, bass.ds(b, 1), :], keep.moments[:, bass.ds(b, 1), 0:1],
                                  keep.rstd[:, bass.ds(b, 1)], ALU.subtract, ALU.mult).then_inc(xn_ready, 1)

            normalise(0)
            dve.wait_ge(w_in, 16 * 5)
            dve.tensor_scalar(k_weight[:, :], norms[:, 0:1], norms[:, 1:2], float(HD1) ** -0.5, ALU.mult, ALU.mult).then_inc(made, 1)

            def power_of(at, n):
                b, slot, trip = at
                dve.wait_ge(squared, NP * b + n + 1)
                after(dve, normed_ready, NP * b + n - 1)
                dve.tensor_reduce(power[:, n % 2, :], square[:, n % 2], AX, ALU.add).then_inc(powered, 1)

            def norm(at, n):
                b, slot, trip = at
                dve.wait_ge(inv_step, 2 * (NP * b + n) + 2)
                after(dve, turned, NP * b + n - 1)
                dve.tensor_tensor(normed[:, n % 2], ps_proj[n % 2][:, :].rearrange("p (h d) -> p h d", h=SHARE),
                                  inverse[:, n % 2, :].unsqueeze(2).broadcast_to([P, SHARE, HD1]), ALU.mult).then_inc(normed_ready, 1)

            def top(at, g):
                b, slot, trip = at
                n = GROUPS * b + g
                dve.wait_ge(score_ready, n + 1)
                after(dve, probs_ready, n - 1)
                dve.tensor_reduce(bias[:, g % 2, :], ps_score[g % 2][:, :].rearrange("p (h m) -> p h m", h=SHARE), AX, ALU.max,
                                  negate=True).then_inc(bias_ready, 1)

            def invert(at, g):
                b, slot, trip = at
                n = GROUPS * b + g
                dve.wait_ge(probs_ready, n + 1)
                after(dve, weights_ready, n - 1)
                dve.reciprocal(sums_inv[:, g % 2, :], sums[:, g % 2, :]).then_inc(inv_ready, 1)

            def weights_out(at, g):
                b, slot, trip = at
                n = GROUPS * b + g
                dve.wait_ge(w_turned, n + 1)
                after(dve, out_ready, n - 1)
                dve.tensor_copy(weights_t[:, g % 2, :], ps_w[:, :]).then_inc(w_t_ready, 1)

            def step(i, at, looped=False):
                first, second = stages(i, looped)
                f = at(first) if first is not None else None
                s = at(second) if second is not None else None
                if s:
                    top(s, 0)
                if f:
                    power_of(f, 0)
                for g in range(GROUPS):
                    if s:
                        if g + 1 < GROUPS:
                            top(s, g + 1)
                        invert(s, g)
                    if f:
                        norm(f, g)
                    if s:
                        weights_out(s, g)
                    if f:
                        power_of(f, g + 1)
                if f:
                    norm(f, GROUPS)
                    if looped or first + 1 < NB:
                        normalise(at(first)[0] + 1)
                if s:
                    b = s[0]
                    dve.wait_ge(merged, GROUPS * (b + 1))
                    dve.scalar_tensor_tensor(keep.x[:, bass.ds(b, 1), :], ps_x[:, 0:D].unsqueeze(1), keep.gate[:, 1:2],
                                             keep.x[:, bass.ds(b, 1), :], ALU.mult, ALU.add).then_inc(x_done, 1)
                    alone(dve, x_done, b + 1, stood)
                    layer_stats(dve, stats, keep.moments, keep.x[:, bass.ds(b, 1), :], b, stats_step, stood)

            steps(step)(dve)

        @block.scalar
        def _(act):
            act.wait_ge(made, 1)

            def squares(at, n):
                b, slot, trip = at
                act.wait_ge(proj_ready, NP * b + n + 1)
                after(act, powered, NP * b + n - 1)
                act.activation(square[:, n % 2], ps_proj[n % 2][:, :].rearrange("p (h d) -> p h d", h=SHARE), ACT.Square).then_inc(squared, 1)

            def turned_out(at, n):
                b, slot, trip = at
                act.wait_ge(turned, NP * b + n + 1)
                after(act, score_ready, GROUPS * (b - 1))
                if n == 0:
                    act.activation(k_t[:, slot], ps_turn[:, :].rearrange("p (g m) -> p g m", g=GROUPS), ACT.Copy,
                                   scale=k_weight[:, :]).then_inc(turned_read, 1)
                else:
                    act.activation(q_t[:, slot, n - 1, :], ps_turn[:, :], ACT.Copy).then_inc(turned_read, 1)

            def exponents(at, g):
                b, slot, trip = at
                n = GROUPS * b + g
                act.wait_ge(bias_ready, n + 1)
                after(act, weights_ready, n - 1)
                for h in range(SHARE):
                    op = act.activation(probs[:, g % 2, h, :], ps_score[g % 2][:, h * P:(h + 1) * P], ACT.Exp,
                                        bias=bias[:, g % 2, h:h + 1], accum_out=sums[:, g % 2, h:h + 1])
                op.then_inc(probs_ready, 1)

            def step(i, at, looped=False):
                first, second = stages(i, looped)
                f = at(first) if first is not None else None
                s = at(second) if second is not None else None
                if s:
                    exponents(s, 0)
                if f:
                    b, slot, trip = f
                    act.wait_ge(x_turned, b + 1)
                    after(act, proj_ready, NP * b)
                    act.activation(x_t[:, :, :], ps_turn[:, 0:D].rearrange("p (k n) -> p k n", k=KD), ACT.Copy).then_inc(x_t_ready, 1)
                    squares(f, 0)
                    act.wait_ge(v_ready, b + 1)
                    after(act, out_ready, GROUPS * (b - 1))
                    act.activation(values[:, slot, :], ps_proj[1][:, :], ACT.Copy).then_inc(v_read, 1)
                for g in range(GROUPS):
                    if f:
                        squares(f, g + 1)
                    if s and g + 1 < GROUPS:
                        exponents(s, g + 1)
                    if f:
                        turned_out(f, g)
                    if s:
                        n = GROUPS * s[0] + g
                        act.wait_ge(out_ready, n + 1)
                        after(act, merged, n - 1)
                        act.activation(out_t[:, g % 2], ps_out[:, :].rearrange("p (h n) -> p h n", h=SHARE), ACT.Copy).then_inc(out_read, 1)
                if f:
                    turned_out(f, GROUPS)

            steps(step)(act)

        @block.gpsimd
        def _(pool):
            def inverse_rms(at, n):
                b, slot, trip = at
                m = NP * b + n
                alone(pool, powered, m + 1, stood)
                pool.tensor_scalar(inverse[:, n % 2, :], power[:, n % 2, :], 1.0 / HD1, RMS_EPS, ALU.mult, ALU.add).then_inc(inv_step, 1)
                pool.wait_ge(inv_step, 2 * m + 1)
                pool.tensor_tensor(inverse[:, n % 2, :], inverse[:, n % 2, :], keep.minus_half[:, 0:SHARE], ALU.pow).then_inc(inv_step, 1)

            def weigh(at, g):
                b, slot, trip = at
                n = GROUPS * b + g
                pool.wait_ge(inv_ready, n + 1)
                after(pool, w_turned, n - 1)
                pool.tensor_tensor(weights[:, g % 2], probs[:, g % 2], sums_inv[:, g % 2, :].unsqueeze(2).broadcast_to([P, SHARE, P]),
                                   ALU.mult).then_inc(weights_ready, 1)

            def step(i, at, looped=False):
                first, second = stages(i, looped)
                f = at(first) if first is not None else None
                s = at(second) if second is not None else None
                if f:
                    inverse_rms(f, 0)
                for g in range(GROUPS):
                    if s:
                        weigh(s, g)
                    if f:
                        inverse_rms(f, g + 1)

            steps(step)(pool)
            pool.wait_ge(stats_step, 3 * NB)
            inverse_deviation(pool, keep, 3)




def normalise(dve, keep, xn, b, done):
    row = bass.ds(b, 1)
    dve.tensor_scalar(xn.unsqueeze(1), keep.x[:, row, :], keep.moments[:, row, 0:1], keep.rstd[:, row], ALU.subtract, ALU.mult).then_inc(done, 1)


def layer1_route(nc, keep, w, weights_in):
    with ExitStack() as ctx:
        sem = lambda n: ctx.enter_context(nc.semaphore("r_" + n))
        sb = lambda n, shape, dt=F32: ctx.enter_context(nc.sbuf_tensor("r_" + n, shape, dt))
        bank = lambda n: ctx.enter_context(nc.psum_tensor("r_" + n, [P, 512], F32))
        w_r = sb("w_r", [P, KE, EXPERTS])
        earlier = sb("earlier", [P, P])
        numbers = sb("numbers", [P, P])
        xn = sb("xn", [P, 4, D])
        x_t = sb("x_t", [P, KE, P])
        top = sb("top", [P, 8])
        low = sb("low", [P, 1])
        exps = sb("exps", [P, EXPERTS])
        total = sb("total", [P, 1])
        total_inv = sb("total_inv", [P, 1])
        scores = sb("scores", [P, EXPERTS])
        best = sb("best", [P, 8])
        best_expert = sb("best_expert", [P, 8], U32)
        expert = sb("expert", [P, TOP_K])
        hits = sb("hits", [P, TOP_K, EXPERTS])
        chosen = sb("chosen", [P, EXPERTS])
        best_sum = sb("best_sum", [P, 1])
        best_inv = sb("best_inv", [P, 1])
        places = sb("places", [P, TOP_K, EXPERTS])
        place = sb("place", [P, TOP_K])
        row = sb("row", [P, TOP_K])
        over = sb("over", [P, TOP_K])
        send_row = sb("send_row", [P, 4, TOP_K], U32)
        before = sb("before", [P, EXPERTS])
        tiles = sb("tiles", [EXPERTS, P])
        passed = sb("passed", [EXPERTS, 2, P])
        at_row = sb("at_row", [EXPERTS, P])
        beyond = sb("beyond", [EXPERTS, P])
        experts = sb("experts", [1, QUADS + 2, 4])
        packed = sb("packed", [1, 2, QUADS])
        ps_turn, ps_place, ps_jobs = bank("ps_turn"), bank("ps_place"), bank("ps_jobs")
        ps_logits = [bank("ps_logits0"), bank("ps_logits1")]

        w_in, made, xn_ready, x_turned, x_t_ready, logits_ready = (
            sem("w_in"), sem("made"), sem("xn_ready"), sem("x_turned"), sem("x_t_ready"), sem("logits_ready"))
        low_ready, exps_ready, chosen_ready, place_ready, rows_ready, step_done, table_step = (
            sem("low_ready"), sem("exps_ready"), sem("chosen_ready"), sem("place_ready"), sem("rows_ready"),
            sem("step_done"), sem("table_step"))
        placed, finish_step = sem("placed"), sem("finish_step")
        sent = [sem(f"sent{k}") for k in range(4)]
        kept = [sem("kept0"), sem("kept1")]
        table_in = sem("table_in")
        stood = keep.stood
        block = ctx.enter_context(nc.Block())

        def steps(step):
            def run(eng):
                for i in range(-1, 3):
                    step(i, lambda b: (b, b % 4, b // 4))
                with eng.Fori(0, 2) as t:
                    for c in range(3, 7):
                        step(c, lambda b: (t * 4 + b, b % 4, t + b // 4), looped=True)
                for i in range(11, 16):
                    step(i, lambda b: (b, b % 4, b // 4))
            return run

        def stages(i, at, looped):
            return tuple(at(b) if looped or 0 <= b < NB else None for b in (i + 1, i))

        @block.sync
        def _(sp):
            sp.dma_start(w_r[:, :, :], w.router.rearrange("(k p) n -> p k n", p=P)).then_inc(w_in, 16)
            sp.dma_start(earlier[:, :], w.earlier).then_inc(w_in, 16)
            sp.dma_start(numbers[:, :], w.numbers).then_inc(w_in, 16)
            sp.dma_start(keep.jobs[0:1, 0:1, ROUTED_JOBS:], w.shared_rows.unsqueeze(0)).then_inc(table_in, 16)
            sp.dma_start(experts[0:1, :, :], w.shared_experts.unsqueeze(0)).then_inc(w_in, 16)

            def step(i, at, looped=False):
                first, _ = stages(i, at, looped)
                if first:
                    b, slot, trip = first
                    alone(sp, xn_ready, b + 1, stood)
                    sp.dma_start(keep.rows[bass.ds(b * P + TOKEN_ROW, P), :], xn[:, slot, :]).then_inc(kept[slot % 2], 16)
                if first:
                    load_experts(b * 2)
                elif i == NB - 1:
                    load_experts(EXPERTS)

            def load_experts(e):
                sp.dma_start(keep.w_gu[:, bass.ds(e, 2)], w.gu[bass.ds(e, 2)].rearrange("e (k p) n -> p e k n", p=P)).then_inc(weights_in, 16)
                sp.dma_start(keep.w_down[:, bass.ds(e, 2)], w.down_e[bass.ds(e, 2)].rearrange("e (k p) n -> p e k n", p=FH)).then_inc(weights_in, 16)

            steps(step)(sp)
            sp.wait_ge(table_in, 16)
            for slot in range(2):
                sp.wait_ge(kept[slot], 16 * NB // 2)

        @block.tensor
        def _(pe):
            pe.wait_ge(w_in, 4 * 16)
            pe.wait_ge(made, 1)

            def step(i, at, looped=False):
                first, second = stages(i, at, looped)
                if first:
                    b, slot, trip = first
                    alone(pe, xn_ready, b + 1, stood)
                    for c in range(KE):
                        mm = pe.transpose(ps_turn[:, c * P:(c + 1) * P], xn[:, slot, c * P:(c + 1) * P], keep.identity[:, :])
                    mm.then_inc(x_turned, 1)
                    alone(pe, x_t_ready, b + 1, stood)
                    for c in range(KE):
                        mm = pe.matmul(ps_logits[slot % 2][:, 0:EXPERTS], x_t[:, c, :], w_r[:, c, :], start=(c == 0), stop=(c == KE - 1))
                    mm.then_inc(logits_ready, 1)
                if second:
                    b, slot, trip = second
                    alone(pe, chosen_ready, b + 1, stood)
                    pe.matmul(ps_place[:, 0:EXPERTS], earlier[:, :], chosen[:, :], start=True, stop=False)
                    pe.matmul(ps_place[:, 0:EXPERTS], keep.ones[:, :], before[:, :], start=False, stop=True).then_inc(place_ready, 1)

            steps(step)(pe)
            pe.wait_ge(rows_ready, NB)
            pe.matmul(ps_jobs[0:EXPERTS, 0:P], before[:, :], keep.ones[:, :], start=True, stop=True).then_inc(table_step, 1)
            pe.wait_ge(table_step, 7)
            pe.matmul(ps_jobs[0:EXPERTS, P:2 * P], earlier[0:EXPERTS, 0:EXPERTS], tiles[:, :], start=True, stop=True).then_inc(table_step, 1)
            pe.wait_ge(table_step, 10)
            pe.matmul(ps_jobs[0:EXPERTS, 2 * P:4 * P], keep.ones[0:EXPERTS, 0:EXPERTS], passed[:, :, :].rearrange("p a n -> p (a n)"),
                      start=True, stop=True).then_inc(table_step, 1)

        @block.scalar
        def _(act):
            def step(i, at, looped=False):
                first, second = stages(i, at, looped)
                if second:
                    b, slot, trip = second
                    alone(act, low_ready, b + 1, stood)
                    act.activation(exps[:, :], ps_logits[slot % 2][:, 0:EXPERTS], ACT.Exp, bias=low[:, :],
                                   accum_out=total[:, :]).then_inc(exps_ready, 1)
                if first:
                    b, slot, trip = first
                    alone(act, x_turned, b + 1, stood)
                    act.activation(x_t[:, :, :], ps_turn[:, 0:D].rearrange("p (k n) -> p k n", k=KE), ACT.Copy).then_inc(x_t_ready, 1)

            steps(step)(act)

        @block.vector
        def _(dve):
            LINKS = 14
            dve.memset(before[:, :], 0.0).then_inc(made, 1)
            dve.wait_ge(w_in, 4 * 16)

            def largest(b, slot, trip):
                alone(dve, logits_ready, b + 1, stood)
                dve.max(top[:, :], ps_logits[slot % 2][:, 0:EXPERTS]).then_inc(step_done, 1)
                alone(dve, step_done, b * LINKS + 1, stood)
                dve.tensor_scalar(low[:, :], top[:, 0:1], -1.0, None, ALU.mult).then_inc(low_ready, 1)

            def place_batch(b, slot, trip):
                def done(n):
                    alone(dve, step_done, b * LINKS + n, stood)

                alone(dve, exps_ready, b + 1, stood)
                dve.reciprocal(total_inv[:, :], total[:, :]).then_inc(step_done, 1)
                done(2)
                dve.tensor_scalar(scores[:, :], exps[:, :], total_inv[:, :], None, ALU.mult).then_inc(step_done, 1)
                done(3)
                dve.max(best[:, :], scores[:, :]).then_inc(step_done, 1)
                done(4)
                dve.max_index(best_expert[:, :], best[:, :], scores[:, :]).then_inc(step_done, 1)
                dve.tensor_reduce(best_sum[:, :], best[:, 0:TOP_K], AX, ALU.add).then_inc(step_done, 1)
                done(5)
                dve.tensor_copy(expert[:, :], best_expert[:, 0:TOP_K]).then_inc(step_done, 1)
                done(7)
                dve.tensor_tensor(hits[:, :, :], numbers[:, 0:EXPERTS].unsqueeze(1).broadcast_to([P, TOP_K, EXPERTS]),
                                  expert[:, :].unsqueeze(2).broadcast_to([P, TOP_K, EXPERTS]), ALU.is_equal).then_inc(step_done, 1)
                done(8)
                dve.tensor_reduce(chosen[:, :], hits[:, :, :].rearrange("p k e -> p e k"), AX, ALU.add).then_inc(chosen_ready, 1)
                dve.tensor_scalar(best_sum[:, :], best_sum[:, :], 1e-20, None, ALU.add).then_inc(step_done, 1)
                done(9)
                dve.reciprocal(best_inv[:, :], best_sum[:, :]).then_inc(step_done, 1)
                done(10)
                dve.tensor_scalar(keep.weight[:, bass.ds(b, 1), :], best[:, 0:TOP_K].unsqueeze(1), best_inv[:, :], None,
                                  ALU.mult).then_inc(step_done, 1)
                dve.tensor_copy(keep.first_row[:, bass.ds(b, 1), :], expert[:, :].unsqueeze(1)).then_inc(step_done, 1)
                alone(dve, place_ready, b + 1, stood)
                dve.tensor_tensor(places[:, :, :], hits[:, :, :], ps_place[:, 0:EXPERTS].unsqueeze(1).broadcast_to([P, TOP_K, EXPERTS]),
                                  ALU.mult).then_inc(step_done, 1)
                dve.tensor_tensor(before[:, :], before[:, :], chosen[:, :], ALU.add).then_inc(rows_ready, 1)
                done(13)
                dve.tensor_reduce(place[:, :], places[:, :, :], AX, ALU.add).then_inc(step_done, 1)
                done(14)
                dve.tensor_copy(keep.place[:, bass.ds(b, 1), :], place[:, :].unsqueeze(1)).then_inc(placed, 1)
                dve.tensor_scalar(over[:, :], place[:, :], float(CAPACITY), SKIP, ALU.is_gt, ALU.mult).then_inc(placed, 1)
                dve.scalar_tensor_tensor(row[:, :], expert[:, :], float(CAPACITY), place[:, :], ALU.mult, ALU.add).then_inc(placed, 1)
                alone(dve, placed, 4 * b + 3, stood)
                dve.scalar_tensor_tensor(send_row[:, slot, :], over[:, :], -1.0, row[:, :], ALU.add, ALU.add).then_inc(placed, 1)

            def step(i, at, looped=False):
                first, second = stages(i, at, looped)
                if second:
                    largest(*second)
                if first:
                    b, slot, trip = first
                    alone(dve, sent[slot], 16 * TOP_K * trip, stood)
                    if not isinstance(trip, int) or trip > 0:
                        alone(dve, kept[slot % 2], 16 * (trip * 2 + slot // 2), stood)
                    normalise(dve, keep, xn[:, slot, :], b, xn_ready)
                if second:
                    place_batch(*second)

            steps(step)(dve)
            dve.wait_ge(placed, 4 * NB)

            every = lambda x: x[:, :, :].rearrange("p b k -> p (b k)")
            dve.scalar_tensor_tensor(every(keep.weight), every(keep.place), float(CAPACITY), every(keep.weight),
                                     ALU.is_le, ALU.mult).then_inc(finish_step, 1)
            dve.tensor_scalar(every(keep.valid), every(keep.place), float(CAPACITY), None, ALU.is_le).then_inc(finish_step, 1)
            dve.tensor_scalar(every(keep.place), every(keep.place), -1.0, None, ALU.add).then_inc(finish_step, 1)
            dve.wait_ge(finish_step, 3)
            dve.tensor_tensor(every(keep.place), every(keep.place), every(keep.valid), ALU.mult).then_inc(finish_step, 1)
            dve.wait_ge(finish_step, 4)
            dve.scalar_tensor_tensor(every(keep.result_row), every(keep.first_row), float(CAPACITY), every(keep.place),
                                     ALU.mult, ALU.add).then_inc(finish_step, 1)

            dve.wait_ge(table_step, 1)
            dve.tensor_scalar(tiles[:, :], ps_jobs[0:EXPERTS, 0:P], 0.0, None, ALU.is_gt).then_inc(table_step, 1)
            for n in range(1, CAPACITY // P):
                dve.wait_ge(table_step, n + 1)
                dve.scalar_tensor_tensor(tiles[:, :], ps_jobs[0:EXPERTS, 0:P], float(n * P), tiles[:, :], ALU.is_gt, ALU.add).then_inc(table_step, 1)
            dve.wait_ge(table_step, 8)
            dve.tensor_tensor(passed[:, 0, :], ps_jobs[0:EXPERTS, P:2 * P], numbers[0:EXPERTS, :], ALU.is_le).then_inc(table_step, 1)
            dve.wait_ge(table_step, 9)
            dve.tensor_tensor(passed[:, 1, :], passed[:, 0, :], tiles[:, :], ALU.mult).then_inc(table_step, 1)
            dve.wait_ge(table_step, 11)
            routed = experts[0:1, 1:1 + ROUTED_JOBS // 4, :].rearrange("p q k -> p (q k)")
            dve.tensor_scalar(routed, ps_jobs[0:1, 2 * P:3 * P], float(EXPERTS - 1), None, ALU.min).then_inc(table_step, 1)
            dve.scalar_tensor_tensor(at_row[0:1, :], ps_jobs[0:1, 3 * P:4 * P], -1.0, numbers[0:1, :], ALU.mult, ALU.add).then_inc(table_step, 1)
            dve.wait_ge(table_step, 13)
            dve.tensor_scalar(at_row[0:1, :], at_row[0:1, :], float(P), None, ALU.mult).then_inc(table_step, 1)
            dve.wait_ge(table_step, 14)
            dve.scalar_tensor_tensor(at_row[0:1, :], ps_jobs[0:1, 2 * P:3 * P], float(CAPACITY), at_row[0:1, :], ALU.mult, ALU.add).then_inc(table_step, 1)
            dve.wait_ge(table_step, 15)
            dve.tensor_scalar(keep.jobs[0:1, 0, 0:ROUTED_JOBS], at_row[0:1, :], float(TOKEN_ROW), None, ALU.min).then_inc(table_step, 1)
            dve.tensor_scalar(beyond[0:1, :], at_row[0:1, :], float(TOKEN_ROW), float(NB * P), ALU.is_ge, ALU.mult).then_inc(table_step, 1)
            dve.wait_ge(table_step, 17)
            dve.tensor_tensor(keep.jobs[0:1, 1, 0:ROUTED_JOBS], at_row[0:1, :], beyond[0:1, :], ALU.add).then_inc(table_step, 1)
            count = 18
            for which, spots in ((0, (6, 5, 4, 3)), (1, (4, 3, 2, 1))):
                of = lambda n: experts[0:1, n // 4:n // 4 + QUADS, n % 4]
                word = packed[0:1, which, :]
                for k in range(1, 4):
                    dve.wait_ge(table_step, count)
                    dve.scalar_tensor_tensor(word if k < 3 else keep.job_experts[0:1, which, :], of(spots[0]) if k == 1 else word,
                                             float(PACK), of(spots[k]), ALU.mult, ALU.add).then_inc(table_step, 1)
                    count += 1

        @block.gpsimd
        def _(pool):
            def step(i, at, looped=False):
                first, second = stages(i, at, looped)
                if second:
                    b, slot, trip = second
                    alone(pool, placed, 4 * (b + 1), stood)
                    for k in range(TOP_K):
                        pool.indirect_dma_start(keep.rows[0:TOKEN_ROW, :], bass.IndirectOffsetOnAxis(ap=send_row[:, slot, k:k + 1], axis=0),
                                                xn[:, slot, :], None, bounds_check=TOKEN_ROW - 1, oob_is_err=False).then_inc(sent[slot], 16)

            steps(step)(pool)
            for slot in range(4):
                pool.wait_ge(sent[slot], 16 * TOP_K * NB // 4)


def layer1_experts(nc, keep, w, weights_in, out):
    with ExitStack() as ctx:
        sem = lambda n: ctx.enter_context(nc.semaphore("h_" + n))
        sb = lambda n, shape, dt=F32: ctx.enter_context(nc.sbuf_tensor("h_" + n, shape, dt))
        bank = lambda n: ctx.enter_context(nc.psum_tensor("h_" + n, [P, 512], F32))
        rows = sb("rows", [P, 4, D])
        x_t = sb("x_t", [P, 2, KE, P])
        act_gate = sb("act_gate", [P, 2, FE])
        h = sb("h", [P, 2, FE])
        h_t = sb("h_t", [FH, 2, 2, P])
        results = sb("results", [P, 2, D])
        gather_row = sb("gather_row", [P, 2, TOP_K], U32)
        gathered = sb("gathered", [P, 2, TOP_K, D])
        weight = sb("weight", [P, TOP_K])
        ps_turn = [bank("ps_turn0"), bank("ps_turn1")]
        ps_gu = [bank("ps_gu0"), bank("ps_gu1")]
        ps_h = [bank("ps_h0"), bank("ps_h1")]
        ps_y = [bank("ps_y0"), bank("ps_y1")]
        sems = lambda n, k: [sem(f"{n}{i}") for i in range(k)]
        rows_in, stored, gathered_in = sems("rows_in", 4), sems("stored", 2), sems("gathered_in", 2)
        x_turned, x_t_ready, gu_ready, silu_ready, h_ready, h_turned, h_t_ready, down_done, result_ready = (
            sem("x_turned"), sem("x_t_ready"), sem("gu_ready"), sem("silu_ready"), sem("h_ready"), sem("h_turned"),
            sem("h_t_ready"), sem("down_done"), sem("result_ready"))
        row_ready, summed, x_done, out_done = sem("row_ready"), sem("summed"), sem("x_done"), sem("out_done")
        stood = keep.stood
        block = ctx.enter_context(nc.Block())

        def run(step):
            def program(eng):
                for s in range(8):
                    step(s, s, s // 4)
                with eng.Fori(0, (ROUTED_JOBS - 8) // 4) as t:
                    for c in range(8, 12):
                        step(t * 4 + c, c, t + 2)
                for s in range(ROUTED_JOBS, ROUTED_JOBS + 8):
                    step(s, s, s // 4)
                with eng.Fori(0, (JOBS - ROUTED_JOBS - 8) // 4) as t:
                    for c in range(ROUTED_JOBS + 8, ROUTED_JOBS + 12):
                        step(t * 4 + c, c, t + (ROUTED_JOBS + 8) // 4)
                for s in range(JOBS, JOBS + 3):
                    step(s, s, s // 4)
            return program

        def batch_of(c, quad):
            if c < ROUTED_JOBS + 4 or c % 2:
                return None
            trip, slot = quad - (ROUTED_JOBS + 4) // 4, c % 4 // 2
            return trip * 2 + slot, slot, trip

        @block.sync
        def _(sp):
            def load(s, c):
                row = sp.value_load(keep.jobs[0:1, 0, bass.ds(s, 1)], min_val=0, max_val=IDLE_ROW - P)
                if c >= 4:
                    alone(sp, x_turned, s - 3, stood)
                sp.dma_start(rows[:, c % 4, :], keep.rows[bass.ds(row, P), :]).then_inc(rows_in[c % 4], 16)

            def step(s, c, quad):
                if c < JOBS:
                    load(s, c)
            run(step)(sp)
            begun = 0
            for end in (NB // 2, NB - 2, NB):
                sp.wait_ge(x_done, end)
                sp.dma_start(out[begun:end].rearrange("b p n -> p b n"), keep.x[:, begun:end, :]).then_inc(out_done, 16)
                begun = end
            sp.wait_ge(out_done, 3 * 16)

        @block.tensor
        def _(pe):
            pe.wait_ge(weights_in, (EXPERTS + SHARED) * 16)

            experts = {}

            def load_experts(quad):
                for which in range(2):
                    word = pe.value_load(keep.job_experts[0:1, which, bass.ds(quad, 1)], min_val=0, max_val=PACK ** 4 - 1)
                    for k in range(4):
                        e = (word >> (k * PACK_BITS)) & (PACK - 1)
                        experts[which, k] = e.with_bounds(min_val=0, max_val=EXPERTS + SHARED - 1)

            def step(s, c, quad):
                if c % 4 == 0:
                    load_experts(quad)
                if 1 <= c <= JOBS:
                    slot = (c - 1) % 2
                    e = experts[0, c % 4]
                    alone(pe, x_t_ready, s, stood)
                    if c > 2:
                        alone(pe, h_ready, s - 2, stood)
                    for k in range(KE):
                        mm = pe.matmul(ps_gu[slot][:, 0:2 * FE].unsqueeze(1), x_t[:, slot, k, :], keep.w_gu[:, bass.ds(e, 1), k, :],
                                       start=(k == 0), stop=(k == KE - 1))
                    mm.then_inc(gu_ready, 1)
                if c < JOBS:
                    alone(pe, rows_in[c % 4], 16 * (quad + 1), stood)
                    if c > 1:
                        alone(pe, x_t_ready, s - 1, stood)
                    for k in range(KE):
                        mm = pe.transpose(ps_turn[c % 2][:, k * P:(k + 1) * P], rows[:, c % 4, k * P:(k + 1) * P], keep.identity[:, :])
                    mm.then_inc(x_turned, 1)
                if 2 <= c <= JOBS + 1:
                    slot = c % 2
                    alone(pe, h_ready, s - 1, stood)
                    if c > 3:
                        alone(pe, h_t_ready, s - 3, stood)
                    for k in range(2):
                        mm = pe.transpose(ps_h[slot][0:FH, k * P:(k + 1) * P], h[:, slot, k * FH:(k + 1) * FH], keep.identity[:, :])
                    mm.then_inc(h_turned, 1)
                if c >= 3:
                    slot = (c - 3) % 2
                    e = experts[1, c % 4]
                    alone(pe, h_t_ready, s - 2, stood)
                    if c < ROUTED_JOBS + 3:
                        bank, start, stop = ps_y[slot], True, True
                        if c > 4:
                            alone(pe, result_ready, s - 4, stood)
                    else:
                        job = c - 3 - ROUTED_JOBS
                        bank, start, stop = ps_y[job // 2 % 2], slot == 0, slot == 1
                        if job == 0:
                            pe.wait_ge(result_ready, ROUTED_JOBS)
                        elif job > 2 and slot == 0:
                            b, _, _ = batch_of(c - 1, quad)
                            alone(pe, summed, (b - 1) * (TOP_K + 1) + 2, stood)
                    for k in range(2):
                        mm = pe.matmul(bank[:, 0:D].unsqueeze(1), h_t[:, slot, k, :], keep.w_down[:, bass.ds(e, 1), k, :],
                                       start=(start and k == 0), stop=(stop and k == 1))
                    mm.then_inc(down_done, 1)

            run(step)(pe)

        @block.scalar
        def _(act):
            def step(s, c, quad):
                if 1 <= c <= JOBS:
                    slot = (c - 1) % 2
                    alone(act, gu_ready, s, stood)
                    if c > 2:
                        alone(act, h_ready, s - 2, stood)
                    act.activation(act_gate[:, slot, :], ps_gu[slot][:, 0:FE], ACT.Silu).then_inc(silu_ready, 1)
                if c < JOBS:
                    alone(act, x_turned, s + 1, stood)
                    if c > 1:
                        alone(act, gu_ready, s - 1, stood)
                    act.activation(x_t[:, c % 2], ps_turn[c % 2][:, 0:D].rearrange("p (k n) -> p k n", k=KE), ACT.Copy).then_inc(x_t_ready, 1)
                if 2 <= c <= JOBS + 1:
                    slot = c % 2
                    alone(act, h_turned, s - 1, stood)
                    if c > 3:
                        alone(act, down_done, s - 3, stood)
                    act.activation(h_t[:, slot], ps_h[slot][0:FH, 0:2 * P].rearrange("p (k n) -> p k n", k=2), ACT.Copy).then_inc(h_t_ready, 1)

            run(step)(act)

        @block.vector
        def _(dve):
            def rows_for(b, slot):
                dve.tensor_copy(gather_row[:, slot, :].unsqueeze(1), keep.result_row[:, bass.ds(b, 1), :]).then_inc(row_ready, 1)

            def combine_first(at):
                b, slot, trip = at
                alone(dve, down_done, b * SHARED + ROUTED_JOBS + SHARED, stood)
                alone(dve, gathered_in[slot], 16 * TOP_K * (trip + 1), stood)
                if not isinstance(b, int) or b + 2 < NB:
                    rows_for(b + 2, slot)
                dve.tensor_copy(weight[:, :].unsqueeze(1), keep.weight[:, bass.ds(b, 1), :]).then_inc(summed, 1)
                alone(dve, summed, b * (TOP_K + 1) + 1, stood)
                add_results(at, range(TOP_K // 2))

            def add_results(at, choices):
                b, slot, trip = at
                total = gathered[:, slot, 0, :]
                for k in choices:
                    dve.scalar_tensor_tensor(total, gathered[:, slot, k, :], weight[:, k:k + 1],
                                             total if k else ps_y[slot][:, 0:D], ALU.mult, ALU.add).then_inc(summed, 1)
                    alone(dve, summed, b * (TOP_K + 1) + k + 2, stood)

            def combine_rest(at):
                b, slot, trip = at
                add_results(at, range(TOP_K // 2, TOP_K))
                total, row = gathered[:, slot, 0, :], keep.x[:, bass.ds(b, 1), :]
                dve.scalar_tensor_tensor(row, total.unsqueeze(1), keep.gate[:, 3:4], row, ALU.mult, ALU.add).then_inc(x_done, 1)
                alone(dve, x_done, b + 1, stood)

            def step(s, c, quad):
                if 1 <= c <= JOBS:
                    slot = (c - 1) % 2
                    alone(dve, silu_ready, s, stood)
                    if c > 2:
                        alone(dve, h_turned, s - 2, stood)
                    dve.tensor_tensor(h[:, slot, :], ps_gu[slot][:, FE:2 * FE], act_gate[:, slot, :], ALU.mult).then_inc(h_ready, 1)
                if 3 <= c < ROUTED_JOBS + 3:
                    slot = (c - 3) % 2
                    n = s - 3
                    alone(dve, down_done, n + 1, stood)
                    if c >= 5:
                        alone(dve, stored[slot], 16 * (quad * 2 + (c % 4 - 3) // 2), stood)
                    dve.tensor_copy(results[:, slot, :], ps_y[slot][:, 0:D]).then_inc(result_ready, 1)
                at = batch_of(c - c % 2, quad)
                if at and c - c % 2 > ROUTED_JOBS + 4:
                    b, slot, trip = at
                    (combine_rest if c % 2 else combine_first)((b - 1, 1 - slot, trip if slot else trip - 1))

            for b in range(2):
                rows_for(b, b)
            run(step)(dve)
            combine_rest((NB - 2, 0, NB // 2 - 1))
            combine_first((NB - 1, 1, NB // 2 - 1))
            combine_rest((NB - 1, 1, NB // 2 - 1))

        @block.gpsimd
        def _(pool):
            def store(s, c):
                n = s - 4
                row = pool.value_load(keep.jobs[0:1, 1, bass.ds(n, 1)], min_val=0, max_val=ALL_ROWS - P)
                alone(pool, result_ready, n + 1, stood)
                pool.dma_start(keep.rows[bass.ds(row, P), :], results[:, c % 2, :]).then_inc(stored[c % 2], 16)

            def step(s, c, quad):
                if 4 <= c < ROUTED_JOBS + 4:
                    store(s, c)

            run(step)(pool)
            for slot in range(2):
                pool.wait_ge(stored[slot], 16 * ROUTED_JOBS // 2)

            def gather(at):
                b, slot, trip = at
                alone(pool, row_ready, b + 1, stood)
                alone(pool, x_done, b - 1, stood)
                for k in range(TOP_K):
                    pool.indirect_dma_start(gathered[:, slot, k, :], None, keep.rows[0:TOKEN_ROW, :],
                                            bass.IndirectOffsetOnAxis(ap=gather_row[:, slot, k:k + 1], axis=0),
                                            bounds_check=TOKEN_ROW - 1, oob_is_err=False).then_inc(gathered_in[slot], 16)

            for b in range(2):
                gather((b, b, 0))
            with pool.Fori(0, NB // 2 - 1) as t:
                for b in (2, 3):
                    gather((t * 2 + b, b % 2, t + 1))


class Named:
    pass


def build(nc, t, out):
    with ExitStack() as ctx:
        keep = Named()
        sb = lambda n, shape, dt=F32: ctx.enter_context(nc.sbuf_tensor(n, shape, dt))
        keep.x = sb("x_tokens", [P, NB, D])
        keep.identity = sb("identity", [P, P])
        keep.identity_bf = sb("identity_bf", [P, P], BF16)
        keep.gate = sb("gate", [P, 4])
        keep.ones = sb("ones", [P, P])
        keep.minus_half = sb("minus_half", [P, NB])
        keep.moments = sb("moments", [P, NB, 2])
        keep.rstd = sb("rstd", [P, NB])
        keep.stood = ctx.enter_context(nc.semaphore("stood"))
        keep.rstd_done = ctx.enter_context(nc.semaphore("rstd_done"))
        keep.rows = nc.dram_tensor("expert_rows", [ALL_ROWS, D], F32).ap()
        setup(nc, keep, t["x"], t["consts"], t["gates"])
        w = Named()
        w.qk, w.v, w.m, w.bqk, w.bv, w.bm, w.enc, w.sign = (
            t[n] for n in ("a_qk", "a_v", "a_m", "a_bqk", "a_bv", "a_bm", "a_enc", "a_sign"))
        w.gate, w.up, w.down = t["b_gate"], t["b_up"], t["b_down"]
        w.q, w.k, w.v1, w.o, w.norms, w.ctx_t = (t[n] for n in ("c_q", "c_k", "c_v", "c_o", "c_norms", "ctx_t"))
        with ExitStack() as early:
            sb = lambda n, shape, dt=F32: early.enter_context(nc.sbuf_tensor(n, shape, dt))
            keep.ffn, keep.attention = Named(), Named()
            keep.ffn.ternary = sb("ternary", [P, 3, KD * F0], BF16)
            keep.ffn.scale = sb("w_scale", [P, 3])
            keep.ffn.inv = sb("w_inv", [P, 3])
            keep.ffn.up_127 = sb("up_127", [P, 1])
            keep.ffn.down_gate = sb("down_gate", [P, 1])
            layer0_attention(nc, keep, t["ctx"], w)
            keep.attention.w_q = sb("w_q", [P, KD, HEADS1 * HD1])
            keep.attention.w_k = sb("w_k", [P, KD, WIDTH])
            keep.attention.w_v = sb("w_v1", [P, KD, WIDTH])
            keep.attention.w_o = sb("w_o", [P, HEADS1, D])
            keep.attention.norms = sb("norms", [P, 2])
            keep.attention_in = early.enter_context(nc.semaphore("attention_in"))
            layer0_ffn(nc, keep, w)
            layer1_attention(nc, keep, w)
        w.router, w.earlier, w.numbers, w.shared_rows, w.shared_experts, w.gu, w.down_e = (
            t[n] for n in ("d_router", "d_earlier", "d_numbers", "d_rows", "d_experts", "d_gu", "d_down"))
        with ExitStack() as moe:
            sb = lambda n, shape, dt=F32: moe.enter_context(nc.sbuf_tensor(n, shape, dt))
            keep.w_gu = sb("w_gu", [P, EXPERTS + SHARED, KE, 2 * FE])
            keep.w_down = sb("w_down", [FH, EXPERTS + SHARED, 2, D])
            keep.jobs = sb("jobs", [1, 2, JOBS], U32)
            keep.job_experts = sb("job_experts", [1, 2, QUADS], U32)
            keep.weight = sb("choice_weight", [P, NB, TOP_K])
            keep.place = sb("choice_place", [P, NB, TOP_K])
            keep.valid = sb("choice_valid", [P, NB, TOP_K])
            keep.first_row = sb("choice_expert", [P, NB, TOP_K])
            keep.result_row = sb("result_row", [P, NB, TOP_K], U32)
            weights_in = moe.enter_context(nc.semaphore("weights_in"))
            layer1_route(nc, keep, w, weights_in)
            layer1_experts(nc, keep, w, weights_in, out)


def lay_out(i):
    a = {k: np.asarray(v) for k, v in i.items()}
    channel = np.arange(P).reshape(HD0, HEADS0)
    order = channel.T.reshape(-1)
    split = channel.reshape(HD0, PAIRS, 2).transpose(2, 0, 1)
    straight, turned = split.reshape(-1), split[:, np.arange(HD0) ^ 1].reshape(-1)
    wq, wqr, bq, bqr = (a[f"L0_xattn_{n}"][o] for n in ("Wq", "bq") for o in (straight, turned))
    wk, wkr, bk, bkr = (a[f"L0_xattn_{n}"][o] for n in ("Wk", "bk") for o in (straight, turned))
    wv, bv = a["L0_xattn_Wv"][order], a["L0_xattn_bv"][order]
    enc = a["L0_xattn_encoding"][:, 0, 0]
    t = {
        "x": a["x"], "ctx": a["ctx_2048"],
        "gates": np.stack([a["g_xattn"], a["g_ffn"]]).reshape(4),
        "consts": np.eye(P, dtype=np.float32),
        "a_qk": np.stack([wq.T, wqr.T, wk.T, wkr.T], axis=1),
        "a_v": wv.T, "a_m": a["L0_xattn_Wm"][:, order].T,
        "a_bqk": np.stack([bq, bqr, bk, bkr], axis=1),
        "a_bv": bv, "a_bm": a["L0_xattn_bm"][:, None],
        "a_enc": np.tile(np.repeat(enc.transpose(2, 0, 1), PAIRS, axis=0), (2, 1, 1)),
        "a_sign": np.tile(np.repeat(np.array([-1.0, 1.0] * (HD0 // 2), np.float32), PAIRS), 2)[:, None],
    }
    t |= {"b_" + n: a["L0_ffn_w_" + n].T for n in ("gate", "up", "down")}
    t |= {"c_" + n: a["L1_xattn_W" + n] for n in "qkvo"}
    t["c_norms"] = np.stack([a["L1_xattn_q_norm_w"], a["L1_xattn_k_norm_w"]], axis=1)
    shared = np.stack([a["L1_ffn_ws_gate"], a["L1_ffn_ws_up"]], axis=1).reshape(D, 2, 2, FE).transpose(2, 0, 1, 3)
    routed = np.stack([a["L1_ffn_w_gate"], a["L1_ffn_w_up"]], axis=2)
    t["d_gu"] = np.concatenate([routed, shared]).reshape(EXPERTS + SHARED, D, 2 * FE)
    t["d_down"] = np.concatenate([a["L1_ffn_w_down"], a["L1_ffn_ws_down"].reshape(2, FE, D)])
    t["d_router"] = a["L1_ffn_wg_router"].T
    t["d_earlier"] = np.triu(np.ones((P, P), np.float32))
    t["d_numbers"] = np.tile(np.arange(P, dtype=np.float32), (P, 1))
    job = np.arange(SHARED * NB, dtype=np.uint32)
    t["d_rows"] = (TOKEN_ROW + job // SHARED * P).astype(np.uint32)[None]
    experts = np.zeros((QUADS + 2) * 4, np.float32)
    experts[4 + ROUTED_JOBS:4 + JOBS] = EXPERTS + job % SHARED
    t["d_experts"] = experts.reshape(QUADS + 2, 4)
    t["ctx_t"] = a["ctx_2048"].transpose(0, 2, 1)
    return {k: np.ascontiguousarray(v) for k, v in t.items()}


def kernel(**inputs):
    import concourse.bacc as bacc
    from concourse.bass_utils import run_bass_kernel_spmd

    nc = bacc.Bacc("TRN2", target_bir_lowering=False, num_devices=1)
    arrays = lay_out(inputs)
    tensors = {n: nc.dram_tensor(f"in_{n}", a.shape, mybir.dt.from_np(a.dtype), kind="ExternalInput").ap()
               for n, a in arrays.items()}
    out = nc.dram_tensor("out", (NB, P, D), F32, kind="ExternalOutput").ap()
    build(nc, tensors, out)
    result = run_bass_kernel_spmd(nc, [{f"in_{n}": a for n, a in arrays.items()}], core_ids=[0])
    return result.results[0]["out"]
```
